# Optimizing a Trainium2 kernel written in Bass

```python
import numpy as np
import jax
import jax.numpy as jnp

def _softmax(x, axis=-1):
    return jax.nn.softmax(x, axis=axis)

def _gelu(x):
    return jax.nn.gelu(x, approximate=True)

def _silu(x):
    return jax.nn.silu(x)

def _sigmoid(x):
    return jax.nn.sigmoid(x)

def _layernorm(x, axis=-1, eps=1e-05):
    m = jnp.mean(x, axis=axis, keepdims=True)
    v = jnp.var(x, axis=axis, keepdims=True)
    return (x - m) / jnp.sqrt(v + eps)

def _scatter_add(tgt, idx, src, axis=0):
    return tgt.at[idx].add(src)

def _segment_sum(src, seg, n):
    return jax.ops.segment_sum(src, seg, n)
kernel_name = 'mk_xattn_ffn_d4_seqx_r8_6a36a4'

def setup_inputs(seed: int=0):
    np.random.seed(seed)
    _w = jnp.asarray

    def _rec_inputs():
        import jax
        import jax.numpy as jnp
        _rk = jax.random.key(seed)
        x = -0.000929 + 1 * jax.random.normal(jax.random.fold_in(_rk, 1), (2, 512, 128), jnp.float32)
        _lenS = 512 - jax.random.randint(jax.random.fold_in(_rk, 7), (2,), 0, max(1, 512 // 4) + 1, jnp.int32)
        _lenS2 = 32 - jax.random.randint(jax.random.fold_in(_rk, 8), (2,), 0, max(1, 32 // 4) + 1, jnp.int32)
        _ctx_1024P = jax.random.normal(jax.random.fold_in(_rk, 11), (2, 16, 128), jnp.float32)
        _ctx_1024c = jax.random.dirichlet(jax.random.fold_in(_rk, 511), 0.3 * jnp.ones((16,), jnp.float32), (2, 32))
        _ctx_1024t = jnp.einsum('bsk,bkd->bsd', _ctx_1024c, _ctx_1024P)
        _ctx_1024t = _ctx_1024t * jax.lax.rsqrt(jnp.mean(jnp.square(_ctx_1024t)) + 1e-12) * 0.953939
        ctx_1024 = -1.52775e-05 + 0.999936 * (_ctx_1024t + 0.3 * jax.random.normal(jax.random.fold_in(_rk, 611), (2, 32, 128), jnp.float32))
        itok_BxS_0_255 = jax.random.randint(jax.random.fold_in(_rk, 12), (2, 512), 0, 32, jnp.int32)
        return (x, ctx_1024, itok_BxS_0_255)
    x, ctx_1024, itok_BxS_0_255 = _rec_inputs()

    def _L0_xattn_setup():
        import jax, jax.numpy as jnp
        import numpy as np
        DIM = 128
        H = 16
        D = 64
        INNER = H * D
        EPS = 1e-05

        def layernorm(x, w, b):
            mu = jnp.mean(x, axis=-1, keepdims=True)
            var = jnp.var(x, axis=-1, keepdims=True)
            return (x - mu) * jax.lax.rsqrt(var + EPS) * w + b
        key = jax.random.key(seed)
        ks = jax.random.split(key, 8)
        B, N, S = (4, 32, 1024)
        s = 1.0 / np.sqrt(DIM)
        return {'latents': jax.random.normal(ks[0], (B, N, DIM), jnp.float32), 'context': jax.random.normal(ks[1], (B, S, DIM), jnp.float32), 'ln_l_w': jnp.ones((DIM,), jnp.float32), 'ln_l_b': jnp.zeros((DIM,), jnp.float32), 'ln_c_w': jnp.ones((DIM,), jnp.float32), 'ln_c_b': jnp.zeros((DIM,), jnp.float32), 'Wq': jax.random.normal(ks[2], (DIM, INNER), jnp.float32) * s, 'Wkv': jax.random.normal(ks[3], (DIM, 2 * INNER), jnp.float32) * s, 'Wo': jax.random.normal(ks[4], (INNER, DIM), jnp.float32) * (1.0 / np.sqrt(INNER)), 'bo': jnp.zeros((DIM,), jnp.float32)}
    _L0_xattn_all = _L0_xattn_setup()
    _L0_xattn_in = {k: v for k, v in _L0_xattn_all.items() if k in ('ln_l_w', 'ln_l_b', 'ln_c_w', 'ln_c_b', 'Wq', 'Wkv', 'Wo', 'bo')}
    del _L0_xattn_all

    def _L0_ffn_setup():
        import jax, jax.numpy as jnp
        import numpy as np
        D = 128
        H = 16
        FF = 512
        E = 8
        K = 2
        EH = 128
        B, S = (2, 256)
        EPS = 1e-05

        def rmsnorm(x, w):
            v = jnp.mean(jnp.square(x), axis=-1, keepdims=True)
            return x * jax.lax.rsqrt(v + EPS) * w

        def _dense_path(x, wq, wk, wv, wo, w1, w2, w3, attn_norm_w, ff_norm_w):
            b, s, d = x.shape
            hd = d // H
            q = (x @ wq).reshape(b, s, H, hd)
            k = (x @ wk).reshape(b, s, H, hd)
            v = (x @ wv).reshape(b, s, H, hd)
            scores = jnp.einsum('bqhd,bkhd->bhqk', q, k) / np.sqrt(hd).astype(np.float32)
            causal = jnp.tril(jnp.ones((s, s), bool))
            scores = jnp.where(causal, scores, jnp.finfo(scores.dtype).min)
            attn = jax.nn.softmax(scores, axis=-1)
            o = jnp.einsum('bhqk,bkhd->bqhd', attn, v).reshape(b, s, d)
            h = x + rmsnorm(o @ wo, attn_norm_w)
            ffn = jax.nn.silu(h @ w1) * (h @ w3) @ w2
            return h + rmsnorm(ffn, ff_norm_w)

        def _sparse_path(x, router_w, ew1, ew2, ew3, moe_norm_w):
            b, s, d = x.shape
            xt = x.reshape(-1, d)
            probs = jax.nn.softmax(xt @ router_w, axis=-1)
            topw, topi = jax.lax.top_k(probs, K)
            g = jax.nn.silu(jnp.einsum('td,edh->eth', xt, ew1)) * jnp.einsum('td,edh->eth', xt, ew3)
            eo = jnp.einsum('eth,ehd->ted', g, ew2)
            sel = jnp.take_along_axis(eo, topi[:, :, None], axis=1)
            moe_out = jnp.sum(topw[:, :, None] * sel, axis=1).reshape(b, s, d)
            return rmsnorm(moe_out, moe_norm_w)
        key = jax.random.key(seed)
        ks = jax.random.split(key, 16)
        s = 0.02
        return {'x': jax.random.normal(ks[0], (B, S, D), jnp.float32), 'wq': jax.random.normal(ks[1], (D, D), jnp.float32) * s, 'wk': jax.random.normal(ks[2], (D, D), jnp.float32) * s, 'wv': jax.random.normal(ks[3], (D, D), jnp.float32) * s, 'wo': jax.random.normal(ks[4], (D, D), jnp.float32) * s, 'w1': jax.random.normal(ks[5], (D, FF), jnp.float32) * s, 'w2': jax.random.normal(ks[6], (FF, D), jnp.float32) * s, 'w3': jax.random.normal(ks[7], (D, FF), jnp.float32) * s, 'attn_norm_w': jnp.ones((D,), jnp.float32), 'ff_norm_w': jnp.ones((D,), jnp.float32), 'moe_norm_w': jnp.ones((D,), jnp.float32), 'router_w': jax.random.normal(ks[8], (D, E), jnp.float32) * s, 'ew1': jax.random.normal(ks[9], (E, D, EH), jnp.float32) * s, 'ew2': jax.random.normal(ks[10], (E, EH, D), jnp.float32) * s, 'ew3': jax.random.normal(ks[11], (E, D, EH), jnp.float32) * s}
    _L0_ffn_all = _L0_ffn_setup()
    _L0_ffn_in = {k: v for k, v in _L0_ffn_all.items() if k in ('wq', 'wk', 'wv', 'wo', 'w1', 'w2', 'w3', 'attn_norm_w', 'ff_norm_w', 'moe_norm_w', 'router_w', 'ew1', 'ew2', 'ew3')}
    del _L0_ffn_all

    def _L1_xattn_setup():
        import jax, jax.numpy as jnp
        import numpy as np
        EMBED_DIM = 128
        NUM_HEADS = 16
        HEAD_DIM = EMBED_DIM // NUM_HEADS
        key = jax.random.key(seed)
        ks = jax.random.split(key, 11)
        B, S, D = (2, 256, EMBED_DIM)
        scale = 1.0 / np.sqrt(D)
        inp = {'query': jax.random.normal(ks[0], (B, S, D), dtype=jnp.float32), 'key': jax.random.normal(ks[1], (B, S, D), dtype=jnp.float32), 'value': jax.random.normal(ks[2], (B, S, D), dtype=jnp.float32), 'Wq': jax.random.normal(ks[3], (D, D), dtype=jnp.float32) * scale, 'bq': jnp.zeros((D,), dtype=jnp.float32), 'Wk': jax.random.normal(ks[4], (D, D), dtype=jnp.float32) * scale, 'bk': jnp.zeros((D,), dtype=jnp.float32), 'Wv': jax.random.normal(ks[5], (D, D), dtype=jnp.float32) * scale, 'bv': jnp.zeros((D,), dtype=jnp.float32), 'Wo': jax.random.normal(ks[6], (D, D), dtype=jnp.float32) * scale, 'bo': jnp.zeros((D,), dtype=jnp.float32)}
        return inp
    _L1_xattn_all = _L1_xattn_setup()
    _L1_xattn_in = {k: v for k, v in _L1_xattn_all.items() if k in ('Wq', 'bq', 'Wk', 'bk', 'Wv', 'bv', 'Wo', 'bo')}
    del _L1_xattn_all

    def _L1_ffn_setup():
        import jax, jax.numpy as jnp
        import numpy as np
        TOP_K = 2
        key = jax.random.key(seed)
        k1, k2, k3, k4 = jax.random.split(key, 4)
        B, T, D, H, E = (2, 256, 128, 256, 8)
        x = jax.random.normal(k1, (B, T, D), dtype=jnp.float32)
        w12 = jax.random.normal(k2, (E, 2 * H, D), dtype=jnp.float32) * D ** (-0.5)
        w3 = jax.random.normal(k3, (E, D, H), dtype=jnp.float32) * H ** (-0.5)
        gate_w = jax.random.normal(k4, (E, D), dtype=jnp.float32) * D ** (-0.5)
        return {'x': x, 'w12': w12, 'w3': w3, 'gate_w': gate_w}
    _L1_ffn_all = _L1_ffn_setup()
    _L1_ffn_in = {k: v for k, v in _L1_ffn_all.items() if k in ('w12', 'w3', 'gate_w')}
    del _L1_ffn_all

    def _L2_xattn_setup():
        import jax, jax.numpy as jnp
        import numpy as np
        N_LAYERS = 4
        H = 16
        LOOKBACK = 128
        EPS = 1e-06
        ROPE_BASE = 10000.0
        NEG = jnp.float32(-1e+30)

        def rmsnorm(x, w):
            return x * jax.lax.rsqrt(jnp.mean(x * x, axis=-1, keepdims=True) + EPS) * w

        def rope_cache(L, hd):
            inv = 1.0 / ROPE_BASE ** (jnp.arange(0, hd, 2, dtype=jnp.float32) / hd)
            t = jnp.arange(L, dtype=jnp.float32)
            f = t[:, None] * inv[None, :]
            emb = jnp.concatenate([f, f], axis=-1)
            return (jnp.cos(emb), jnp.sin(emb))

        def apply_rope(x, cos, sin):
            d = x.shape[-1]
            x1, x2 = (x[..., :d // 2], x[..., d // 2:])
            rot = jnp.concatenate([-x2, x1], axis=-1)
            return x * cos + rot * sin

        def split_heads(x, n_heads):
            B, L, D = x.shape
            return x.reshape(B, L, n_heads, D // n_heads).transpose(0, 2, 1, 3)

        def merge_heads(x):
            B, h, L, d = x.shape
            return x.transpose(0, 2, 1, 3).reshape(B, L, h * d)

        def sdpa(q, k, v, bias):
            scale = q.shape[-1] ** (-0.5)
            s = jnp.einsum('bhqd,bhkd->bhqk', q, k) * scale + bias
            p = jax.nn.softmax(s, axis=-1)
            return jnp.einsum('bhqk,bhkd->bhqd', p, v)

        def forward(x, memory, seg_ids, Wqkv, bqkv, Wo, bo, Wq_c, Wkv_c, Wo_c, Wg, Wu, Wd, n1, n2, n3, nf):
            B, L, D = x.shape
            S = memory.shape[1]
            hd = D // H
            cos, sin = rope_cache(L, hd)
            i = jnp.arange(L)
            causal_bias = jnp.where(i[None, :] <= i[:, None], 0.0, NEG)[None, None]
            j = jnp.arange(S)
            allowed = (j[None, None, :] <= seg_ids[:, :, None]) & (j[None, None, :] > seg_ids[:, :, None] - LOOKBACK)
            cross_bias = jnp.where(allowed, 0.0, NEG)[:, None]
            for l in range(N_LAYERS):
                h = rmsnorm(x, n1[l])
                qkv = h @ Wqkv[l].T + bqkv[l]
                q, k, v = jnp.split(qkv, 3, axis=-1)
                q = apply_rope(split_heads(q, H), cos, sin)
                k = apply_rope(split_heads(k, H), cos, sin)
                v = split_heads(v, H)
                o = merge_heads(sdpa(q, k, v, causal_bias)) @ Wo[l].T + bo[l]
                x = x + o
                h2 = rmsnorm(x, n2[l])
                qc = split_heads(h2 @ Wq_c[l].T, H)
                kv = memory @ Wkv_c[l].T
                kc, vc = jnp.split(kv, 2, axis=-1)
                kc, vc = (split_heads(kc, H), split_heads(vc, H))
                oc = merge_heads(sdpa(qc, kc, vc, cross_bias)) @ Wo_c[l].T
                x = x + oc
                h3 = rmsnorm(x, n3[l])
                x = x + jax.nn.silu(h3 @ Wg[l].T) * (h3 @ Wu[l].T) @ Wd[l].T
            return rmsnorm(x, nf)
        key = jax.random.key(seed)
        ks = jax.random.split(key, 16)
        B, L, S, D, F = (2, 256, 32, 128, 512)
        w = 0.02
        inp = {'x': jax.random.normal(ks[0], (B, L, D), jnp.float32), 'memory': jax.random.normal(ks[1], (B, S, D), jnp.float32), 'seg_ids': jnp.sort(jax.random.randint(ks[2], (B, L), 0, S), axis=-1), 'Wqkv': jax.random.normal(ks[3], (N_LAYERS, 3 * D, D), jnp.float32) * w, 'bqkv': jnp.zeros((N_LAYERS, 3 * D), jnp.float32), 'Wo': jax.random.normal(ks[4], (N_LAYERS, D, D), jnp.float32) * w, 'bo': jnp.zeros((N_LAYERS, D), jnp.float32), 'Wq_c': jax.random.normal(ks[5], (N_LAYERS, D, D), jnp.float32) * w, 'Wkv_c': jax.random.normal(ks[6], (N_LAYERS, 2 * D, D), jnp.float32) * w, 'Wo_c': jax.random.normal(ks[7], (N_LAYERS, D, D), jnp.float32) * w, 'Wg': jax.random.normal(ks[8], (N_LAYERS, F, D), jnp.float32) * w, 'Wu': jax.random.normal(ks[9], (N_LAYERS, F, D), jnp.float32) * w, 'Wd': jax.random.normal(ks[10], (N_LAYERS, D, F), jnp.float32) * w, 'n1': jnp.ones((N_LAYERS, D), jnp.float32), 'n2': jnp.ones((N_LAYERS, D), jnp.float32), 'n3': jnp.ones((N_LAYERS, D), jnp.float32), 'nf': jnp.ones((D,), jnp.float32)}
        return inp
    _L2_xattn_all = _L2_xattn_setup()
    _L2_xattn_in = {k: v for k, v in _L2_xattn_all.items() if k in ('Wqkv', 'bqkv', 'Wo', 'bo', 'Wq_c', 'Wkv_c', 'Wo_c', 'Wg', 'Wu', 'Wd', 'n1', 'n2', 'n3', 'nf')}
    del _L2_xattn_all

    def _L2_ffn_setup():
        import jax, jax.numpy as jnp
        import numpy as np
        K = 2
        key = jax.random.key(seed)
        ks = jax.random.split(key, 9)
        B, S, D, O, E = (4, 128, 128, 128, 8)
        sc = 0.02
        return {'x': jax.random.normal(ks[0], (B, S, D), dtype=jnp.float32), 'gate_w': jax.random.normal(ks[1], (D, E), dtype=jnp.float32) * sc, 'gate_b': jax.random.normal(ks[2], (E,), dtype=jnp.float32) * sc, 'w1': jax.random.normal(ks[3], (E, D, O), dtype=jnp.float32) * sc, 'b1': jax.random.normal(ks[4], (E, O), dtype=jnp.float32) * sc, 'w2': jax.random.normal(ks[5], (E, O, O), dtype=jnp.float32) * sc, 'b2': jax.random.normal(ks[6], (E, O), dtype=jnp.float32) * sc, 'w3': jax.random.normal(ks[7], (E, O, O), dtype=jnp.float32) * sc, 'b3': jax.random.normal(ks[8], (E, O), dtype=jnp.float32) * sc}
    _L2_ffn_all = _L2_ffn_setup()
    _L2_ffn_in = {k: v for k, v in _L2_ffn_all.items() if k in ('gate_w', 'gate_b', 'w1', 'b1', 'w2', 'b2', 'w3', 'b3')}
    del _L2_ffn_all

    def _L3_xattn_setup():
        import jax, jax.numpy as jnp
        import numpy as np
        B, M, N, DIM, DH, H = (8, 512, 64, 128, 128, 8)
        INNER = DH * H
        EPS = 1e-05

        def _layernorm(x, g, b):
            mu = jnp.mean(x, axis=-1, keepdims=True)
            var = jnp.var(x, axis=-1, keepdims=True)
            return (x - mu) * jax.lax.rsqrt(var + EPS) * g + b
        key = jax.random.key(seed)
        ks = jax.random.split(key, 8)
        sd = 0.02
        return {'x': jax.random.normal(ks[0], (B, M, DIM), jnp.float32), 'latents': jax.random.normal(ks[1], (B, N, DIM), jnp.float32), 'gamma_media': jnp.ones((DIM,), jnp.float32), 'beta_media': jnp.zeros((DIM,), jnp.float32), 'gamma_lat': jnp.ones((DIM,), jnp.float32), 'beta_lat': jnp.zeros((DIM,), jnp.float32), 'Wq': jax.random.normal(ks[2], (DIM, INNER), jnp.float32) * sd, 'bq': jnp.zeros((INNER,), jnp.float32), 'Wkv': jax.random.normal(ks[3], (DIM, 2 * INNER), jnp.float32) * sd, 'bkv': jnp.zeros((2 * INNER,), jnp.float32), 'Wo': jax.random.normal(ks[4], (INNER, DIM), jnp.float32) * sd, 'bo': jnp.zeros((DIM,), jnp.float32)}
    _L3_xattn_all = _L3_xattn_setup()
    _L3_xattn_in = {k: v for k, v in _L3_xattn_all.items() if k in ('gamma_media', 'beta_media', 'gamma_lat', 'beta_lat', 'Wq', 'bq', 'Wkv', 'bkv', 'Wo', 'bo')}
    del _L3_xattn_all

    def _L3_ffn_setup():
        import jax, jax.numpy as jnp
        import numpy as np
        N_EXPERTS = 8
        D_MODEL = 128
        D_FF = 512
        TOP_K = 2
        B, S = (1, 256)
        key = jax.random.key(seed)
        ks = jax.random.split(key, 5)
        scale_in = 1.0 / np.sqrt(D_MODEL)
        scale_ff = 1.0 / np.sqrt(D_FF)
        return {'x': jax.random.normal(ks[0], (B, S, D_MODEL), dtype=jnp.float32), 'w_gate': jax.random.normal(ks[1], (D_MODEL, N_EXPERTS), dtype=jnp.float32) * scale_in, 'b_gate': jnp.zeros((N_EXPERTS,), dtype=jnp.float32), 'w1': jax.random.normal(ks[2], (N_EXPERTS, D_MODEL, D_FF), dtype=jnp.float32) * scale_in, 'b1': jnp.zeros((N_EXPERTS, D_FF), dtype=jnp.float32), 'w2': jax.random.normal(ks[3], (N_EXPERTS, D_FF, D_MODEL), dtype=jnp.float32) * scale_ff, 'b2': jnp.zeros((N_EXPERTS, D_MODEL), dtype=jnp.float32)}
    _L3_ffn_all = _L3_ffn_setup()
    _L3_ffn_in = {k: v for k, v in _L3_ffn_all.items() if k in ('w_gate', 'b_gate', 'w1', 'b1', 'w2', 'b2')}
    del _L3_ffn_all
    return {'x': x, 'ctx_1024': ctx_1024, 'itok_BxS_0_255': itok_BxS_0_255, 'L0_xattn_ln_l_w': _L0_xattn_in['ln_l_w'], 'L0_xattn_ln_l_b': _L0_xattn_in['ln_l_b'], 'L0_xattn_ln_c_w': _L0_xattn_in['ln_c_w'], 'L0_xattn_ln_c_b': _L0_xattn_in['ln_c_b'], 'L0_xattn_Wq': _L0_xattn_in['Wq'], 'L0_xattn_Wkv': _L0_xattn_in['Wkv'], 'L0_xattn_Wo': _L0_xattn_in['Wo'], 'L0_xattn_bo': _L0_xattn_in['bo'], 'L0_ffn_wq': _L0_ffn_in['wq'], 'L0_ffn_wk': _L0_ffn_in['wk'], 'L0_ffn_wv': _L0_ffn_in['wv'], 'L0_ffn_wo': _L0_ffn_in['wo'], 'L0_ffn_w1': _L0_ffn_in['w1'], 'L0_ffn_w2': _L0_ffn_in['w2'], 'L0_ffn_w3': _L0_ffn_in['w3'], 'L0_ffn_attn_norm_w': _L0_ffn_in['attn_norm_w'], 'L0_ffn_ff_norm_w': _L0_ffn_in['ff_norm_w'], 'L0_ffn_moe_norm_w': _L0_ffn_in['moe_norm_w'], 'L0_ffn_router_w': _L0_ffn_in['router_w'], 'L0_ffn_ew1': _L0_ffn_in['ew1'], 'L0_ffn_ew2': _L0_ffn_in['ew2'], 'L0_ffn_ew3': _L0_ffn_in['ew3'], 'L1_xattn_Wq': _L1_xattn_in['Wq'], 'L1_xattn_bq': _L1_xattn_in['bq'], 'L1_xattn_Wk': _L1_xattn_in['Wk'], 'L1_xattn_bk': _L1_xattn_in['bk'], 'L1_xattn_Wv': _L1_xattn_in['Wv'], 'L1_xattn_bv': _L1_xattn_in['bv'], 'L1_xattn_Wo': _L1_xattn_in['Wo'], 'L1_xattn_bo': _L1_xattn_in['bo'], 'L1_ffn_w12': _L1_ffn_in['w12'], 'L1_ffn_w3': _L1_ffn_in['w3'], 'L1_ffn_gate_w': _L1_ffn_in['gate_w'], 'L2_xattn_Wqkv': _L2_xattn_in['Wqkv'], 'L2_xattn_bqkv': _L2_xattn_in['bqkv'], 'L2_xattn_Wo': _L2_xattn_in['Wo'], 'L2_xattn_bo': _L2_xattn_in['bo'], 'L2_xattn_Wq_c': _L2_xattn_in['Wq_c'], 'L2_xattn_Wkv_c': _L2_xattn_in['Wkv_c'], 'L2_xattn_Wo_c': _L2_xattn_in['Wo_c'], 'L2_xattn_Wg': _L2_xattn_in['Wg'], 'L2_xattn_Wu': _L2_xattn_in['Wu'], 'L2_xattn_Wd': _L2_xattn_in['Wd'], 'L2_xattn_n1': _L2_xattn_in['n1'], 'L2_xattn_n2': _L2_xattn_in['n2'], 'L2_xattn_n3': _L2_xattn_in['n3'], 'L2_xattn_nf': _L2_xattn_in['nf'], 'L2_ffn_gate_w': _L2_ffn_in['gate_w'], 'L2_ffn_gate_b': _L2_ffn_in['gate_b'], 'L2_ffn_w1': _L2_ffn_in['w1'], 'L2_ffn_b1': _L2_ffn_in['b1'], 'L2_ffn_w2': _L2_ffn_in['w2'], 'L2_ffn_b2': _L2_ffn_in['b2'], 'L2_ffn_w3': _L2_ffn_in['w3'], 'L2_ffn_b3': _L2_ffn_in['b3'], 'L3_xattn_gamma_media': _L3_xattn_in['gamma_media'], 'L3_xattn_beta_media': _L3_xattn_in['beta_media'], 'L3_xattn_gamma_lat': _L3_xattn_in['gamma_lat'], 'L3_xattn_beta_lat': _L3_xattn_in['beta_lat'], 'L3_xattn_Wq': _L3_xattn_in['Wq'], 'L3_xattn_bq': _L3_xattn_in['bq'], 'L3_xattn_Wkv': _L3_xattn_in['Wkv'], 'L3_xattn_bkv': _L3_xattn_in['bkv'], 'L3_xattn_Wo': _L3_xattn_in['Wo'], 'L3_xattn_bo': _L3_xattn_in['bo'], 'L3_ffn_w_gate': _L3_ffn_in['w_gate'], 'L3_ffn_b_gate': _L3_ffn_in['b_gate'], 'L3_ffn_w1': _L3_ffn_in['w1'], 'L3_ffn_b1': _L3_ffn_in['b1'], 'L3_ffn_w2': _L3_ffn_in['w2'], 'L3_ffn_b2': _L3_ffn_in['b2']}

def reference(x, ctx_1024, itok_BxS_0_255, L0_xattn_ln_l_w, L0_xattn_ln_l_b, L0_xattn_ln_c_w, L0_xattn_ln_c_b, L0_xattn_Wq, L0_xattn_Wkv, L0_xattn_Wo, L0_xattn_bo, L0_ffn_wq, L0_ffn_wk, L0_ffn_wv, L0_ffn_wo, L0_ffn_w1, L0_ffn_w2, L0_ffn_w3, L0_ffn_attn_norm_w, L0_ffn_ff_norm_w, L0_ffn_moe_norm_w, L0_ffn_router_w, L0_ffn_ew1, L0_ffn_ew2, L0_ffn_ew3, L1_xattn_Wq, L1_xattn_bq, L1_xattn_Wk, L1_xattn_bk, L1_xattn_Wv, L1_xattn_bv, L1_xattn_Wo, L1_xattn_bo, L1_ffn_w12, L1_ffn_w3, L1_ffn_gate_w, L2_xattn_Wqkv, L2_xattn_bqkv, L2_xattn_Wo, L2_xattn_bo, L2_xattn_Wq_c, L2_xattn_Wkv_c, L2_xattn_Wo_c, L2_xattn_Wg, L2_xattn_Wu, L2_xattn_Wd, L2_xattn_n1, L2_xattn_n2, L2_xattn_n3, L2_xattn_nf, L2_ffn_gate_w, L2_ffn_gate_b, L2_ffn_w1, L2_ffn_b1, L2_ffn_w2, L2_ffn_b2, L2_ffn_w3, L2_ffn_b3, L3_xattn_gamma_media, L3_xattn_beta_media, L3_xattn_gamma_lat, L3_xattn_beta_lat, L3_xattn_Wq, L3_xattn_bq, L3_xattn_Wkv, L3_xattn_bkv, L3_xattn_Wo, L3_xattn_bo, L3_ffn_w_gate, L3_ffn_b_gate, L3_ffn_w1, L3_ffn_b1, L3_ffn_w2, L3_ffn_b2):
    import jax
    import jax.numpy as jnp

    def _L0_xattn_ref(latents, context, ln_l_w, ln_l_b, ln_c_w, ln_c_b, Wq, Wkv, Wo, bo):
        import jax, jax.numpy as jnp
        import numpy as np
        DIM = 128
        H = 16
        D = 64
        INNER = H * D
        EPS = 1e-05

        def layernorm(x, w, b):
            mu = jnp.mean(x, axis=-1, keepdims=True)
            var = jnp.var(x, axis=-1, keepdims=True)
            return (x - mu) * jax.lax.rsqrt(var + EPS) * w + b
        b, n, _ = latents.shape
        s = context.shape[1]
        lat = layernorm(latents, ln_l_w, ln_l_b)
        ctx = layernorm(context, ln_c_w, ln_c_b)
        q = (lat @ Wq).reshape(b, n, H, D).transpose(0, 2, 1, 3)
        kv = ctx @ Wkv
        k, v = jnp.split(kv, 2, axis=-1)
        k = k.reshape(b, s, H, D).transpose(0, 2, 1, 3)
        v = v.reshape(b, s, H, D).transpose(0, 2, 1, 3)
        scale = D ** (-0.5)
        attn = jnp.einsum('bhnd,bhsd->bhns', q, k) * scale
        attn = jnp.clip(attn, -11.0, 11.0)
        attn = jax.nn.softmax(attn, axis=-1)
        out = jnp.einsum('bhns,bhsd->bhnd', attn, v)
        out = out.transpose(0, 2, 1, 3).reshape(b, n, INNER)
        return out @ Wo + bo

    def _L0_ffn_ref(x, wq, wk, wv, wo, w1, w2, w3, attn_norm_w, ff_norm_w, moe_norm_w, router_w, ew1, ew2, ew3):
        import jax, jax.numpy as jnp
        import numpy as np
        D = 128
        H = 16
        FF = 512
        E = 8
        K = 2
        EH = 128
        B, S = (2, 256)
        EPS = 1e-05

        def rmsnorm(x, w):
            v = jnp.mean(jnp.square(x), axis=-1, keepdims=True)
            return x * jax.lax.rsqrt(v + EPS) * w

        def _dense_path(x, wq, wk, wv, wo, w1, w2, w3, attn_norm_w, ff_norm_w):
            b, s, d = x.shape
            hd = d // H
            q = (x @ wq).reshape(b, s, H, hd)
            k = (x @ wk).reshape(b, s, H, hd)
            v = (x @ wv).reshape(b, s, H, hd)
            scores = jnp.einsum('bqhd,bkhd->bhqk', q, k) / np.sqrt(hd).astype(np.float32)
            causal = jnp.tril(jnp.ones((s, s), bool))
            scores = jnp.where(causal, scores, jnp.finfo(scores.dtype).min)
            attn = jax.nn.softmax(scores, axis=-1)
            o = jnp.einsum('bhqk,bkhd->bqhd', attn, v).reshape(b, s, d)
            h = x + rmsnorm(o @ wo, attn_norm_w)
            ffn = jax.nn.silu(h @ w1) * (h @ w3) @ w2
            return h + rmsnorm(ffn, ff_norm_w)

        def _sparse_path(x, router_w, ew1, ew2, ew3, moe_norm_w):
            b, s, d = x.shape
            xt = x.reshape(-1, d)
            probs = jax.nn.softmax(xt @ router_w, axis=-1)
            topw, topi = jax.lax.top_k(probs, K)
            g = jax.nn.silu(jnp.einsum('td,edh->eth', xt, ew1)) * jnp.einsum('td,edh->eth', xt, ew3)
            eo = jnp.einsum('eth,ehd->ted', g, ew2)
            sel = jnp.take_along_axis(eo, topi[:, :, None], axis=1)
            moe_out = jnp.sum(topw[:, :, None] * sel, axis=1).reshape(b, s, d)
            return rmsnorm(moe_out, moe_norm_w)
        dense_out = _dense_path(x, wq, wk, wv, wo, w1, w2, w3, attn_norm_w, ff_norm_w)
        sparse_out = _sparse_path(x, router_w, ew1, ew2, ew3, moe_norm_w)
        return dense_out + sparse_out

    def _L1_xattn_ref(query, key, value, Wq, bq, Wk, bk, Wv, bv, Wo, bo):
        import jax, jax.numpy as jnp
        import numpy as np
        EMBED_DIM = 128
        NUM_HEADS = 16
        HEAD_DIM = EMBED_DIM // NUM_HEADS
        B, Sq, D = query.shape
        Sk = key.shape[1]
        H, Hd = (NUM_HEADS, HEAD_DIM)
        Q = (query @ Wq.T + bq).reshape(B, Sq, H, Hd).transpose(0, 2, 1, 3)
        K = (key @ Wk.T + bk).reshape(B, Sk, H, Hd).transpose(0, 2, 1, 3)
        V = (value @ Wv.T + bv).reshape(B, Sk, H, Hd).transpose(0, 2, 1, 3)
        scores = jnp.einsum('bhqd,bhkd->bhqk', Q, K) / jnp.sqrt(jnp.float32(Hd))
        attn = jax.nn.softmax(scores, axis=-1)
        out = jnp.einsum('bhqk,bhkd->bhqd', attn, V)
        out = out.transpose(0, 2, 1, 3).reshape(B, Sq, D)
        return out @ Wo.T + bo

    def _L1_ffn_ref(x, w12, w3, gate_w):
        import jax, jax.numpy as jnp
        import numpy as np
        TOP_K = 2
        E = gate_w.shape[0]
        H = w3.shape[-1]
        scores = jnp.einsum('btd,ed->bte', x, gate_w)
        topk_scores, topk_idx = jax.lax.top_k(scores, TOP_K)
        topk_probs = jax.nn.softmax(topk_scores, axis=-1)
        total_probs = jnp.sum(jax.nn.one_hot(topk_idx, E, dtype=topk_probs.dtype) * topk_probs[..., None], axis=-2)
        h12 = jnp.einsum('btd,ehd->bteh', x, w12)
        h1, h2 = (h12[..., :H], h12[..., H:])
        hidden = jax.nn.silu(h1) * h2
        expert_out = jnp.einsum('bteh,edh->bted', hidden, w3)
        y = jnp.sum(total_probs[..., None] * expert_out, axis=-2)
        return y

    def _L2_xattn_ref(x, memory, seg_ids, Wqkv, bqkv, Wo, bo, Wq_c, Wkv_c, Wo_c, Wg, Wu, Wd, n1, n2, n3, nf):
        import jax, jax.numpy as jnp
        import numpy as np
        N_LAYERS = 4
        H = 16
        LOOKBACK = 128
        EPS = 1e-06
        ROPE_BASE = 10000.0
        NEG = jnp.float32(-1e+30)

        def rmsnorm(x, w):
            return x * jax.lax.rsqrt(jnp.mean(x * x, axis=-1, keepdims=True) + EPS) * w

        def rope_cache(L, hd):
            inv = 1.0 / ROPE_BASE ** (jnp.arange(0, hd, 2, dtype=jnp.float32) / hd)
            t = jnp.arange(L, dtype=jnp.float32)
            f = t[:, None] * inv[None, :]
            emb = jnp.concatenate([f, f], axis=-1)
            return (jnp.cos(emb), jnp.sin(emb))

        def apply_rope(x, cos, sin):
            d = x.shape[-1]
            x1, x2 = (x[..., :d // 2], x[..., d // 2:])
            rot = jnp.concatenate([-x2, x1], axis=-1)
            return x * cos + rot * sin

        def split_heads(x, n_heads):
            B, L, D = x.shape
            return x.reshape(B, L, n_heads, D // n_heads).transpose(0, 2, 1, 3)

        def merge_heads(x):
            B, h, L, d = x.shape
            return x.transpose(0, 2, 1, 3).reshape(B, L, h * d)

        def sdpa(q, k, v, bias):
            scale = q.shape[-1] ** (-0.5)
            s = jnp.einsum('bhqd,bhkd->bhqk', q, k) * scale + bias
            p = jax.nn.softmax(s, axis=-1)
            return jnp.einsum('bhqk,bhkd->bhqd', p, v)

        def forward(x, memory, seg_ids, Wqkv, bqkv, Wo, bo, Wq_c, Wkv_c, Wo_c, Wg, Wu, Wd, n1, n2, n3, nf):
            B, L, D = x.shape
            S = memory.shape[1]
            hd = D // H
            cos, sin = rope_cache(L, hd)
            i = jnp.arange(L)
            causal_bias = jnp.where(i[None, :] <= i[:, None], 0.0, NEG)[None, None]
            j = jnp.arange(S)
            allowed = (j[None, None, :] <= seg_ids[:, :, None]) & (j[None, None, :] > seg_ids[:, :, None] - LOOKBACK)
            cross_bias = jnp.where(allowed, 0.0, NEG)[:, None]
            for l in range(N_LAYERS):
                h = rmsnorm(x, n1[l])
                qkv = h @ Wqkv[l].T + bqkv[l]
                q, k, v = jnp.split(qkv, 3, axis=-1)
                q = apply_rope(split_heads(q, H), cos, sin)
                k = apply_rope(split_heads(k, H), cos, sin)
                v = split_heads(v, H)
                o = merge_heads(sdpa(q, k, v, causal_bias)) @ Wo[l].T + bo[l]
                x = x + o
                h2 = rmsnorm(x, n2[l])
                qc = split_heads(h2 @ Wq_c[l].T, H)
                kv = memory @ Wkv_c[l].T
                kc, vc = jnp.split(kv, 2, axis=-1)
                kc, vc = (split_heads(kc, H), split_heads(vc, H))
                oc = merge_heads(sdpa(qc, kc, vc, cross_bias)) @ Wo_c[l].T
                x = x + oc
                h3 = rmsnorm(x, n3[l])
                x = x + jax.nn.silu(h3 @ Wg[l].T) * (h3 @ Wu[l].T) @ Wd[l].T
            return rmsnorm(x, nf)
        return forward(x, memory, seg_ids, Wqkv, bqkv, Wo, bo, Wq_c, Wkv_c, Wo_c, Wg, Wu, Wd, n1, n2, n3, nf)

    def _L2_ffn_ref(x, gate_w, gate_b, w1, b1, w2, b2, w3, b3):
        import jax, jax.numpy as jnp
        import numpy as np
        K = 2
        E = gate_w.shape[-1]
        logits = jnp.einsum('bsd,de->bse', x, gate_w) + gate_b
        probs = jax.nn.softmax(logits, axis=1)
        vals, idx = jax.lax.top_k(probs, K)
        h = jax.nn.relu(jnp.einsum('bsd,edo->ebso', x, w1) + b1[:, None, None, :])
        h = jax.nn.relu(jnp.einsum('ebso,eop->ebsp', h, w2) + b2[:, None, None, :])
        y = jax.nn.relu(jnp.einsum('ebso,eop->ebsp', h, w3) + b3[:, None, None, :])
        onehot = jax.nn.one_hot(idx, E, dtype=x.dtype)
        w_tok = jnp.einsum('bske,bsk->bse', onehot, vals)
        ind = onehot.max(axis=2)
        v = jnp.einsum('ebso,bse->eo', y, w_tok)
        out = jnp.einsum('bse,eo->bso', ind, v)
        return out

    def _L3_xattn_ref(x, latents, gamma_media, beta_media, gamma_lat, beta_lat, Wq, bq, Wkv, bkv, Wo, bo):
        import jax, jax.numpy as jnp
        import numpy as np
        B, M, N, DIM, DH, H = (8, 512, 64, 128, 128, 8)
        INNER = DH * H
        EPS = 1e-05

        def _layernorm(x, g, b):
            mu = jnp.mean(x, axis=-1, keepdims=True)
            var = jnp.var(x, axis=-1, keepdims=True)
            return (x - mu) * jax.lax.rsqrt(var + EPS) * g + b
        b = x.shape[0]
        xn = _layernorm(x, gamma_media, beta_media)
        ln = _layernorm(latents, gamma_lat, beta_lat)
        q = ln @ Wq + bq
        kv_input = jnp.concatenate([xn, ln], axis=1)
        kv = kv_input @ Wkv + bkv
        k, v = jnp.split(kv, 2, axis=-1)

        def to_heads(t):
            return t.reshape(b, t.shape[1], H, DH).transpose(0, 2, 1, 3)
        q, k, v = (to_heads(q), to_heads(k), to_heads(v))
        q = q * DH ** (-0.5)
        sim = jnp.einsum('bhid,bhjd->bhij', q, k)
        attn = jax.nn.softmax(sim, axis=-1)
        out = jnp.einsum('bhij,bhjd->bhid', attn, v)
        out = out.transpose(0, 2, 1, 3).reshape(b, -1, INNER)
        return out @ Wo + bo

    def _L3_ffn_ref(x, w_gate, b_gate, w1, b1, w2, b2):
        import jax, jax.numpy as jnp
        import numpy as np
        N_EXPERTS = 8
        D_MODEL = 128
        D_FF = 512
        TOP_K = 2
        B, S = (1, 256)
        d = x.shape[-1]
        xs = x.reshape(-1, d)
        T = xs.shape[0]
        gate_logits = xs @ w_gate + b_gate
        topk_vals, topk_idx = jax.lax.top_k(gate_logits, TOP_K)
        weights = jax.nn.softmax(topk_vals, axis=-1)
        comb = jnp.zeros((T, N_EXPERTS), dtype=xs.dtype)
        comb = comb.at[jnp.arange(T)[:, None], topk_idx].add(weights)
        h = jax.nn.relu(jnp.einsum('td,edf->etf', xs, w1) + b1[:, None, :])
        y = jnp.einsum('etf,efd->etd', h, w2) + b2[:, None, :]
        out = jnp.einsum('te,etd->td', comb, y)
        return out.reshape(x.shape)
    x = x + _L0_xattn_ref(_layernorm(x, axis=-1), ctx_1024, L0_xattn_ln_l_w, L0_xattn_ln_l_b, L0_xattn_ln_c_w, L0_xattn_ln_c_b, L0_xattn_Wq, L0_xattn_Wkv, L0_xattn_Wo, L0_xattn_bo)
    x = x + _L0_ffn_ref(_layernorm(x, axis=-1), L0_ffn_wq, L0_ffn_wk, L0_ffn_wv, L0_ffn_wo, L0_ffn_w1, L0_ffn_w2, L0_ffn_w3, L0_ffn_attn_norm_w, L0_ffn_ff_norm_w, L0_ffn_moe_norm_w, L0_ffn_router_w, L0_ffn_ew1, L0_ffn_ew2, L0_ffn_ew3)
    x = x + _L1_xattn_ref(_layernorm(x, axis=-1), ctx_1024, ctx_1024, L1_xattn_Wq, L1_xattn_bq, L1_xattn_Wk, L1_xattn_bk, L1_xattn_Wv, L1_xattn_bv, L1_xattn_Wo, L1_xattn_bo)
    x = x + _L1_ffn_ref(_layernorm(x, axis=-1), L1_ffn_w12, L1_ffn_w3, L1_ffn_gate_w)
    x = x + _L2_xattn_ref(_layernorm(x, axis=-1), ctx_1024, itok_BxS_0_255, L2_xattn_Wqkv, L2_xattn_bqkv, L2_xattn_Wo, L2_xattn_bo, L2_xattn_Wq_c, L2_xattn_Wkv_c, L2_xattn_Wo_c, L2_xattn_Wg, L2_xattn_Wu, L2_xattn_Wd, L2_xattn_n1, L2_xattn_n2, L2_xattn_n3, L2_xattn_nf)
    x = x + _L2_ffn_ref(_layernorm(x, axis=-1), L2_ffn_gate_w, L2_ffn_gate_b, L2_ffn_w1, L2_ffn_b1, L2_ffn_w2, L2_ffn_b2, L2_ffn_w3, L2_ffn_b3)
    x = x + _L3_xattn_ref(ctx_1024, _layernorm(x, axis=-1), L3_xattn_gamma_media, L3_xattn_beta_media, L3_xattn_gamma_lat, L3_xattn_beta_lat, L3_xattn_Wq, L3_xattn_bq, L3_xattn_Wkv, L3_xattn_bkv, L3_xattn_Wo, L3_xattn_bo)
    x = x + _L3_ffn_ref(_layernorm(x, axis=-1), L3_ffn_w_gate, L3_ffn_b_gate, L3_ffn_w1, L3_ffn_b1, L3_ffn_w2, L3_ffn_b2)
    return x

_drawn_inputs = setup_inputs


def setup_inputs(seed=0):
    import zlib

    import numpy as np

    out = dict(_drawn_inputs(seed))
    spreads = {'L0_xattn_ln_l_w': (1.0, 0.2),
     'L0_xattn_ln_l_b': (0.0, 0.1),
     'L0_xattn_ln_c_w': (1.0, 0.2),
     'L0_xattn_ln_c_b': (0.0, 0.1),
     'L0_xattn_bo': (0.0, 0.1),
     'L0_ffn_attn_norm_w': (1.0, 0.2),
     'L0_ffn_ff_norm_w': (1.0, 0.2),
     'L0_ffn_moe_norm_w': (1.0, 0.2),
     'L1_xattn_bq': (0.0, 0.463),
     'L1_xattn_bk': (0.0, 2.0),
     'L1_xattn_bv': (0.0, 0.1),
     'L1_xattn_bo': (0.0, 0.1),
     'L2_xattn_bqkv': (0.0, 0.626),
     'L2_xattn_bo': (0.0, 0.1),
     'L2_xattn_n1': (1.0, 0.6),
     'L2_xattn_n2': (1.0, 0.6),
     'L2_xattn_n3': (1.0, 0.6),
     'L2_xattn_nf': (1.0, 0.2),
     'L3_xattn_gamma_media': (1.0, 0.6),
     'L3_xattn_beta_media': (0.0, 2.0),
     'L3_xattn_gamma_lat': (1.0, 0.6),
     'L3_xattn_beta_lat': (0.0, 2.0),
     'L3_xattn_bq': (0.0, 2.0),
     'L3_xattn_bkv': (0.0, 0.356),
     'L3_xattn_bo': (0.0, 0.377),
     'L3_ffn_b_gate': (0.0, 0.275),
     'L3_ffn_b1': (0.0, 0.557),
     'L3_ffn_b2': (0.0, 0.392)}
    factors = {'L0_ffn_wq': 4.611,
     'L0_ffn_wk': 4.801,
     'L2_xattn_Wq_c': 8.0,
     'L2_xattn_Wkv_c': 3.147,
     'L2_xattn_Wo_c': 2.84,
     'L2_xattn_Wg': 5.492,
     'L2_xattn_Wu': 6.576,
     'L2_xattn_Wd': 6.019,
     'L2_ffn_gate_w': 8.0,
     'L2_ffn_gate_b': 64.0,
     'L2_ffn_w1': 8.0,
     'L2_ffn_b1': 8.0,
     'L2_ffn_w2': 8.0,
     'L2_ffn_b2': 8.0,
     'L2_ffn_w3': 8.0,
     'L2_ffn_b3': 8.0,
     'L3_xattn_Wq': 51.683}
    for name, (base, spread) in spreads.items():
        noise = np.random.default_rng([zlib.crc32(name.encode()), seed]).standard_normal(out[name].shape)
        drawn = base * np.exp(spread * noise) if base else spread * noise
        out[name] = jnp.asarray(drawn.astype(out[name].dtype))
    for name, factor in factors.items():
        out[name] = (out[name] * factor).astype(out[name].dtype)
    return out
```

```python
from contextlib import ExitStack, contextmanager

import numpy as np

import concourse.bass as bass
from concourse import mybir

ALU = mybir.AluOpType
ACT = mybir.ActivationFunctionType
AX = mybir.AxisListType
F32 = mybir.dt.float32
F16 = mybir.dt.float16
BF16 = mybir.dt.bfloat16
I32 = mybir.dt.int32

P = 128
B, S = 2, 512
T = B * S
NT = T // P
NTB = S // P
CK = 32
H = 16
HD = P // H
HROWS = 32
HPC = P // HROWS
NC = H // HPC
ONE_ROW = 3 * HD
NEG = -1e30
SIGNALS = 24
E8 = 8
L2_LAYERS = 4
H3 = 8
LOOKBACK = 128


class Core:

    def __init__(self, nc, ctx, ins, out):
        self.nc, self.ctx, self.ins, self.out = nc, ctx, ins, out
        self.sets = [[ctx.enter_context(nc.semaphore(f"stage_{i}_signal_{j}")) for j in range(SIGNALS)]
                     for i in range(2)]
        self.n_stages = 0

    def sbuf(self, name, shape, dt=F32):
        return self.ctx.enter_context(self.nc.sbuf_tensor(name, shape, dt))

    def eps_col(self, eps):
        return self.eps[:, 0:1] if eps == 1e-5 else self.eps[:, 1:2]

    @contextmanager
    def stage(self):
        mine, idle = self.sets[self.n_stages % 2], self.sets[1 - self.n_stages % 2]
        self.n_stages += 1
        with self.nc.Block(no_gpsimd_drain=True) as block:
            @block.gpsimd
            def _(pool):
                pool.sem_clear(range(idle[0].num, idle[-1].num + 1))
            yield block, mine


def chained(engine, done):
    count = [0]

    def link(instruction):
        count[0] += 1
        instruction.then_inc(done, 1)
        engine.wait_ge(done, count[0])
    return link


LAYOUTS = {
    "consts": dict(ident=P, pick_sum=P, head_rows=H, head_rows_scaled=H, half_rows=2, half_rows_scaled=2,
                   stack_rows=HPC, one_row=1, zero=1, lower=E8 * E8, cos=S, sin=S, keys=CK),
    "l0x": dict(wq_t=8 * P, wk=8 * P, wv=8 * P, wo=8 * P, lat_w=1, lat_b=1, ctx_w=1, ctx_b=1, bo=P),
    "l0f": dict(wq=P, wk=P, wv=P, wo_stacked=NC * P, w1=4 * P, w3=4 * P, w2=4 * P, router=E8,
                ew1=E8 * P, ew3=E8 * P, ew2=E8 * P, attn_w=P, ff_w=P, moe_w=P),
    "l1x": dict(wq=P, wk_t=P, wv_t=P, wo_t=P, bq=1, bk=1, bv=1, bo=P),
    "l1f": dict(w12_t=E8 * 4 * P, w3_t=E8 * 2 * P, gate=E8),
    "l2a": dict(wq=P, wq_turned=P, wk=P, wk_turned=P, wv=P, wo_stacked=NC * P, wo_t=P, bo=P,
                wq_cross=P, wk_cross=P, wv_cross=P, wo_cross=P,
                bq=1, bq_turned=1, bk=1, bk_turned=1, bv=1, n1=1, n2=1, n3=1),
    "l2b": dict(wg=4 * P, wu=4 * P, wd=4 * P),
    "l2f": dict(w1=E8 * P, w2=E8 * P, w3=E8 * P, b1=E8, b2=E8, b3=E8, gate=E8, gate_b=1, nf=P),
    "l3x": dict(wq=H3 * P, wk=H3 * P, wv=H3 * P, wo=H3 * P, bq=H3, bk=H3, bv=H3, bo=P,
                media_w=1, media_b=1, lat_w=1, lat_b=1),
    "l3f": dict(w1=E8 * 4 * P, w2=E8 * 4 * P, b1=E8 * 4, gate=E8, gate_b=E8, b2=P),
}


def width(blob):
    return sum(LAYOUTS[blob].values())


class Fields:

    def __init__(self, region, blob, start=0):
        self.all = region[:, start:start + width(blob)]
        self.parts = {}
        for name, n in LAYOUTS[blob].items():
            self.parts[name] = region[:, start:start + n]
            start += n

    def __getitem__(self, name):
        return self.parts[name]

    def tiled(self, name, w=P):
        return self.parts[name].rearrange("p (a w) -> p a w", w=w)


def load(sp, fields, source, landed):
    sp.dma_start(fields.all, source).then_inc(landed, 16)
    sp.wait_ge(landed, 16)


def norm(core, src, xn, xt, mode, eps, scale=None, bias=None, extra=None):
    nc, ps, ident = core.nc, core.ps, core.consts["ident"]
    with core.stage() as (block, (stats_ready, means_ready, log_ready, rstd_ready, tile_ready, turned,
                                  landed, turned_out, *_)):
        if extra is not None:
            @block.sync
            def _(sp):
                extra(sp, landed)

        @block.vector
        def _(dve):
            for n in range(NT):
                if mode == "layer":
                    nc.vector.bn_stats(core.stats[:, n, :], src[:, n, :]).then_inc(stats_ready, 1)
                else:
                    nc.vector.scalar_tensor_tensor(core.junk[:, n, :], src[:, n, :], 1.0, src[:, n, :], ALU.mult,
                                                   ALU.mult, accum_out=core.mean_var[:, n, 1:2]).then_inc(means_ready, 1)
            if mode == "layer":
                for n in range(NT):
                    dve.wait_ge(stats_ready, n + 1)
                    nc.vector.bn_aggr(core.mean_var[:, n, :], core.stats[:, n, :]).then_inc(means_ready, 1)
            dve.wait_ge(rstd_ready, 1)
            for n in range(NT):
                if mode == "layer":
                    nc.vector.tensor_scalar(xn[:, n, :], src[:, n, :], core.mean_var[:, n, 0:1], core.rstd[:, n:n + 1],
                                            ALU.subtract, ALU.mult).then_inc(tile_ready, 1)
                else:
                    nc.vector.tensor_scalar(xn[:, n, :], src[:, n, :], core.rstd[:, n:n + 1], None,
                                            ALU.mult).then_inc(tile_ready, 1)
            if xt is not None:
                dve.wait_ge(turned, NT)
                if scale is None:
                    nc.vector.tensor_copy(xt[:, S:T], ps[:, 1, :]).then_inc(turned_out, 1)
                elif bias is None:
                    nc.vector.tensor_scalar(xt[:, S:T], ps[:, 1, :], scale, None, ALU.mult).then_inc(turned_out, 1)
                else:
                    nc.vector.tensor_scalar(xt[:, S:T], ps[:, 1, :], scale, bias, ALU.mult, ALU.add).then_inc(turned_out, 1)

        @block.scalar
        def _(act):
            act.wait_ge(means_ready, NT)
            nc.scalar.activation(core.log_var[:, :], core.mean_var[:, :, 1], ACT.Ln, bias=core.eps_col(eps),
                                 scale=1.0 if mode == "layer" else 1.0 / P).then_inc(log_ready, 1)
            act.wait_ge(log_ready, 1)
            nc.scalar.activation(core.rstd[:, :], core.log_var[:, :], ACT.Exp, scale=-0.5).then_inc(rstd_ready, 1)
            if xt is not None:
                act.wait_ge(turned, NTB)
                kw = {}
                if scale is not None:
                    kw["scale"] = scale
                if bias is not None:
                    kw["bias"] = bias
                nc.scalar.activation(xt[:, 0:S], ps[:, 0, :], ACT.Identity, **kw).then_inc(turned_out, 1)

        if xt is not None:
            @block.tensor
            def _(pe):
                for n in range(NT):
                    pe.wait_ge(tile_ready, n + 1)
                    nc.tensor.transpose(ps[:, n // NTB, (n % NTB) * P:(n % NTB + 1) * P], xn[:, n, :],
                                        ident).then_inc(turned, 1)


def add_rows(core, dst, rows):
    nc = core.nc
    with core.stage() as (block, (added, *_)):
        @block.vector
        def _(dve):
            nc.vector.tensor_tensor(dst, dst, rows.unsqueeze(1).to_broadcast([P, NT, P]), ALU.add).then_inc(added, 1)


def turn_rows(core, src, xt):
    nc, ps = core.nc, core.ps
    with core.stage() as (block, (turned, turned_out, *_)):
        @block.tensor
        def _(pe):
            for n in range(NT):
                nc.tensor.transpose(ps[:, n // NTB, (n % NTB) * P:(n % NTB + 1) * P], src[:, n, :],
                                    core.consts["ident"]).then_inc(turned, 1)

        @block.scalar
        def _(act):
            act.wait_ge(turned, NTB)
            nc.scalar.activation(xt[:, 0:S], ps[:, 0, :], ACT.Copy).then_inc(turned_out, 1)

        @block.vector
        def _(dve):
            dve.wait_ge(turned, NT)
            nc.vector.tensor_copy(xt[:, S:T], ps[:, 1, :]).then_inc(turned_out, 1)


def rms_add(core, v, weight, base, dst, eps=1e-5):
    nc = core.nc
    norm(core, v, v, None, "rms", eps)
    with core.stage() as (block, (scaled, added, *_)):
        @block.vector
        def _(dve):
            nc.vector.tensor_tensor(v, v, weight.unsqueeze(1).to_broadcast([P, NT, P]), ALU.mult).then_inc(scaled, 1)
            dve.wait_ge(scaled, 1)
            nc.vector.tensor_tensor(dst, base, v, ALU.add).then_inc(added, 1)


def fold_context(core, w, ctx_t, wk, wv, wq, wo, head_mask, value_mask, bq=None, bk=None, bv=None):
    nc, ps = core.nc, core.ps
    with core.stage() as (block, (kv_ready, spread, product, evacuated, *_)):
        @block.tensor
        def _(pe):
            nc.tensor.matmul(ps[:, 0, 0:B * CK], wk, ctx_t, start=True, stop=True)
            nc.tensor.matmul(ps[:, 1, 0:B * CK], wv, ctx_t, start=True, stop=True).then_inc(kv_ready, 1)
            pe.wait_ge(spread, 2)
            for b in range(B):
                nc.tensor.matmul(ps[:, 2 + b, :], wq, core.k_spread[:, b, :], start=True, stop=True).then_inc(product, 1)
            if bq is not None:
                for b in range(B):
                    nc.tensor.matmul(ps[:, 6 + b, :], bq.to_broadcast([P, P]), core.k_spread[:, b, :],
                                     start=True, stop=True).then_inc(product, 1)
            pe.wait_ge(spread, 4)
            for b in range(B):
                for c in range(NC):
                    last = nc.tensor.matmul(ps[:, 4 + b, c * P:(c + 1) * P], core.v_spread[:, b, c * P:(c + 1) * P], wo,
                                            start=True, stop=True)
                last.then_inc(product, 1)

        @block.vector
        def _(dve):
            dve.wait_ge(kv_ready, 1)
            for bank, dst, mask, bias in ((0, core.k_spread, head_mask, bk), (1, core.v_spread, value_mask, bv)):
                for b in range(B):
                    nc.vector.scalar_tensor_tensor(
                        dst[:, b, :].rearrange("p (h k) -> p h k", k=CK),
                        ps[:, bank, b * CK:(b + 1) * CK].unsqueeze(1).to_broadcast([P, H, CK]),
                        bias if bias is not None else core.consts["zero"],
                        mask.unsqueeze(2).to_broadcast([P, H, CK]), ALU.add, ALU.mult).then_inc(spread, 1)
            dve.wait_ge(product, 2)
            nc.vector.tensor_copy(core.a[:, :, :], ps[:, 2:4, :]).then_inc(evacuated, 1)
            if bq is not None:
                dve.wait_ge(product, 4)
                nc.vector.tensor_copy(core.q_bias[:, :, :], ps[:, 6:8, :]).then_inc(evacuated, 1)

        @block.scalar
        def _(act):
            act.wait_ge(product, 4 + (2 if bq is not None else 0))
            nc.scalar.activation(core.bb[:, :, :], ps[:, 4:6, :], ACT.Copy).then_inc(evacuated, 1)


def fold_context_l0(core, w, ctx_t):
    nc, ps = core.nc, core.ps
    n_chunks = 8
    wq_t, wk, wv, wo = (w.tiled(n) for n in ("wq_t", "wk", "wv", "wo"))
    with core.stage() as (block, (kv_ready, spread, product, evacuated, *_)):
        @block.tensor
        def _(pe):
            for bank, weights in ((0, wk), (1, wv)):
                for i in range(n_chunks):
                    last = nc.tensor.matmul(ps[:, bank, i * B * CK:(i + 1) * B * CK], weights[:, i, :], ctx_t,
                                            start=True, stop=True)
            last.then_inc(kv_ready, 1)
            pe.wait_ge(spread, 4)
            for b in range(B):
                for i in range(n_chunks):
                    last = nc.tensor.matmul(ps[:, 2 + b, 64 * i:64 * i + 64], wq_t[:, i, :],
                                            core.k_spread[:, b, 64 * i:64 * i + 64], start=True, stop=True)
                last.then_inc(product, 1)
            for b in range(B):
                for i in range(n_chunks):
                    rows = 64 * (i % 2)
                    last = nc.tensor.matmul(ps[rows:rows + 64, 4 + b, (i // 2) * P:(i // 2 + 1) * P],
                                            core.v_spread[:, b, 64 * i:64 * i + 64], wo[:, i, :],
                                            start=True, stop=True)
                last.then_inc(product, 1)

        @block.vector
        def _(dve):
            dve.wait_ge(kv_ready, 1)
            for bank, dst, mask in ((0, core.k_spread, core.consts["half_rows_scaled"]),
                                    (1, core.v_spread, core.consts["half_rows"])):
                kv = ps[:, bank, :].rearrange("p (i b k) -> p i b k", b=B, k=CK)
                for b in range(B):
                    out = dst[:, b, :].rearrange("p (i r k) -> p i r k", r=2, k=CK)
                    for r in range(2):
                        last = nc.vector.tensor_scalar(out[:, :, r, :], kv[:, :, b, :], mask[:, r:r + 1], None, ALU.mult)
                    last.then_inc(spread, 1)
            dve.wait_ge(product, 2)
            nc.vector.tensor_copy(core.a[:, :, :], ps[:, 2:4, :]).then_inc(evacuated, 1)

        @block.scalar
        def _(act):
            act.wait_ge(product, 4)
            nc.scalar.activation(core.bb[:, :, :], ps[:, 4:6, :], ACT.Copy).then_inc(evacuated, 1)


def cross_attention(core, x_t, resid, mode, rows=None, extra=None):
    nc, ps, ident = core.nc, core.ps, core.consts["ident"]
    with core.stage() as (block, (scores_ready, probs_raw, exp_ready, probs_ready, turned, turned_out, output_ready,
                                  added, link_signal, landed, *_)):
        if extra is not None:
            @block.sync
            def _(sp):
                extra(sp, landed)

        @block.tensor
        def _(pe):
            for n in range(NT + 2):
                if n < NT:
                    if n >= 2:
                        pe.wait_ge(probs_raw, n - 1)
                    nc.tensor.matmul(ps[:, n % 2, :], x_t[:, n * P:(n + 1) * P], core.a[:, n // NTB, :],
                                     start=True, stop=True).then_inc(scores_ready, 1)
                m = n - 1
                if 0 <= m < NT:
                    pe.wait_ge(probs_ready, m + 1)
                    if m >= 2:
                        pe.wait_ge(turned_out, m - 1)
                    for c in range(NC):
                        last = nc.tensor.transpose(ps[:, 2 + m % 2, c * P:(c + 1) * P],
                                                   core.probs[:, m % 2, c * P:(c + 1) * P], ident)
                    last.then_inc(turned, 1)
                m = n - 2
                if 0 <= m < NT:
                    pe.wait_ge(turned_out, m + 1)
                    if m >= 2:
                        pe.wait_ge(added, m - 1)
                    for c in range(NC):
                        last = nc.tensor.matmul(ps[:, 4 + m % 2, 0:P], core.probs_t[:, m % 2, c * P:(c + 1) * P],
                                                core.bb[:, m // NTB, c * P:(c + 1) * P], start=(c == 0), stop=(c == NC - 1))
                    last.then_inc(output_ready, 1)

        @block.scalar
        def _(act):
            for n in range(NT + 1):
                if n < NT:
                    act.wait_ge(probs_raw, n + 1)
                    if n >= 2:
                        act.wait_ge(turned, n - 1)
                    nc.scalar.activation(core.probs[:, n % 2, :], core.shifted[:, n % 2, :], ACT.Exp).then_inc(exp_ready, 1)
                m = n - 1
                if m >= 0:
                    act.wait_ge(turned, m + 1)
                    if m >= 2:
                        act.wait_ge(output_ready, m - 1)
                    nc.scalar.activation(core.probs_t[:, m % 2, :], ps[:, 2 + m % 2, :], ACT.Copy).then_inc(turned_out, 1)

        @block.vector
        def _(dve):
            link = chained(dve, link_signal)
            if rows is not None:
                link(nc.vector.tensor_tensor(resid, resid, rows.unsqueeze(1).to_broadcast([P, NT, P]), ALU.add))
            for n in range(NT + 2):
                if n < NT:
                    dve.wait_ge(scores_ready, n + 1)
                    if n >= 2:
                        dve.wait_ge(exp_ready, n - 1)
                    shifted = core.shifted[:, n % 2, :]
                    if mode == "clip":
                        nc.vector.tensor_scalar(shifted, ps[:, n % 2, :], 11.0, -11.0, ALU.min, ALU.max).then_inc(probs_raw, 1)
                    else:
                        by_head = shifted.rearrange("p (h k) -> p h k", k=CK)
                        if mode == "bias":
                            link(nc.vector.tensor_tensor(shifted, ps[:, n % 2, :], core.q_bias[:, n // NTB, :], ALU.add))
                        else:
                            link(nc.vector.tensor_tensor(
                                by_head, ps[:, n % 2, :].rearrange("p (h k) -> p h k", k=CK),
                                core.key_mask[:, n, :].unsqueeze(1).to_broadcast([P, H, CK]), ALU.add))
                        link(nc.vector.tensor_reduce(core.row_max[:, :], by_head, AX.X, ALU.max))
                        nc.vector.tensor_tensor(by_head, by_head, core.row_max[:, :].unsqueeze(2).to_broadcast([P, H, CK]),
                                                ALU.subtract).then_inc(probs_raw, 1)
                m = n - 1
                if 0 <= m < NT:
                    dve.wait_ge(exp_ready, m + 1)
                    by_head = core.probs[:, m % 2, :].rearrange("p (h k) -> p h k", k=CK)
                    link(nc.vector.tensor_reduce(core.row_sum[:, :], by_head, AX.X, ALU.add))
                    link(nc.vector.reciprocal(core.row_rsum[:, :], core.row_sum[:, :]))
                    nc.vector.tensor_tensor(by_head, by_head, core.row_rsum[:, :].unsqueeze(2).to_broadcast([P, H, CK]),
                                            ALU.mult).then_inc(probs_ready, 1)
                m = n - 2
                if 0 <= m < NT:
                    dve.wait_ge(output_ready, m + 1)
                    nc.vector.tensor_tensor(resid[:, m, :], resid[:, m, :], ps[:, 4 + m % 2, 0:P], ALU.add).then_inc(added, 1)


def project_heads(core, x_t, wq, wk, wv, turned=None, bias=None):
    nc, ps = core.nc, core.ps
    cos, sin = core.consts["cos"], core.consts["sin"]
    with core.stage() as (block, (qk_ready, whole, high_ready, low_ready, stacked, even_out, odd_out, v_ready,
                                  v_out, link_signal, *_)):
        @block.tensor
        def _(pe):
            weights = [wq, wk] + (list(turned) if turned else [])
            for i, weight in enumerate(weights):
                for b in range(B):
                    last = nc.tensor.matmul(ps[:, 2 * i + b, :], weight, x_t[:, b * S:(b + 1) * S], start=True, stop=True)
                last.then_inc(qk_ready, 1)
            n = 0
            for i, (pick_high, pick_low) in enumerate(((core.pick[:, 0], core.pick[:, 1]), (core.pick[:, 2], core.pick[:, 3]))):
                pe.wait_ge(low_ready, i + 1)
                for c in range(NC):
                    bank = 2 * (n % 2)
                    if n >= 2:
                        pe.wait_ge(even_out if n % 2 == 0 else odd_out, n // 2)
                    if n == 1:
                        pe.wait_ge(low_ready, 2)
                    for b in range(B):
                        half = slice(b * S, (b + 1) * S)
                        nc.tensor.matmul(ps[:, bank + b, :], pick_high[:, c, :], core.high[:, i, half], start=True, stop=False)
                        last = nc.tensor.matmul(ps[:, bank + b, :], pick_low[:, c, :], core.low[:, i, half], start=False, stop=True)
                    last.then_inc(stacked, 1)
                    n += 1
            for n in range(NT):
                last = nc.tensor.matmul(ps[:, 4 + n // NTB, (n % NTB) * P:(n % NTB + 1) * P], x_t[:, n * P:(n + 1) * P], wv,
                                        start=True, stop=True)
                if n % NTB == NTB - 1:
                    last.then_inc(v_ready, 1)

        def two_banks(bank):
            return ps[:, bank:bank + 2, :]

        def v_target(b):
            return core.v_ones[:, b * NTB:(b + 1) * NTB, :, 0:HD]

        def v_source(b):
            return ps[:, 4 + b, :].rearrange("p (n h d) -> p n h d", n=NTB, h=H)

        def evacuate_stack(engine, n):
            target = (core.q_stack if n < NC else core.k_stack)[:, n % NC, :].rearrange("p (b s) -> p b s", b=B)
            source = two_banks(2 * (n % 2))
            if n % 2 == 0:
                if n < NC:
                    nc.scalar.activation(target, source, ACT.Identity).then_inc(even_out, 1)
                else:
                    nc.scalar.activation(target, source, ACT.Identity, bias=core.consts["one_row"]).then_inc(even_out, 1)
            else:
                nc.vector.tensor_scalar(target, source, core.consts["zero" if n < NC else "one_row"], None,
                                        ALU.add).then_inc(odd_out, 1)

        @block.scalar
        def _(act):
            for i in range(2):
                if turned:
                    act.wait_ge(whole, i + 1)
                    source = core.rotated[:, i, :]
                else:
                    act.wait_ge(qk_ready, i + 1)
                    source = two_banks(2 * i)
                nc.scalar.activation(core.high[:, i, :] if turned else core.high[:, i, :].rearrange("p (b s) -> p b s", b=B),
                                     source, ACT.Copy).then_inc(high_ready, 1)
            for n in range(0, 2 * NC, 2):
                act.wait_ge(stacked, n + 1)
                evacuate_stack(act, n)
                if n == NC:
                    act.wait_ge(v_ready, 1)
                    nc.scalar.activation(v_target(0), v_source(0), ACT.Copy).then_inc(v_out, 1)

        @block.vector
        def _(dve):
            link = chained(dve, link_signal)

            def by_batch(ap):
                return ap.rearrange("p (b s) -> p b s", b=B)

            for i in range(2):
                if turned:
                    for bank, table, dst, column in ((2 * i, cos, core.rotated[:, i, :], bias[2 * i]),
                                                     (2 * i + 4, sin, core.turn_part[:, :], bias[2 * i + 1])):
                        dve.wait_ge(qk_ready, bank // 2 + 1)
                        link(nc.vector.scalar_tensor_tensor(by_batch(dst), two_banks(bank), column,
                                                            table.unsqueeze(1).to_broadcast([P, B, S]), ALU.add, ALU.mult))
                    nc.vector.tensor_tensor(core.rotated[:, i, :], core.rotated[:, i, :], core.turn_part[:, :],
                                            ALU.add).then_inc(whole, 1)
                    dve.wait_ge(whole, i + 1)
                    dve.wait_ge(high_ready, i + 1)
                    nc.vector.tensor_tensor(core.low[:, i, :], core.rotated[:, i, :], core.high[:, i, :],
                                            ALU.subtract).then_inc(low_ready, 1)
                else:
                    dve.wait_ge(high_ready, i + 1)
                    nc.vector.tensor_tensor(by_batch(core.low[:, i, :]), two_banks(2 * i), by_batch(core.high[:, i, :]),
                                            ALU.subtract).then_inc(low_ready, 1)
            for n in range(1, 2 * NC, 2):
                dve.wait_ge(stacked, n + 1)
                evacuate_stack(dve, n)
            dve.wait_ge(v_ready, 2)
            nc.vector.tensor_copy(v_target(1), v_source(1)).then_inc(v_out, 1)


UNITS = B * NC
GROUPS = 2 * NTB


def self_attention(core, extra=None):
    nc, ps = core.nc, core.ps
    ident, ident_b = core.consts["ident"], core.masks[:, 0, :]
    mask_rows, mask_cols = core.masks[:, 1, :], core.masks[:, 2, :]
    PLACE = {0: (4, 0, 0), 1: (5, 0, S), 3: (5, S - P, 2 * S - P), 2: (6, 0, 2 * S)}
    PIECES = ((4, (0,), 0, S), (5, (1, 3), S, S), (6, (2,), 2 * S, S // 2))

    with core.stage() as (block, (keys_masked, rows_ready, max_ready, max_turned, max_added, scores_ready, exp_ready,
                                  sums_in, attended_raw, raw_out, sums_ready, rsum_ready, attended_ready, landed,
                                  sent, *_)):
        if extra is not None:
            @block.sync
            def _(sp):
                extra(sp, landed)

        @block.tensor
        def _(pe):
            def maxima(u, g):
                b, c, pair, i = u // NC, u % NC, g // NTB, g % NTB
                n = u * GROUPS + g
                if g == 0:
                    pe.wait_ge(keys_masked, HPC * (u + 1))
                    if u >= 1:
                        pe.wait_ge(max_added, u)
                if n >= 2:
                    pe.wait_ge(max_ready, n - 1)
                for k in range(2):
                    j = 2 * pair + k
                    out = ps[:, 2 * (n % 2) + k, :]
                    nc.tensor.matmul(out[:, 0:(i + 1) * P], core.q_stack[:, c, b * S + i * P:b * S + (i + 1) * P],
                                     core.k_head[:, (u % 2) * HPC + j, 0:(i + 1) * P], start=True, stop=False)
                    last = nc.tensor.matmul(out[:, i * P:(i + 1) * P], ident_b, mask_rows, start=False, stop=True)
                last.then_inc(rows_ready, 1)

            def turn_maxima(u):
                pe.wait_ge(max_ready, GROUPS * (u + 1))
                for i in range(NTB):
                    last = nc.tensor.transpose(ps[:, 0, i * P:(i + 1) * P], core.minus_max[:, u % 2, i, :], ident)
                last.then_inc(max_turned, 1)

            def scores(u, j):
                b, c = u // NC, u % NC
                if j == 0:
                    pe.wait_ge(max_added, u + 1)
                for piece, (bank, tiles, _, _) in enumerate(PIECES):
                    n = (u * HPC + j) * len(PIECES) + piece
                    if n >= len(PIECES):
                        pe.wait_ge(exp_ready, n - len(PIECES) + 1)
                    for kt in tiles:
                        _, col, _ = PLACE[kt]
                        w = S - kt * P
                        nc.tensor.matmul(ps[:, bank, col:col + w], core.k_head[:, (u % 2) * HPC + j, kt * P:(kt + 1) * P],
                                         core.q_stack[:, c, b * S + kt * P:(b + 1) * S], start=True, stop=False)
                        last = nc.tensor.matmul(ps[:, bank, col:col + P], ident_b, mask_cols, start=False, stop=True)
                    last.then_inc(scores_ready, 1)

            def values(u):
                b, c = u // NC, u % NC
                pe.wait_ge(exp_ready, (u + 1) * HPC * len(PIECES))
                if u >= 1:
                    pe.wait_ge(rsum_ready, u)
                for kt in range(NTB):
                    _, _, at = PLACE[kt]
                    w = S - kt * P
                    for j in range(HPC):
                        rows = slice(HROWS * j, HROWS * (j + 1))
                        last = nc.tensor.matmul(ps[rows, 7, kt * P:S], core.v_ones[:, b * NTB + kt, HPC * c + j, :],
                                                core.head_probs[:, (u % 2) * HPC + j, at:at + w],
                                                start=(kt == 0), stop=(kt == NTB - 1), tile_position=(0, HROWS * j))
                last.then_inc(attended_raw, 1)

            def sums(u):
                pe.wait_ge(raw_out, u + 1)
                nc.tensor.matmul(ps[:, 7, :], core.consts["pick_sum"], core.attended[:, u // NC, u % NC, :],
                                 start=True, stop=True).then_inc(sums_ready, 1)

            for u in range(UNITS + 1):
                for j in range(HPC):
                    if u >= 1:
                        scores(u - 1, j)
                    if u >= 2 and j == 0:
                        sums(u - 2)
                    if u < UNITS:
                        maxima(u, 2 * j)
                        maxima(u, 2 * j + 1)
                if u < UNITS:
                    turn_maxima(u)
                if u >= 1:
                    values(u - 1)
            sums(UNITS - 1)

        def evacuate_raw(act, u):
            act.wait_ge(attended_raw, u + 1)
            nc.scalar.activation(core.attended[:, u // NC, u % NC, :], ps[:, 7, :], ACT.Copy).then_inc(raw_out, 1)

        @block.scalar
        def _(act):
            for u in range(UNITS):
                for j in range(HPC):
                    if u >= 2 and j == 0:
                        act.wait_ge(attended_raw, u - 1)
                    for piece, (bank, _, at, w) in enumerate(PIECES):
                        act.wait_ge(scores_ready, (u * HPC + j) * len(PIECES) + piece + 1)
                        nc.scalar.activation(core.head_probs[:, (u % 2) * HPC + j, at:at + w], ps[:, bank, 0:w], ACT.Exp,
                                             scale=float(HD) ** -0.5).then_inc(exp_ready, 1)
                    if j == 0 and u >= 1:
                        evacuate_raw(act, u - 1)
            evacuate_raw(act, UNITS - 1)

        @block.vector
        def _(dve):
            def mask_keys(u):
                b, c = u // NC, u % NC
                for j in range(HPC):
                    if u >= 2 and j == 0:
                        dve.wait_ge(scores_ready, (u - 1) * HPC * len(PIECES))
                    nc.vector.tensor_scalar(core.k_head[:, (u % 2) * HPC + j, :], core.k_stack[:, c, b * S:(b + 1) * S],
                                            core.consts["stack_rows"][:, j:j + 1], None, ALU.mult).then_inc(keys_masked, 1)

            def normalise(u):
                attended = core.attended[:, u // NC, u % NC, :]
                dve.wait_ge(sums_ready, u + 1)
                nc.vector.reciprocal(core.rsum[:, u % 2, :], ps[:, 7, :]).then_inc(rsum_ready, 1)
                dve.wait_ge(rsum_ready, u + 1)
                nc.vector.tensor_tensor(attended, attended, core.rsum[:, u % 2, :], ALU.mult).then_inc(attended_ready, 1)

            mask_keys(0)
            for u in range(UNITS):
                b, c = u // NC, u % NC
                for g in range(GROUPS):
                    pair, i = g // NTB, g % NTB
                    n = u * GROUPS + g
                    dve.wait_ge(rows_ready, n + 1)
                    if g == 0 and u >= 2:
                        dve.wait_ge(max_turned, u - 1)
                    first = ONE_ROW + 2 * pair * HROWS
                    nc.vector.tensor_reduce(core.minus_max[:, u % 2, i, first:first + HROWS + 1:HROWS],
                                            ps[:, 2 * (n % 2):2 * (n % 2) + 2, 0:(i + 1) * P], AX.X, ALU.max,
                                            negate=True).then_inc(max_ready, 1)
                    if g == 3 and u >= 2:
                        normalise(u - 2)
                if u + 1 < UNITS:
                    mask_keys(u + 1)
                dve.wait_ge(max_turned, u + 1)
                q = core.q_stack[:, c, b * S:(b + 1) * S]
                nc.vector.tensor_tensor(q, q, ps[:, 0, :], ALU.add).then_inc(max_added, 1)
            normalise(UNITS - 2)
            normalise(UNITS - 1)


def attention_output(core, wo, resid, rows=None, bv=None, wo_t=None):
    nc, ps = core.nc, core.ps
    with core.stage() as (block, (output_ready, bias_ready, rows_in, rows_added, added, *_)):
        @block.tensor
        def _(pe):
            if bv is not None:
                nc.tensor.matmul(ps[:, 2, 0:P], bv.to_broadcast([P, P]), wo_t, start=True, stop=True).then_inc(bias_ready, 1)
            for n in range(NT):
                b, i = n // NTB, n % NTB
                for c in range(NC):
                    last = nc.tensor.matmul(ps[:, b, i * P:(i + 1) * P], core.attended[:, b, c, i * P:(i + 1) * P], wo[:, c, :],
                                            start=(c == 0), stop=(c == NC - 1))
                if i == NTB - 1:
                    last.then_inc(output_ready, 1)

        @block.vector
        def _(dve):
            if bv is not None:
                dve.wait_ge(bias_ready, 1)
                nc.vector.tensor_tensor(core.junk[:, 0, :], ps[:, 2, 0:P], rows, ALU.add).then_inc(rows_in, 1)
                dve.wait_ge(rows_in, 1)
                nc.vector.tensor_tensor(resid, resid, core.junk[:, 0, :].unsqueeze(1).to_broadcast([P, NT, P]),
                                        ALU.add).then_inc(rows_added, 1)
                dve.wait_ge(rows_added, 1)
            for b in range(B):
                dve.wait_ge(output_ready, b + 1)
                half = resid[:, b * NTB:(b + 1) * NTB, :]
                source = ps[:, b, :].rearrange("p (n d) -> p n d", d=P)
                if bv is not None:
                    nc.vector.tensor_tensor(half, half, source, ALU.add).then_inc(added, 1)
                else:
                    nc.vector.tensor_copy(half, source).then_inc(added, 1)


def feed_forward(core, x_t, n_experts, n_chunks, gate, up, down, acc, comb=None, b1=None, b2=None, add=False,
                 extra=None):
    nc, ps = core.nc, core.ps
    halves = [(e, b) for e in range(n_experts) for b in range(B)]
    with core.stage() as (block, (gate_ready, act_ready, hidden_ready, hidden_ready_b, output_ready, accumulated,
                                  bias_ready, bias_in, landed, *_)):
        if extra is not None:
            @block.sync
            def _(sp):
                extra(sp, landed)

        per_half = n_chunks

        @block.tensor
        def _(pe):
            if b2 is not None:
                for n in range(NT):
                    last = nc.tensor.matmul(ps[:, 6 + n // NTB, (n % NTB) * P:(n % NTB + 1) * P],
                                            core.comb_t[0:E8, n * P:(n + 1) * P], b2[0:E8, :], start=True, stop=True)
                last.then_inc(bias_ready, 1)

            def hidden(h):
                e, b = halves[h]
                for c in range(n_chunks):
                    n = h * per_half + c
                    half = x_t[:, b * S:(b + 1) * S]
                    if up is not None:
                        if n >= 2:
                            pe.wait_ge(hidden_ready, n - 1)
                        nc.tensor.matmul(ps[:, 2 * (n % 2), :], gate[:, e * n_chunks + c, :], half, start=True, stop=True)
                        nc.tensor.matmul(ps[:, 2 * (n % 2) + 1, :], up[:, e * n_chunks + c, :], half,
                                         start=True, stop=True).then_inc(gate_ready, 1)
                    else:
                        if n >= 4:
                            pe.wait_ge(hidden_ready if n % 2 == 0 else hidden_ready_b, (n - 4) // 2 + 1)
                        nc.tensor.matmul(ps[:, n % 4, :], gate[:, e * n_chunks + c, :], half,
                                         start=True, stop=True).then_inc(gate_ready, 1)

            def output(h):
                e, b = halves[h]
                done = (h + 1) * per_half
                if up is not None:
                    pe.wait_ge(hidden_ready, done)
                else:
                    pe.wait_ge(hidden_ready, (done + 1) // 2)
                    pe.wait_ge(hidden_ready_b, done // 2)
                if h >= 2:
                    pe.wait_ge(accumulated, h - 1)
                for i in range(NTB):
                    for c in range(n_chunks):
                        last = nc.tensor.matmul(ps[:, 4 + h % 2, i * P:(i + 1) * P], core.hidden[:, h % 2, c, i * P:(i + 1) * P],
                                                down[:, e * n_chunks + c, :], start=(c == 0), stop=(c == n_chunks - 1))
                last.then_inc(output_ready, 1)

            for h in range(len(halves) + 1):
                if h < len(halves):
                    hidden(h)
                if h >= 1:
                    output(h - 1)

        def slot(n):
            h, c = n // per_half, n % per_half
            return core.hidden[:, h % 2, c, :]

        @block.scalar
        def _(act):
            for n in range(len(halves) * per_half):
                if up is not None:
                    act.wait_ge(gate_ready, n + 1)
                    if n >= 2:
                        act.wait_ge(hidden_ready, n - 1)
                    nc.scalar.activation(core.gated[:, n % 2, :], ps[:, 2 * (n % 2), :], ACT.Silu).then_inc(act_ready, 1)
                elif n % 2 == 0:
                    h, c = n // per_half, n % per_half
                    e = halves[h][0]
                    act.wait_ge(gate_ready, n + 1)
                    if h >= 2:
                        act.wait_ge(output_ready, h - 1)
                    nc.scalar.activation(slot(n), ps[:, n % 4, :], ACT.Relu,
                                         bias=b1[:, e * n_chunks + c:e * n_chunks + c + 1]).then_inc(hidden_ready, 1)

        @block.vector
        def _(dve):
            if b2 is not None:
                dve.wait_ge(bias_ready, 1)
                bias_rows = ps[:, 6:8, :].rearrange("p b (n d) -> p (b n) d", d=P)
                if add:
                    nc.vector.tensor_tensor(acc, acc, bias_rows, ALU.add).then_inc(bias_in, 1)
                else:
                    nc.vector.tensor_copy(acc, bias_rows).then_inc(bias_in, 1)
                dve.wait_ge(bias_in, 1)

            def hidden(h):
                e = halves[h][0]
                for c in range(n_chunks):
                    n = h * per_half + c
                    if up is not None:
                        dve.wait_ge(act_ready, n + 1)
                        if h >= 2 and c == 0:
                            dve.wait_ge(output_ready, h - 1)
                        nc.vector.tensor_tensor(slot(n), core.gated[:, n % 2, :], ps[:, 2 * (n % 2) + 1, :],
                                                ALU.mult).then_inc(hidden_ready, 1)
                    elif n % 2 == 1:
                        dve.wait_ge(gate_ready, n + 1)
                        if h >= 2:
                            dve.wait_ge(output_ready, h - 1)
                        nc.vector.tensor_scalar(slot(n), ps[:, n % 4, :], b1[:, e * n_chunks + c:e * n_chunks + c + 1], 0.0,
                                                ALU.add, ALU.max).then_inc(hidden_ready_b, 1)

            def accumulate(h):
                e, b = halves[h]
                dve.wait_ge(output_ready, h + 1)
                if h >= 2:
                    dve.wait_ge(accumulated, h - 1)
                bank = ps[:, 4 + h % 2, :].rearrange("p (n d) -> p n d", d=P)
                rows = acc[:, b * NTB:(b + 1) * NTB, :]
                if comb is None:
                    if add:
                        last = nc.vector.tensor_tensor(rows, rows, bank, ALU.add)
                    else:
                        last = nc.vector.tensor_copy(rows, bank)
                else:
                    for i in range(NTB):
                        weight = comb[:, b * NTB + i, e:e + 1]
                        if e == 0 and not add and b2 is None:
                            last = nc.vector.tensor_scalar(rows[:, i, :], bank[:, i, :], weight, None, ALU.mult)
                        else:
                            last = nc.vector.scalar_tensor_tensor(rows[:, i, :], bank[:, i, :], weight, rows[:, i, :],
                                                                  ALU.mult, ALU.add)
                last.then_inc(accumulated, 1)

            for h in range(len(halves) + 1):
                if h < len(halves):
                    hidden(h)
                if h >= 1:
                    accumulate(h - 1)


def choose_two(core, link, key, chosen):
    nc = core.nc
    greater, equal, rank = core.compare[:, 0], core.compare[:, 1], core.rank
    mine, other = key.unsqueeze(3).to_broadcast([P, NT, E8, E8]), key.unsqueeze(2).to_broadcast([P, NT, E8, E8])
    lower = core.consts["lower"].rearrange("p (e j) -> p e j", j=E8)
    link(nc.vector.tensor_tensor(greater, other, mine, ALU.is_gt))
    link(nc.vector.tensor_tensor(equal, other, mine, ALU.is_equal))
    link(nc.vector.tensor_tensor(equal, equal, lower.unsqueeze(1).to_broadcast([P, NT, E8, E8]), ALU.mult))
    link(nc.vector.tensor_tensor(greater, greater, equal, ALU.add))
    link(nc.vector.tensor_reduce(rank, greater, AX.X, ALU.add))
    link(nc.vector.tensor_scalar(chosen, rank, 1.5, None, ALU.is_lt))


def by_expert(ap):
    return ap.unsqueeze(2).to_broadcast([P, NT, E8])


def route(core, x_t, gate, bias=None, among_chosen=False):
    nc, ps = core.nc, core.ps
    with core.stage() as (block, (logits_ready, shifted_ready, exp_ready, link_signal, *_)):
        @block.tensor
        def _(pe):
            for n in range(NT):
                last = nc.tensor.matmul(ps[:, 0, n * E8:(n + 1) * E8], x_t[:, n * P:(n + 1) * P], gate, start=True, stop=True)
            last.then_inc(logits_ready, 1)

        @block.scalar
        def _(act):
            act.wait_ge(shifted_ready, 1)
            nc.scalar.activation(core.exps, core.exps, ACT.Exp).then_inc(exp_ready, 1)

        @block.vector
        def _(dve):
            link = chained(dve, link_signal)
            logits, exps, chosen = core.logits, core.exps, core.chosen
            dve.wait_ge(logits_ready, 1)
            source = ps[:, 0, 0:NT * E8].rearrange("p (n e) -> p n e", e=E8)
            if bias is None:
                link(nc.vector.tensor_copy(logits, source))
            else:
                link(nc.vector.tensor_tensor(logits, source, bias.unsqueeze(1).to_broadcast([P, NT, E8]), ALU.add))
            link(nc.vector.tensor_reduce(core.per_token, logits, AX.X, ALU.max))
            nc.vector.tensor_tensor(exps, logits, by_expert(core.per_token), ALU.subtract).then_inc(shifted_ready, 1)
            if among_chosen:
                choose_two(core, link, logits, chosen)
                dve.wait_ge(exp_ready, 1)
                link(nc.vector.tensor_tensor(exps, exps, chosen, ALU.mult))
            else:
                dve.wait_ge(exp_ready, 1)
            link(nc.vector.tensor_reduce(core.per_token, exps, AX.X, ALU.add))
            link(nc.vector.reciprocal(core.per_token, core.per_token))
            if among_chosen:
                link(nc.vector.tensor_tensor(core.comb, exps, by_expert(core.per_token), ALU.mult))
            else:
                link(nc.vector.tensor_tensor(exps, exps, by_expert(core.per_token), ALU.mult))
                choose_two(core, link, exps, chosen)
                link(nc.vector.tensor_tensor(core.comb, exps, chosen, ALU.mult))


def turn_experts(core, pairs):
    nc, ps, ident = core.nc, core.ps, core.consts["ident"]
    with core.stage() as (block, (turned, evacuated, *_)):
        @block.tensor
        def _(pe):
            for i, (source, _) in enumerate(pairs):
                for n in range(NT):
                    last = nc.tensor.transpose(ps[0:E8, 2 * i + n // NTB, (n % NTB) * P:(n % NTB + 1) * P], source[:, n, :], ident)
                last.then_inc(turned, 1)

        @block.vector
        def _(dve):
            for i, (_, target) in enumerate(pairs):
                dve.wait_ge(turned, i + 1)
                nc.vector.tensor_copy(target[0:E8, :].rearrange("p (b s) -> p b s", b=B),
                                      ps[0:E8, 2 * i:2 * i + 2, :]).then_inc(evacuated, 1)


def route_over_tokens(core, x_t, gate, gate_b):
    nc, ps, ident = core.nc, core.ps, core.consts["ident"]
    probs_t = core.comb_t[0:E8, :].rearrange("p (b s) -> p b s", b=B)
    per_batch = core.per_batch[0:E8, :]
    with core.stage() as (block, (logits_ready, shifted_ready, exp_ready, probs_ready, turned, link_signal, *_)):
        @block.tensor
        def _(pe):
            for b in range(B):
                last = nc.tensor.matmul(ps[0:E8, b, :], gate, x_t[:, b * S:(b + 1) * S], start=True, stop=True)
            last.then_inc(logits_ready, 1)
            pe.wait_ge(probs_ready, 1)
            for n in range(NT):
                last = nc.tensor.transpose(ps[:, 2, n * E8:(n + 1) * E8], core.comb_t[0:E8, n * P:(n + 1) * P], ident[0:E8, 0:E8])
            last.then_inc(turned, 1)

        @block.scalar
        def _(act):
            act.wait_ge(shifted_ready, 1)
            nc.scalar.activation(probs_t, probs_t, ACT.Exp).then_inc(exp_ready, 1)

        @block.vector
        def _(dve):
            link = chained(dve, link_signal)
            dve.wait_ge(logits_ready, 1)
            link(nc.vector.tensor_scalar(probs_t, ps[0:E8, 0:2, :], gate_b, None, ALU.add))
            link(nc.vector.tensor_reduce(per_batch, probs_t, AX.X, ALU.max))
            nc.vector.tensor_tensor(probs_t, probs_t, per_batch.unsqueeze(2).to_broadcast([E8, B, S]),
                                    ALU.subtract).then_inc(shifted_ready, 1)
            dve.wait_ge(exp_ready, 1)
            link(nc.vector.tensor_reduce(per_batch, probs_t, AX.X, ALU.add))
            link(nc.vector.reciprocal(per_batch, per_batch))
            nc.vector.tensor_tensor(probs_t, probs_t, per_batch.unsqueeze(2).to_broadcast([E8, B, S]),
                                    ALU.mult).then_inc(probs_ready, 1)
            dve.wait_ge(turned, 1)
            link(nc.vector.tensor_copy(core.exps, ps[:, 2, 0:NT * E8].rearrange("p (n e) -> p n e", e=E8)))
            choose_two(core, link, core.exps, core.chosen)
            link(nc.vector.tensor_tensor(core.comb, core.exps, core.chosen, ALU.mult))
    turn_experts(core, [(core.comb, core.comb_t), (core.chosen, core.chosen_t)])


def pooled_experts(core, x_t, w, resid, extra=None):
    nc, ps, ident = core.nc, core.ps, core.consts["ident"]
    jobs = [(e, b) for e in range(E8) for b in range(B)]
    w1, w2, w3 = w.tiled("w1"), w.tiled("w2"), w.tiled("w3")
    first, second, third = core.hidden[:, :, 0, :], core.hidden[:, :, 1, :], core.hidden[:, :, 2, :]
    with core.stage() as (block, (first_raw, first_ready, second_raw, second_ready, third_raw, third_ready,
                                  pooled, landed, *_)):
        if extra is not None:
            @block.sync
            def _(sp):
                extra(sp, landed)

        @block.tensor
        def _(pe):
            for s in range(len(jobs) + 2):
                if s < len(jobs):
                    e, b = jobs[s]
                    if s >= 2:
                        pe.wait_ge(first_ready, s - 1)
                    nc.tensor.matmul(ps[:, s % 2, :], w1[:, e, :], x_t[:, b * S:(b + 1) * S], start=True,
                                     stop=True).then_inc(first_raw, 1)
                j = s - 1
                if 0 <= j < len(jobs):
                    pe.wait_ge(first_ready, j + 1)
                    if j >= 2:
                        pe.wait_ge(second_ready, j - 1)
                    nc.tensor.matmul(ps[:, 2 + j % 2, :], w2[:, jobs[j][0], :], first[:, j % 2, :], start=True,
                                     stop=True).then_inc(second_raw, 1)
                j = s - 2
                if 0 <= j < len(jobs):
                    e, b = jobs[j]
                    pe.wait_ge(second_ready, j + 1)
                    if j >= 2:
                        pe.wait_ge(third_ready, j - 1)
                        pe.wait_ge(pooled, j - 1)
                    nc.tensor.matmul(ps[:, 6 + j % 2, :], ident[:, e:e + 1].to_broadcast([P, P]),
                                     core.comb_t[:, b * S:(b + 1) * S], start=True, stop=True)
                    nc.tensor.matmul(ps[:, 4 + j % 2, :], w3[:, e, :], second[:, j % 2, :], start=True,
                                     stop=True).then_inc(third_raw, 1)

        @block.scalar
        def _(act):
            for s in range(len(jobs) + 2):
                if s < len(jobs):
                    act.wait_ge(first_raw, s + 1)
                    if s >= 2:
                        act.wait_ge(second_raw, s - 1)
                    nc.scalar.activation(first[:, s % 2, :], ps[:, s % 2, :], ACT.Relu,
                                         bias=w["b1"][:, jobs[s][0]:jobs[s][0] + 1]).then_inc(first_ready, 1)
                j = s - 2
                if 0 <= j < len(jobs):
                    act.wait_ge(third_raw, j + 1)
                    if j >= 2:
                        act.wait_ge(pooled, j - 1)
                    nc.scalar.activation(third[:, j % 2, :], ps[:, 4 + j % 2, :], ACT.Relu,
                                         bias=w["b3"][:, jobs[j][0]:jobs[j][0] + 1]).then_inc(third_ready, 1)

        def pool(dve, j):
            e, b = jobs[j]
            dve.wait_ge(third_ready, j + 1)
            nc.vector.scalar_tensor_tensor(third[:, j % 2, :], third[:, j % 2, :], 1.0, ps[:, 6 + j % 2, :], ALU.mult,
                                           ALU.mult, accum_out=core.pool_sums[:, e, b:b + 1]).then_inc(pooled, 1)

        @block.vector
        def _(dve):
            for s in range(1, len(jobs) + 3):
                j = s - 1
                if j < len(jobs):
                    e = jobs[j][0]
                    dve.wait_ge(second_raw, j + 1)
                    if j >= 2:
                        dve.wait_ge(third_raw, j - 1)
                    nc.vector.tensor_scalar(second[:, j % 2, :], ps[:, 2 + j % 2, :], w["b2"][:, e:e + 1], 0.0,
                                            ALU.add, ALU.max).then_inc(second_ready, 1)
                j = s - 3
                if 0 <= j < len(jobs):
                    pool(dve, j)

    with core.stage() as (block, (summed, turned, rows_ready, output_ready, added, *_)):
        @block.tensor
        def _(pe):
            pe.wait_ge(summed, 1)
            nc.tensor.transpose(ps[0:E8, 0, 0:P], core.pool_total[:, :], ident).then_inc(turned, 1)
            pe.wait_ge(rows_ready, 1)
            for n in range(NT):
                last = nc.tensor.matmul(ps[:, 1 + n // NTB, (n % NTB) * P:(n % NTB + 1) * P],
                                        core.chosen_t[0:E8, n * P:(n + 1) * P], core.pool_rows[0:E8, :],
                                        start=True, stop=True)
            last.then_inc(output_ready, 1)

        @block.vector
        def _(dve):
            nc.vector.tensor_tensor(core.pool_total[:, :], core.pool_sums[:, :, 0], core.pool_sums[:, :, 1],
                                    ALU.add).then_inc(summed, 1)
            dve.wait_ge(turned, 1)
            nc.vector.tensor_copy(core.pool_rows[0:E8, :], ps[0:E8, 0, 0:P]).then_inc(rows_ready, 1)
            dve.wait_ge(output_ready, 1)
            nc.vector.tensor_tensor(resid, resid, ps[:, 1:3, :].rearrange("p b (n d) -> p (b n) d", d=P),
                                    ALU.add).then_inc(added, 1)


def norm_context(core, scale, bias, target):
    nc, ps, ident = core.nc, core.ps, core.consts["ident"]
    rows = B * CK
    x, xn = core.ctx_rows[0:rows, :], core.ctx_norm[0:rows, :]
    mean_var, rstd, log_var = core.mean_var[0:rows, 0, :], core.rstd[0:rows, 0:1], core.log_var[0:rows, 0:1]
    with core.stage() as (block, (link_signal, log_ready, rstd_ready, tile_ready, turned, turned_out, *_)):
        @block.vector
        def _(dve):
            link = chained(dve, link_signal)
            link(nc.vector.bn_stats(core.stats[0:rows, 0, :], x))
            link(nc.vector.bn_aggr(mean_var, core.stats[0:rows, 0, :]))
            dve.wait_ge(rstd_ready, 1)
            nc.vector.tensor_scalar(xn, x, mean_var[:, 0:1], rstd, ALU.subtract, ALU.mult).then_inc(tile_ready, 1)
            dve.wait_ge(turned, 1)
            nc.vector.tensor_scalar(target, ps[:, 0, 0:rows], scale, bias, ALU.mult, ALU.add).then_inc(turned_out, 1)

        @block.scalar
        def _(act):
            act.wait_ge(link_signal, 2)
            nc.scalar.activation(log_var, mean_var[:, 1:2], ACT.Ln, bias=core.eps_col(1e-5)[0:rows, :]).then_inc(log_ready, 1)
            act.wait_ge(log_ready, 1)
            nc.scalar.activation(rstd, log_var, ACT.Exp, scale=-0.5).then_inc(rstd_ready, 1)

        @block.tensor
        def _(pe):
            pe.wait_ge(tile_ready, 1)
            nc.tensor.transpose(ps[:, 0, 0:rows], xn, ident[0:rows, 0:rows]).then_inc(turned, 1)


KT3 = NTB + 1


def latent_attention(core, x_t, media_t, w, extra=None):
    nc, ps, ident = core.nc, core.ps, core.consts["ident"]
    wq, wk, wv = w.tiled("wq"), w.tiled("wk"), w.tiled("wv")
    units = [(b, h) for b in range(B) for h in range(H3)]
    SCALE = float(P) ** -0.5
    ROW_BANKS = (0, 1, 3, 0)
    with core.stage() as (block, (qkv_raw, q_out, k_out, v_out, q_round, k_round, rows_ready, max_ready, max_joined,
                                  max_turned, max_out, scores_ready, exp_ready, attended_raw, rsum_ready,
                                  attended_norm, attended_turned, attended_ready, zeroed, max_ctx, landed, *_)):
        if extra is not None:
            @block.sync
            def _(sp):
                extra(sp, landed)

        @block.tensor
        def _(pe):
            def front(u):
                b, h = units[u]
                half, media = x_t[:, b * S:(b + 1) * S], media_t[:, b * CK:(b + 1) * CK]
                if u >= 1:
                    pe.wait_ge(max_out, u)
                nc.tensor.matmul(ps[:, 0, :], wq[:, h, :], half, start=True, stop=True)
                nc.tensor.matmul(ps[:, 2, 0:CK], wk[:, h, :], media, start=True, stop=True)
                nc.tensor.matmul(ps[0:CK, 2, P:2 * P], media, wv[:, h, :], start=True, stop=True)
                nc.tensor.matmul(ps[:, 1, :], wk[:, h, :], half, start=True, stop=True).then_inc(qkv_raw, 1)
                for i in range(NTB):
                    last = nc.tensor.matmul(ps[:, 3, i * P:(i + 1) * P], x_t[:, b * S + i * P:b * S + (i + 1) * P],
                                            wv[:, h, :], start=True, stop=True)
                last.then_inc(qkv_raw, 1)

            def rows(u):
                pe.wait_ge(q_round, u + 1)
                pe.wait_ge(k_round, u + 1)
                pe.wait_ge(v_out, u + 1)
                for i in range(NTB):
                    q = core.q_round[:, i * P:(i + 1) * P]
                    nc.tensor.matmul(ps[:, 2, 2 * P + i * CK:2 * P + (i + 1) * CK], q, core.k_round[:, S:S + CK],
                                     start=True, stop=True)
                    if i == 3:
                        pe.wait_ge(max_ready, NTB * u + 1)
                    nc.tensor.matmul(ps[:, ROW_BANKS[i], :], q, core.k_round[:, 0:S], start=True, stop=True).then_inc(rows_ready, 1)
                pe.wait_ge(max_joined, u + 1)
                for i in range(NTB):
                    last = nc.tensor.transpose(ps[:, 1, i * P:(i + 1) * P], core.max3[:, i, :], ident)
                last.then_inc(max_turned, 1)

            def scores(u):
                q, k = core.q3[:, u % 2, :], core.k3[:, u % 2, :]
                pe.wait_ge(max_out, u + 1)
                for kt in range(KT3):
                    n = u * KT3 + kt
                    if n >= 2:
                        pe.wait_ge(exp_ready, n - 1)
                    m = P if kt < NTB else CK
                    out = ps[0:m, 4 + n % 2, :]
                    nc.tensor.matmul(out, k[:, kt * P:kt * P + m], q, start=True, stop=False)
                    nc.tensor.matmul(out, core.ones_b[:, 0:m], core.max_row[:, u % 2, :], start=False, stop=True)\
                        .then_inc(scores_ready, 1)

            def values(u):
                pe.wait_ge(exp_ready, KT3 * (u + 1))
                if u >= 1:
                    pe.wait_ge(attended_ready, u)
                for i in range(NTB):
                    out = ps[:, 6 + i // 2, (i % 2) * (P + 1):(i % 2 + 1) * (P + 1)]
                    for kt in range(KT3):
                        last = nc.tensor.matmul(out, core.probs3[:, kt, i * P:(i + 1) * P], core.v3[:, u % 2, kt, :],
                                                start=(kt == 0), stop=(kt == KT3 - 1))
                last.then_inc(attended_raw, 1)

            def turn(u):
                pe.wait_ge(attended_norm, u + 1)
                for i in range(NTB):
                    last = nc.tensor.transpose(ps[:, 6, i * P:(i + 1) * P], core.attended_rows[:, i, :], ident)
                last.then_inc(attended_turned, 1)

            pe.wait_ge(zeroed, 1)
            front(0)
            rows(0)
            for u in range(len(units)):
                scores(u)
                if u + 1 < len(units):
                    front(u + 1)
                values(u)
                if u + 1 < len(units):
                    rows(u + 1)
                turn(u)

        @block.scalar
        def _(act):
            def front(u):
                b, h = units[u]
                act.wait_ge(qkv_raw, 2 * u + 1)
                bias = w["bk"][:, h:h + 1]
                nc.scalar.activation(core.k3[:, u % 2, 0:S], ps[:, 1, :], ACT.Identity, bias=bias)
                nc.scalar.activation(core.v3[0:CK, u % 2, NTB, 0:P], ps[0:CK, 2, P:2 * P], ACT.Copy)
                nc.scalar.activation(core.k3[:, u % 2, S:S + CK], ps[:, 2, 0:CK], ACT.Identity, bias=bias).then_inc(k_out, 1)
                act.wait_ge(k_out, u + 1)
                nc.scalar.activation(core.k_round[:, :], core.k3[:, u % 2, :], ACT.Copy).then_inc(k_round, 1)
                act.wait_ge(q_out, u + 1)
                nc.scalar.activation(core.q_round[:, :], core.q3[:, u % 2, :], ACT.Copy).then_inc(q_round, 1)

            def finish(u):
                b, h = units[u]
                act.wait_ge(attended_turned, u + 1)
                nc.scalar.activation(core.attended3[:, b, h, :], ps[:, 6, :], ACT.Identity,
                                     bias=w["bv"][:, h:h + 1]).then_inc(attended_ready, 1)

            front(0)
            for u in range(len(units)):
                for kt in range(KT3):
                    m = P if kt < NTB else CK
                    act.wait_ge(scores_ready, u * KT3 + kt + 1)
                    nc.scalar.activation(core.probs3[0:m, kt, :], ps[0:m, 4 + (u * KT3 + kt) % 2, :], ACT.Exp).then_inc(exp_ready, 1)
                if u + 1 < len(units):
                    front(u + 1)
                finish(u)

        @block.vector
        def _(dve):
            nc.vector.memset(core.probs3[:, NTB, :], 0.0)
            nc.vector.memset(core.max3[:, :, :], 0.0)
            nc.vector.memset(core.v3[:, :, :, :], 0.0).then_inc(zeroed, 1)
            dve.wait_ge(zeroed, 1)
            nc.vector.memset(core.v3[:, :, 0:NTB, P:P + 1], 1.0)
            nc.vector.memset(core.v3[0:CK, :, NTB, P:P + 1], 1.0)

            def front(u):
                b, h = units[u]
                dve.wait_ge(qkv_raw, 2 * u + 1)
                nc.vector.tensor_scalar(core.q3[:, u % 2, :], ps[:, 0, :], w["bq"][:, h:h + 1], SCALE, ALU.add,
                                        ALU.mult).then_inc(q_out, 1)
                dve.wait_ge(qkv_raw, 2 * u + 2)
                nc.vector.tensor_copy(core.v3[:, u % 2, 0:NTB, 0:P], ps[:, 3, :].rearrange("p (n d) -> p n d", d=P))\
                    .then_inc(v_out, 1)

            def maxima(u):
                for i in range(NTB):
                    dve.wait_ge(rows_ready, NTB * u + i + 1)
                    nc.vector.tensor_reduce(core.max_parts[:, 0, i:i + 1], ps[:, ROW_BANKS[i], :], AX.X, ALU.max,
                                            negate=True).then_inc(max_ready, 1)
                nc.vector.tensor_reduce(core.max_parts[:, 1, :],
                                        ps[:, 2, 2 * P:2 * P + NTB * CK].rearrange("p (i k) -> p i k", k=CK), AX.X, ALU.max,
                                        negate=True).then_inc(max_ctx, 1)
                dve.wait_ge(max_ctx, u + 1)
                if u >= 1:
                    dve.wait_ge(max_turned, u)
                nc.vector.tensor_tensor(core.max3[:, :, 0], core.max_parts[:, 0, :], core.max_parts[:, 1, :],
                                        ALU.min).then_inc(max_joined, 1)
                dve.wait_ge(max_turned, u + 1)
                nc.vector.tensor_copy(core.max_row[:, u % 2, :], ps[:, 1, :]).then_inc(max_out, 1)

            def normalise(u):
                dve.wait_ge(attended_raw, u + 1)
                raw = ps[:, 6:8, 0:2 * (P + 1)].rearrange("p b (i d) -> p b i d", d=P + 1)
                nc.vector.reciprocal(core.rsum3[:, :, :], raw[:, :, :, P]).then_inc(rsum_ready, 1)
                dve.wait_ge(rsum_ready, u + 1)
                for i in range(NTB):
                    last = nc.vector.tensor_scalar(core.attended_rows[:, i, :], raw[:, i // 2, i % 2, 0:P],
                                                   core.rsum3[:, i // 2, i % 2:i % 2 + 1], None, ALU.mult)
                last.then_inc(attended_norm, 1)

            front(0)
            maxima(0)
            for u in range(len(units)):
                if u + 1 < len(units):
                    front(u + 1)
                normalise(u)
                if u + 1 < len(units):
                    maxima(u + 1)

    wo = w.tiled("wo")
    with core.stage() as (block, (output_ready, rows_added, added, *_)):
        @block.tensor
        def _(pe):
            for n in range(NT):
                b, i = n // NTB, n % NTB
                for h in range(H3):
                    last = nc.tensor.matmul(ps[:, b, i * P:(i + 1) * P], core.attended3[:, b, h, i * P:(i + 1) * P], wo[:, h, :],
                                            start=(h == 0), stop=(h == H3 - 1))
                if i == NTB - 1:
                    last.then_inc(output_ready, 1)

        @block.vector
        def _(dve):
            nc.vector.tensor_tensor(core.x, core.x, w["bo"].unsqueeze(1).to_broadcast([P, NT, P]), ALU.add).then_inc(rows_added, 1)
            dve.wait_ge(rows_added, 1)
            for b in range(B):
                dve.wait_ge(output_ready, b + 1)
                half = core.x[:, b * NTB:(b + 1) * NTB, :]
                nc.vector.tensor_tensor(half, half, ps[:, b, :].rearrange("p (n d) -> p n d", d=P), ALU.add).then_inc(added, 1)


def carve(region, start, shape, dt=F32):
    n = 1
    for s in shape:
        n *= s
    columns = n if dt == F32 else n // 2
    view = region[:, start:start + columns]
    if dt != F32:
        view = view.bitcast(dt)
    names = "abcd"[:len(shape)]
    if len(shape) > 1:
        view = view.rearrange(f"p ({' '.join(names)}) -> p {' '.join(names)}", **dict(zip(names, shape)))
    return view, start + columns


def allot(core):
    tokens, experts = [P, NT, P], [P, NT, E8]
    core.ps = core.ctx.enter_context(core.nc.psum_tensor("ps", [P, 8, S], F32))
    core.x = core.sbuf("x", tokens)[:, :, :]
    core.xn = core.sbuf("xn", tokens)[:, :, :]
    core.z = core.sbuf("z", tokens)[:, :, :]
    core.acc = core.sbuf("acc", tokens)[:, :, :]
    core.junk = core.sbuf("junk", tokens)[:, :, :]
    core.x_t = core.sbuf("x_t", [P, T])[:, :]
    core.comb_t = core.sbuf("comb_t", [P, T])[:, :]
    core.chosen_t = core.sbuf("chosen_t", [P, T])[:, :]
    core.weights_1 = core.sbuf("weights_1", [P, max(width("l0x"), width("l2a") + width("l2b"), width("l3x"))])
    core.weights_2 = core.sbuf("weights_2", [P, width("l1f") + width("l2f")])
    core.consts = Fields(core.sbuf("consts", [P, width("consts")]), "consts")
    core.masks = core.sbuf("masks", [P, 3, P], BF16)[:, :, :]
    core.ones_b = core.sbuf("ones_b", [P, P], BF16)[:, :]
    core.pick = core.sbuf("pick", [P, 4, NC, P], F16)[:, :, :, :]
    core.key_mask = core.sbuf("key_mask", [P, NT, CK])[:, :, :]
    core.key_low = core.sbuf("key_low", [P, NT, CK])[:, :, :]
    core.tokens_i = core.sbuf("tokens_i", [P, NT], I32)[:, :]
    core.tokens_f = core.sbuf("tokens_f", [P, 2, NT])[:, :, :]
    core.stats = core.sbuf("stats", [P, NT, 6])[:, :, :]
    core.mean_var = core.sbuf("mean_var", [P, NT, 2])[:, :, :]
    core.log_var = core.sbuf("log_var", [P, NT])[:, :]
    core.rstd = core.sbuf("rstd", [P, NT])[:, :]
    core.eps = core.sbuf("eps", [P, 2])
    core.logits = core.sbuf("logits", experts)[:, :, :]
    core.exps = core.sbuf("exps", experts)[:, :, :]
    core.chosen = core.sbuf("chosen", experts)[:, :, :]
    core.comb = core.sbuf("comb", experts)[:, :, :]
    core.rank = core.sbuf("rank", experts)[:, :, :]
    core.per_token = core.sbuf("per_token", [P, NT])[:, :]
    core.per_batch = core.sbuf("per_batch", [P, B])[:, :]
    core.row_max = core.sbuf("row_max", [P, H])[:, :]
    core.row_sum = core.sbuf("row_sum", [P, H])[:, :]
    core.row_rsum = core.sbuf("row_rsum", [P, H])[:, :]
    core.pool_sums = core.sbuf("pool_sums", [P, E8, B])[:, :, :]
    core.pool_total = core.sbuf("pool_total", [P, E8])[:, :]
    core.pool_rows = core.sbuf("pool_rows", [P, P])[:, :]
    core.ctx_rows = core.sbuf("ctx_rows", [P, P])[:, :]
    core.ctx_norm = core.sbuf("ctx_norm", [P, P])[:, :]
    core.ctx_t = core.sbuf("ctx_t", [P, B * CK])[:, :]
    core.media_t = core.sbuf("media_t", [P, B * CK])[:, :]
    stacks = core.sbuf("stacks", [P, B * H3 * S])
    core.q_stack, at = carve(stacks, 0, [NC, T], F16)
    core.k_stack, at = carve(stacks, at, [NC, T], F16)
    core.v_ones, at = carve(stacks, at, [NT, H, HROWS])
    assert at <= B * H3 * S
    core.attended3, _ = carve(stacks, 0, [B, H3, S])
    core.k_head = core.sbuf("k_head", [P, 2 * HPC, S], F16)[:, :, :]
    core.minus_max = core.sbuf("minus_max", [P, 2, NTB, P])[:, :, :, :]
    hidden = core.sbuf("hidden", [P, B * NC * S + 2 * S])
    core.attended, at = carve(hidden, 0, [B, NC, S])
    core.rsum, at = carve(hidden, at, [2, S])
    core.hidden, at = carve(hidden, 0, [2, 4, S])
    core.gated, at = carve(hidden, at, [2, S])
    scratch = core.sbuf("scratch", [P, 2 * HPC * 5 * S // 2])
    core.head_probs, _ = carve(scratch, 0, [2 * HPC, 5 * S // 2])
    core.high, at = carve(scratch, 0, [2, T], F16)
    core.low, at = carve(scratch, at, [2, T], F16)
    core.rotated, at = carve(scratch, at, [2, T])
    core.turn_part, at = carve(scratch, at, [1, T])
    core.turn_part = core.turn_part[:, 0, :]
    core.compare, _ = carve(scratch, 0, [2, NT * E8 * E8])
    core.compare = core.compare.rearrange("p a (n e j) -> p a n e j", e=E8, j=E8)
    core.k_spread, at = carve(scratch, 0, [B, H * CK])
    core.v_spread, at = carve(scratch, at, [B, H * CK])
    core.a, at = carve(scratch, at, [B, H * CK])
    core.bb, at = carve(scratch, at, [B, H * CK])
    core.q_bias, at = carve(scratch, at, [B, H * CK])
    core.shifted, at = carve(scratch, at, [2, H * CK])
    core.probs, at = carve(scratch, at, [2, H * CK])
    core.probs_t, at = carve(scratch, at, [2, H * CK])
    core.q3, at = carve(scratch, 0, [2, S])
    core.k3, at = carve(scratch, at, [2, S + CK])
    core.probs3, at = carve(scratch, at, [KT3, S])
    core.v3, at = carve(scratch, at, [2, KT3, P + 1])
    core.max3, at = carve(scratch, at, [NTB, P])
    core.attended_rows, at = carve(scratch, at, [NTB, P])
    core.q_round, at = carve(scratch, at, [1, S], BF16)
    core.k_round, at = carve(scratch, at, [1, S + CK], BF16)
    core.q_round, core.k_round = core.q_round[:, 0, :], core.k_round[:, 0, :]
    core.max_row, at = carve(scratch, at, [2, S], BF16)
    core.max_parts, at = carve(scratch, at, [2, NTB])
    core.rsum3, at = carve(scratch, at, [2, 2])
    assert at <= 2 * HPC * 5 * S // 2


def first_loads(core):
    nc, ins = core.nc, core.ins
    with core.stage() as (block, (landed, tokens_landed, set_done, tokens_ready, link_signal, *_)):
        @block.sync
        def _(sp):
            sp.dma_start(core.x, ins["x"].rearrange("(n p) d -> p n d", p=P)).then_inc(landed, 16)
            sp.dma_start(core.consts.all, ins["consts"]).then_inc(landed, 16)
            sp.dma_start(core.ctx_rows[0:B * CK, :], ins["ctx"]).then_inc(landed, 16)
            sp.dma_start(core.ctx_t, ins["ctx_t"]).then_inc(landed, 16)
            sp.dma_start(core.masks, ins["masks"]).then_inc(landed, 16)
            sp.dma_start(core.pick, ins["pick"]).then_inc(landed, 16)
            sp.dma_start(core.tokens_i, ins["tokens"]).then_inc(tokens_landed, 16)
            sp.wait_ge(landed, 6 * 16)

        @block.scalar
        def _(act):
            act.dma_start(Fields(core.weights_1, "l0x").all, ins["l0x"]).then_inc(tokens_landed, 16)
            act.wait_ge(tokens_landed, 32)

        @block.gpsimd
        def _(pool):
            nc.gpsimd.memset(core.v_ones[:, :, :, :], 0.0).then_inc(set_done, 1)
            pool.wait_ge(set_done, 1)
            nc.gpsimd.memset(core.v_ones[:, :, :, HD:HD + 1], 1.0).then_inc(set_done, 1)
            pool.wait_ge(set_done, 2)

        @block.vector
        def _(dve):
            link = chained(dve, link_signal)
            nc.vector.memset(core.minus_max, 0.0)
            nc.vector.memset(core.comb_t, 0.0)
            nc.vector.memset(core.ones_b, 1.0)
            nc.vector.memset(core.eps[:, 0:1], 1e-5)
            nc.vector.memset(core.eps[:, 1:2], 1e-6)
            dve.wait_ge(tokens_landed, 32)
            dve.wait_ge(landed, 6 * 16)
            last, before = core.tokens_f[:, 0, :], core.tokens_f[:, 1, :]
            link(nc.vector.tensor_copy(last, core.tokens_i))
            link(nc.vector.tensor_scalar(before, last, -float(LOOKBACK), None, ALU.add))
            keys = core.consts["keys"].unsqueeze(1).to_broadcast([P, NT, CK])
            link(nc.vector.tensor_tensor(core.key_mask, keys, last.unsqueeze(2).to_broadcast([P, NT, CK]), ALU.is_le))
            link(nc.vector.tensor_tensor(core.key_low, keys, before.unsqueeze(2).to_broadcast([P, NT, CK]), ALU.is_gt))
            link(nc.vector.tensor_tensor(core.key_mask, core.key_mask, core.key_low, ALU.mult))
            link(nc.vector.tensor_scalar(core.key_mask, core.key_mask, -NEG, NEG, ALU.mult, ALU.add))


def build(nc, ins, out):
    with ExitStack() as ctx:
        core = Core(nc, ctx, ins, out)
        allot(core)
        x, xn, z, acc, x_t = core.x, core.xn, core.z, core.acc, core.x_t
        ones = core.consts

        def loader(fields, source):
            return lambda sp, landed: load(sp, fields, source, landed)

        first_loads(core)

        w = Fields(core.weights_1, "l0x")
        norm(core, x, xn, None, "layer", 1e-5)
        norm(core, xn, xn, x_t, "layer", 1e-5, w["lat_w"], w["lat_b"])
        norm_context(core, w["ctx_w"], w["ctx_b"], core.media_t)
        fold_context_l0(core, w, core.media_t)
        dense = Fields(core.weights_2, "l0f")
        cross_attention(core, x_t, x, "clip", rows=w["bo"], extra=loader(dense, ins["l0f"]))

        w = dense
        norm(core, x, xn, x_t, "layer", 1e-5)
        project_heads(core, x_t, w["wq"], w["wk"], w["wv"])
        l1x = Fields(core.weights_1, "l1x")
        self_attention(core, extra=loader(l1x, ins["l1x"]))
        attention_output(core, w.tiled("wo_stacked"), acc)
        rms_add(core, acc, w["attn_w"], xn, z)
        route(core, x_t, w["router"])
        feed_forward(core, x_t, E8, 1, w.tiled("ew1"), w.tiled("ew3"), w.tiled("ew2"), acc, comb=core.comb)
        rms_add(core, acc, w["moe_w"], x, x)
        turn_rows(core, z, x_t)
        feed_forward(core, x_t, 1, 4, w.tiled("w1"), w.tiled("w3"), w.tiled("w2"), acc)
        rms_add(core, acc, w["ff_w"], z, z)
        add(core, x, z)

        w = l1x
        l1f = Fields(core.weights_2, "l1f")
        norm(core, x, xn, x_t, "layer", 1e-5)
        fold_context(core, w, core.ctx_t, w["wk_t"], w["wv_t"], w["wq"], w["wo_t"], ones["head_rows_scaled"],
                     ones["head_rows"], w["bq"], w["bk"], w["bv"])
        cross_attention(core, x_t, x, "bias", rows=w["bo"], extra=loader(l1f, ins["l1f"]))

        w = l1f
        l2a = Fields(core.weights_1, "l2a")
        l2b = Fields(core.weights_1, "l2b", width("l2a"))
        norm(core, x, xn, x_t, "layer", 1e-5)
        route(core, x_t, w["gate"], among_chosen=True)
        w12 = w["w12_t"].rearrange("p (e c w) -> p e c w", c=4, w=P)
        feed_forward(core, x_t, E8, 2, Pairs(w12, 0), Pairs(w12, 2), w.tiled("w3_t"), x, comb=core.comb, add=True,
                     extra=loader(l2a, ins["l2a"][0]))

        l2f = Fields(core.weights_2, "l2f", width("l1f"))
        norm(core, x, z, None, "layer", 1e-5, extra=loader(l2f, ins["l2f"]))
        with nc.Fori(0, L2_LAYERS) as layer:
            w = l2a
            norm(core, z, xn, x_t, "rms", 1e-6, w["n1"])
            project_heads(core, x_t, w["wq"], w["wk"], w["wv"], (w["wq_turned"], w["wk_turned"]),
                          (w["bq"], w["bq_turned"], w["bk"], w["bk_turned"]))
            self_attention(core, extra=loader(l2b, ins["l2b"][bass.ds(layer, 1)].rearrange("a p n -> (a p) n")))
            attention_output(core, w.tiled("wo_stacked"), z, w["bo"], w["bv"], w["wo_t"])
            norm(core, z, xn, x_t, "rms", 1e-6, w["n2"])
            fold_context(core, w, core.ctx_t, w["wk_cross"], w["wv_cross"], w["wq_cross"], w["wo_cross"],
                         ones["head_rows_scaled"], ones["head_rows"])
            cross_attention(core, x_t, z, "mask")
            norm(core, z, xn, x_t, "rms", 1e-6, w["n3"])
            feed_forward(core, x_t, 1, 4, l2b.tiled("wg"), l2b.tiled("wu"), l2b.tiled("wd"), z, add=True,
                         extra=loader(l2a, ins["l2a"][bass.ds(layer + 1, 1)].rearrange("a p n -> (a p) n")))
            with core.stage():
                pass
        rms_add(core, z, l2f["nf"], x, x, 1e-6)

        w = l2f
        l3x = Fields(core.weights_1, "l3x")
        norm(core, x, xn, x_t, "layer", 1e-5)
        route_over_tokens(core, x_t, w["gate"], w["gate_b"][0:E8, :])
        pooled_experts(core, x_t, w, x, extra=loader(l3x, ins["l3x"]))

        w = l3x
        l3f = Fields(core.weights_2, "l3f")
        norm(core, x, xn, None, "layer", 1e-5)
        norm(core, xn, xn, x_t, "layer", 1e-5, w["lat_w"], w["lat_b"])
        norm_context(core, w["media_w"], w["media_b"], core.media_t)
        latent_attention(core, x_t, core.media_t, w, extra=loader(l3f, ins["l3f"]))

        w = l3f
        norm(core, x, xn, x_t, "layer", 1e-5)
        route(core, x_t, w["gate"], bias=w["gate_b"], among_chosen=True)
        turn_experts(core, [(core.comb, core.comb_t)])
        feed_forward(core, x_t, E8, 4, w.tiled("w1"), None, w.tiled("w2"), x, comb=core.comb, b1=w["b1"], b2=w["b2"],
                     add=True)
        finish(core)


class Pairs:

    def __init__(self, tiles, first):
        self.tiles, self.first = tiles, first

    def __getitem__(self, key):
        rows, n, cols = key
        return self.tiles[rows, n // 2, self.first + n % 2, cols]


def add(core, dst, other):
    nc = core.nc
    with core.stage() as (block, (added, *_)):
        @block.vector
        def _(dve):
            nc.vector.tensor_tensor(dst, dst, other, ALU.add).then_inc(added, 1)


def finish(core):
    with core.stage() as (block, (written, *_)):
        @block.sync
        def _(sp):
            sp.dma_start(core.out.rearrange("(n p) d -> p n d", p=P), core.x).then_inc(written, 16)
            sp.wait_ge(written, 16)


def rows_of(v):
    return np.broadcast_to(np.asarray(v).reshape(1, -1), (P, np.asarray(v).size))


def cols_of(v):
    return np.ascontiguousarray(np.asarray(v).reshape(-1, P).T)


def tiles_of(w):
    w = np.asarray(w)
    return w.reshape(-1, P, w.shape[1]).transpose(1, 0, 2).reshape(P, -1)


def experts_of(w):
    w = np.asarray(w)
    return w.transpose(1, 0, 2).reshape(P, -1)


def head_turned(w):
    w = np.asarray(w)
    return w.reshape(H, 2, HD // 2, *w.shape[1:])[:, ::-1].reshape(w.shape)


def stacked_rows(w):
    w = np.asarray(w)
    out = np.zeros((NC, HPC, HROWS, w.shape[1]), w.dtype)
    out[:, :, 0:HD] = w.reshape(NC, HPC, HD, w.shape[1])
    return out.reshape(NC, P, w.shape[1]).transpose(1, 0, 2).reshape(P, -1)


def pack(blob, parts):
    for name, n in LAYOUTS[blob].items():
        assert parts[name].shape == (P, n), (blob, name, parts[name].shape)
    assert len(parts) == len(LAYOUTS[blob])
    return np.ascontiguousarray(np.concatenate([parts[name] for name in LAYOUTS[blob]], axis=1))


def constants():
    row = np.arange(P)
    half = HD // 2
    angle = np.arange(S, dtype=np.float32)[None, :] * \
        (np.float32(1.0) / np.float32(10000.0) ** (np.arange(0, HD, 2, dtype=np.float32) / np.float32(HD)))[row % half][:, None]
    head_rows = (row[:, None] // HD == np.arange(H)[None, :]).astype(np.float32)
    half_rows = (row[:, None] // (P // 2) == np.arange(2)[None, :]).astype(np.float32)
    lower = (np.arange(E8)[None, :] < np.arange(E8)[:, None]).astype(np.float32).reshape(1, -1)
    parts = dict(
        ident=np.eye(P, dtype=np.float32),
        pick_sum=((row[:, None] % HROWS == HD) & (row[:, None] // HROWS == row[None, :] // HROWS)).astype(np.float32),
        head_rows=head_rows, head_rows_scaled=head_rows * np.float32(HD ** -0.5),
        half_rows=half_rows, half_rows_scaled=half_rows * np.float32((P // 2) ** -0.5),
        stack_rows=(row[:, None] // HROWS == np.arange(HPC)[None, :]).astype(np.float32),
        one_row=(row[:, None] % HROWS == ONE_ROW).astype(np.float32), zero=np.zeros((P, 1), np.float32),
        lower=np.repeat(lower, P, axis=0), cos=np.cos(angle),
        sin=np.sin(angle) * np.where(row % HD < half, np.float32(-1), np.float32(1))[:, None],
        keys=np.repeat(np.arange(CK, dtype=np.float32)[None, :], P, axis=0))
    above = row[None, :] > row[:, None]
    masks = np.stack([np.eye(P, dtype=np.float32), np.where(above, np.float32(NEG), np.float32(0)),
                      np.where(above.T, np.float32(NEG), np.float32(0))], axis=1)
    pick = np.zeros((P, 4, NC, P), np.float16)
    for which, parts_taken in enumerate(((0, 1), (2,), (0, 2), (1,))):
        for c in range(NC):
            for j in range(HPC):
                for r in parts_taken:
                    for d in range(HD):
                        pick[(c * HPC + j) * HD + d, which, c, j * HROWS + r * HD + d] = 1
    return pack("consts", {k: v.astype(np.float32) for k, v in parts.items()}), masks.astype(mybir.dt.np(BF16)), pick


def host_arrays(a):
    l0, f0, l1, f1 = "L0_xattn_", "L0_ffn_", "L1_xattn_", "L1_ffn_"
    l2, f2, l3, f3 = "L2_xattn_", "L2_ffn_", "L3_xattn_", "L3_ffn_"
    inner = H3 * P
    out = {}
    out["consts"], out["masks"], out["pick"] = constants()
    out["x"] = a["x"].reshape(T, P)
    out["ctx"] = a["ctx_1024"].reshape(B * CK, P)
    out["ctx_t"] = np.ascontiguousarray(out["ctx"].T)
    out["tokens"] = np.ascontiguousarray(a["itok_BxS_0_255"].reshape(NT, P).T)
    out["l0x"] = pack("l0x", dict(
        wq_t=tiles_of(a[l0 + "Wq"].T), wk=a[l0 + "Wkv"][:, :inner], wv=a[l0 + "Wkv"][:, inner:], wo=tiles_of(a[l0 + "Wo"]),
        lat_w=cols_of(a[l0 + "ln_l_w"]), lat_b=cols_of(a[l0 + "ln_l_b"]), ctx_w=cols_of(a[l0 + "ln_c_w"]),
        ctx_b=cols_of(a[l0 + "ln_c_b"]), bo=rows_of(a[l0 + "bo"])))
    out["l0f"] = pack("l0f", dict(
        wq=a[f0 + "wq"], wk=a[f0 + "wk"], wv=a[f0 + "wv"], wo_stacked=stacked_rows(a[f0 + "wo"]), w1=a[f0 + "w1"],
        w3=a[f0 + "w3"], w2=tiles_of(a[f0 + "w2"]), router=a[f0 + "router_w"], ew1=experts_of(a[f0 + "ew1"]),
        ew3=experts_of(a[f0 + "ew3"]), ew2=experts_of(a[f0 + "ew2"]), attn_w=rows_of(a[f0 + "attn_norm_w"]),
        ff_w=rows_of(a[f0 + "ff_norm_w"]), moe_w=rows_of(a[f0 + "moe_norm_w"])))
    out["l1x"] = pack("l1x", dict(
        wq=a[l1 + "Wq"], wk_t=a[l1 + "Wk"].T, wv_t=a[l1 + "Wv"].T, wo_t=a[l1 + "Wo"].T, bq=cols_of(a[l1 + "bq"]),
        bk=cols_of(a[l1 + "bk"]), bv=cols_of(a[l1 + "bv"]), bo=rows_of(a[l1 + "bo"])))
    out["l1f"] = pack("l1f", dict(
        w12_t=experts_of(a[f1 + "w12"].transpose(0, 2, 1)),
        w3_t=a[f1 + "w3"].transpose(0, 2, 1).reshape(E8, 2, P, P).transpose(2, 0, 1, 3).reshape(P, -1),
        gate=a[f1 + "gate_w"].T))
    l2a, l2b = [], []
    for i in range(L2_LAYERS):
        wqkv, bqkv = a[l2 + "Wqkv"][i], a[l2 + "bqkv"][i]
        wq, wk, wv = wqkv[0:P], wqkv[P:2 * P], wqkv[2 * P:]
        bq, bk, bv = bqkv[0:P], bqkv[P:2 * P], bqkv[2 * P:]
        wkv = a[l2 + "Wkv_c"][i]
        l2a.append(pack("l2a", dict(
            wq=wq.T, wq_turned=head_turned(wq).T, wk=wk.T, wk_turned=head_turned(wk).T, wv=wv.T,
            wo_stacked=stacked_rows(a[l2 + "Wo"][i].T), wo_t=a[l2 + "Wo"][i].T, bo=rows_of(a[l2 + "bo"][i]),
            wq_cross=a[l2 + "Wq_c"][i], wk_cross=wkv[0:P].T, wv_cross=wkv[P:].T, wo_cross=a[l2 + "Wo_c"][i].T,
            bq=cols_of(bq), bq_turned=cols_of(head_turned(bq)), bk=cols_of(bk), bk_turned=cols_of(head_turned(bk)),
            bv=cols_of(bv), n1=cols_of(a[l2 + "n1"][i]), n2=cols_of(a[l2 + "n2"][i]), n3=cols_of(a[l2 + "n3"][i]))))
        l2b.append(pack("l2b", dict(wg=a[l2 + "Wg"][i].T, wu=a[l2 + "Wu"][i].T, wd=tiles_of(a[l2 + "Wd"][i].T))))
    l2a.append(np.zeros_like(l2a[0]))
    out["l2a"], out["l2b"] = np.stack(l2a), np.stack(l2b)
    gate_b = np.zeros((P, 1), np.float32)
    gate_b[0:E8, 0] = a[f2 + "gate_b"]
    out["l2f"] = pack("l2f", dict(
        w1=experts_of(a[f2 + "w1"]), w2=experts_of(a[f2 + "w2"]), w3=experts_of(a[f2 + "w3"]), b1=a[f2 + "b1"].T,
        b2=a[f2 + "b2"].T, b3=a[f2 + "b3"].T, gate=a[f2 + "gate_w"], gate_b=gate_b, nf=rows_of(a[l2 + "nf"])))
    out["l3x"] = pack("l3x", dict(
        wq=a[l3 + "Wq"], wk=a[l3 + "Wkv"][:, :inner], wv=a[l3 + "Wkv"][:, inner:], wo=tiles_of(a[l3 + "Wo"]),
        bq=cols_of(a[l3 + "bq"]), bk=cols_of(a[l3 + "bkv"][:inner]), bv=cols_of(a[l3 + "bkv"][inner:]),
        bo=rows_of(a[l3 + "bo"]), media_w=cols_of(a[l3 + "gamma_media"]), media_b=cols_of(a[l3 + "beta_media"]),
        lat_w=cols_of(a[l3 + "gamma_lat"]), lat_b=cols_of(a[l3 + "beta_lat"])))
    b2 = np.zeros((P, P), np.float32)
    b2[0:E8] = a[f3 + "b2"]
    out["l3f"] = pack("l3f", dict(
        w1=experts_of(a[f3 + "w1"]), w2=a[f3 + "w2"].reshape(E8, 4, P, P).transpose(2, 0, 1, 3).reshape(P, -1),
        b1=a[f3 + "b1"].reshape(E8 * 4, P).T, gate=a[f3 + "w_gate"], gate_b=rows_of(a[f3 + "b_gate"]), b2=b2))
    return out


def kernel(**inputs):
    import concourse.bacc as bacc
    from concourse.bass_utils import run_bass_kernel_spmd

    nc = bacc.Bacc("TRN2", target_bir_lowering=False, num_devices=1)
    arrays = {f"in_{name}": np.ascontiguousarray(v)
              for name, v in host_arrays({k: np.asarray(v) for k, v in inputs.items()}).items()}
    ins = {name[3:]: nc.dram_tensor(name, v.shape, mybir.dt.from_np(v.dtype), kind="ExternalInput").ap()
           for name, v in arrays.items()}
    out = nc.dram_tensor("out", (T, P), F32, kind="ExternalOutput").ap()
    build(nc, ins, out)
    result = run_bass_kernel_spmd(nc, [arrays], core_ids=[0]).results[0]["out"]
    return result.reshape(B, S, P)
```

```python
from contextlib import ExitStack, contextmanager

import numpy as np

import concourse.bass as bass
from concourse import mybir

ALU = mybir.AluOpType
ACT = mybir.ActivationFunctionType
AX = mybir.AxisListType
F32 = mybir.dt.float32
F16 = mybir.dt.float16
BF16 = mybir.dt.bfloat16
I32 = mybir.dt.int32

P = 128
B, S = 2, 512
T = B * S
NT = T // P
NTB = S // P
CK = 32
H = 16
HD = P // H
HROWS = 32
HPC = P // HROWS
NC = H // HPC
ONE_ROW = 3 * HD
NEG = -1e30
SIGNALS = 50
WARM_COLUMNS = 16
E8 = 8
L2_LAYERS = 4
H3 = 8
LOOKBACK = 128


class Core:

    def __init__(self, nc, ctx, ins, out):
        self.nc, self.ctx, self.ins, self.out = nc, ctx, ins, out
        self.sets = [[ctx.enter_context(nc.semaphore(f"stage_{i}_signal_{j}")) for j in range(SIGNALS)]
                     for i in range(2)]
        self.n_blocks = 0
        self.shared = None
        self.n_warm = 0

    def sbuf(self, name, shape, dt=F32):
        return self.ctx.enter_context(self.nc.sbuf_tensor(name, shape, dt))

    def eps_col(self, eps):
        return self.eps[:, 0:1] if eps == 1e-5 else self.eps[:, 1:2]

    @contextmanager
    def stage(self, n_signals=24):
        if self.shared is None:
            with self.new_block() as (block, signals):
                yield block, signals
        else:
            block, signals = self.shared
            self.shared = block, signals[n_signals:]
            yield block, signals[:n_signals]

    @contextmanager
    def joined(self):
        with self.new_block() as self.shared:
            yield
        self.shared = None

    @contextmanager
    def new_block(self):
        mine, idle = self.sets[self.n_blocks % 2], self.sets[1 - self.n_blocks % 2]
        self.n_blocks += 1
        with self.nc.Block(no_gpsimd_drain=True) as block:
            @block.gpsimd
            def _(pool):
                pool.sem_clear(range(idle[0].num, idle[-1].num + 1))
            yield block, mine


def chained(engine, done):
    count = [0]

    def link(instruction):
        count[0] += 1
        instruction.then_inc(done, 1)
        engine.wait_ge(done, count[0])
    return link


LAYOUTS = {
    "consts": dict(ident=P, head_rows=H, head_rows_scaled=H, half_rows=2, half_rows_scaled=2,
                   stack_rows=HPC, one_row=1, zero=1, lower=E8 * E8, keys=CK),
    "tables": dict(cos=S, sin=S),
    "l0x": dict(wq_t=8 * P, wk=8 * P, wv=8 * P, wo=8 * P, lat_w=1, lat_b=1, ctx_w=1, ctx_b=1, bo=P),
    "l0f": dict(wq=P, wk=P, wv=P, wo=P, w1=4 * P, w3=4 * P, w2=4 * P, router=E8,
                ew1=E8 * P, ew3=E8 * P, ew2=E8 * P, attn_w=P, ff_w=P, moe_w=P),
    "l1x": dict(wq=P, wk_t=P, wv_t=P, wo_t=P, bq=1, bk=1, bv=1, bo=P),
    "l1f": dict(w12_t=E8 * 4 * P, w3_t=E8 * 2 * P, gate=E8),
    "l2a": dict(wq=P, wq_turned=P, wk=P, wk_turned=P, wv=P, wo_t=P, bo=P,
                wq_cross=P, wk_cross=P, wv_cross=P, wo_cross=P,
                bq=1, bq_turned=1, bk=1, bk_turned=1, bv=1, n1=1, n2=1),
    "l2b": dict(wg=4 * P, wu=4 * P, wd=4 * P, n3=1),
    "l2f": dict(w1=E8 * P, w2=E8 * P, w3=E8 * P, b1=E8, b2=E8, b3=E8, gate=E8, gate_b=1, nf=P),
    "l3x": dict(wq=H3 * P, wk=H3 * P, wv_t=H3 * P, wo=H3 * P, bq=H3, bk=H3, bv=H3, bo=P,
                media_w=1, media_b=1, lat_w=1, lat_b=1),
    "l3f": dict(w1=E8 * 4 * P, w2=E8 * 4 * P, b1=E8 * 4, gate=E8, gate_b=E8, b2=P),
}


def width(blob):
    return sum(LAYOUTS[blob].values())


class Fields:

    def __init__(self, region, blob, start=0):
        self.all = region[:, start:start + width(blob)]
        self.parts = {}
        for name, n in LAYOUTS[blob].items():
            self.parts[name] = region[:, start:start + n]
            start += n

    def __getitem__(self, name):
        return self.parts[name]

    def tiled(self, name, w=P):
        return self.parts[name].rearrange("p (a w) -> p a w", w=w)


def load(sp, fields, source, landed):
    sp.dma_start(fields.all, source).then_inc(landed, 16)
    sp.wait_ge(landed, 16)


def warm(core, function):
    column = core.n_warm % WARM_COLUMNS
    core.n_warm += 1
    core.nc.scalar.activation(core.warm[:, column:column + 1], core.eps[:, 0:1], function)


def norm(core, src, xn, xt, mode, eps, scale=None, bias=None, extra=None, beside=None):
    nc, ps, ident = core.nc, core.ps, core.consts["ident"]
    scalars, vectors = (1, 4, 7), (0, 2, 3, 5, 6)
    halves = (range(0, NTB), range(NTB, NT))
    banks = (0, 0, 0, 0, 1, 1, 2, 2)
    with core.stage(12) as (block, (stats_ready, means_ready, root_ready, rstd_ready, scaled_by_vector, scaled_by_scalar,
                                  shift_ready, turned, landed, turned_out, beside_1, beside_2, *_)):
        if beside is not None:
            beside.signals(beside_1, beside_2)

        if extra is not None:
            @block.sync
            def _(sp):
                extra(sp, landed)

        @block.vector
        def _(dve):
            for half in halves:
                if mode == "layer":
                    for n in half:
                        nc.vector.bn_stats(core.stats[:, n, :], src[:, n, :]).then_inc(stats_ready, 1)
                    for n in half:
                        dve.wait_ge(stats_ready, n + 1)
                        nc.vector.bn_aggr(core.mean_var[:, n, :], core.stats[:, n, :]).then_inc(means_ready, 1)
                else:
                    for n in half:
                        nc.vector.scalar_tensor_tensor(core.junk[:, n, :], src[:, n, :], 1.0, src[:, n, :], ALU.mult,
                                                       ALU.mult, accum_out=core.mean_var[:, n, 1:2]).then_inc(means_ready, 1)
            for k, half in enumerate(halves):
                columns = slice(half[0], half[-1] + 1)
                dve.wait_ge(root_ready, k + 1)
                nc.vector.reciprocal(core.rstd[:, columns], core.root[:, columns]).then_inc(rstd_ready, 1)
                dve.wait_ge(rstd_ready, k + 1)
                if mode == "layer":
                    nc.vector.scalar_tensor_tensor(core.shift[:, columns], core.mean_var[:, columns, 0], -1.0,
                                                   core.rstd[:, columns], ALU.mult, ALU.mult).then_inc(shift_ready, 1)
                for n in half:
                    if n in scalars:
                        continue
                    if mode == "layer":
                        nc.vector.tensor_scalar(xn[:, n, :], src[:, n, :], core.mean_var[:, n, 0:1], core.rstd[:, n:n + 1],
                                                ALU.subtract, ALU.mult).then_inc(scaled_by_vector, 1)
                    else:
                        nc.vector.tensor_scalar(xn[:, n, :], src[:, n, :], core.rstd[:, n:n + 1], None,
                                                ALU.mult).then_inc(scaled_by_vector, 1)
            dve.wait_ge(scaled_by_scalar, len(scalars))
            dve.wait_ge(scaled_by_vector, len(vectors))
            if xt is not None:
                for n in (4, 6):
                    dve.wait_ge(turned, n + 2)
                    out, source = xt[:, n * P:(n + 2) * P], ps[:, banks[n], 0:2 * P]
                    if scale is None:
                        nc.vector.tensor_copy(out, source).then_inc(turned_out, 1)
                    elif bias is None:
                        nc.vector.tensor_scalar(out, source, scale, None, ALU.mult).then_inc(turned_out, 1)
                    else:
                        nc.vector.tensor_scalar(out, source, scale, bias, ALU.mult, ALU.add).then_inc(turned_out, 1)
            if beside is not None:
                beside.vector(dve)

        @block.scalar
        def _(act):
            warm(core, ACT.Sqrt)
            for half in halves:
                columns = slice(half[0], half[-1] + 1)
                act.wait_ge(means_ready, half[-1] + 1)
                nc.scalar.activation(core.root[:, columns], core.mean_var[:, columns, 1], ACT.Sqrt, bias=core.eps_col(eps),
                                     scale=1.0 if mode == "layer" else 1.0 / P).then_inc(root_ready, 1)
            for k, half in enumerate(halves):
                act.wait_ge(rstd_ready, k + 1)
                if mode == "layer":
                    act.wait_ge(shift_ready, k + 1)
                for n in half:
                    if n in scalars:
                        kw = dict(bias=core.shift[:, n:n + 1]) if mode == "layer" else {}
                        nc.scalar.activation(xn[:, n, :], src[:, n, :], ACT.Identity, scale=core.rstd[:, n:n + 1],
                                             **kw).then_inc(scaled_by_scalar, 1)
            act.wait_ge(scaled_by_vector, len(vectors))
            act.wait_ge(scaled_by_scalar, len(scalars))
            if xt is not None:
                act.wait_ge(turned, NTB)
                kw = {}
                if scale is not None:
                    kw["scale"] = scale
                if bias is not None:
                    kw["bias"] = bias
                nc.scalar.activation(xt[:, 0:S], ps[:, 0, :], ACT.Identity, **kw).then_inc(turned_out, 1)
            if beside is not None:
                beside.scalar(act)

        @block.tensor
        def _(pe):
            if beside is not None:
                beside.tensor(pe)
            if xt is not None:
                for n in range(NT):
                    if n in scalars:
                        pe.wait_ge(scaled_by_scalar, scalars.index(n) + 1)
                    else:
                        pe.wait_ge(scaled_by_vector, vectors.index(n) + 1)
                    column = (n - banks.index(banks[n])) * P
                    nc.tensor.transpose(ps[:, banks[n], column:column + P], xn[:, n, :], ident).then_inc(turned, 1)
                pe.wait_ge(turned_out, 3)


def turn_rows(core, src, xt, also):
    nc, ps = core.nc, core.ps
    with core.stage(3) as (block, (turned, turned_out, added, *_)):
        @block.tensor
        def _(pe):
            for n in range(NT):
                nc.tensor.transpose(ps[:, n // NTB, (n % NTB) * P:(n % NTB + 1) * P], src[:, n, :],
                                    core.consts["ident"]).then_inc(turned, 1)
            pe.wait_ge(turned_out, B)

        @block.scalar
        def _(act):
            for b in range(B):
                act.wait_ge(turned, NTB * (b + 1))
                nc.scalar.activation(xt[:, b * S:(b + 1) * S], ps[:, b, :], ACT.Copy).then_inc(turned_out, 1)

        @block.vector
        def _(dve):
            nc.vector.tensor_tensor(also, also, src, ALU.add).then_inc(added, 1)
            dve.wait_ge(added, 1)


def rms_add(core, v, weight, base, dst, eps=1e-5):
    nc = core.nc
    with core.stage(5) as (block, (means_ready, root_ready, rstd_ready, scaled, added, *_)):
        @block.scalar
        def _(act):
            warm(core, ACT.Sqrt)
            act.wait_ge(means_ready, NT)
            nc.scalar.activation(core.root[:, :], core.mean_var[:, :, 1], ACT.Sqrt, bias=core.eps_col(eps),
                                 scale=1.0 / P).then_inc(root_ready, 1)

        @block.vector
        def _(dve):
            for n in range(NT):
                nc.vector.scalar_tensor_tensor(core.junk[:, n, :], v[:, n, :], 1.0, v[:, n, :], ALU.mult, ALU.mult,
                                               accum_out=core.mean_var[:, n, 1:2]).then_inc(means_ready, 1)
            dve.wait_ge(root_ready, 1)
            nc.vector.reciprocal(core.rstd[:, :], core.root[:, :]).then_inc(rstd_ready, 1)
            dve.wait_ge(rstd_ready, 1)
            for n in range(NT):
                nc.vector.scalar_tensor_tensor(v[:, n, :], v[:, n, :], core.rstd[:, n:n + 1], weight, ALU.mult,
                                               ALU.mult).then_inc(scaled, 1)
            dve.wait_ge(scaled, NT)
            nc.vector.tensor_tensor(dst, base, v, ALU.add).then_inc(added, 1)
            dve.wait_ge(added, 1)


class ContextFold:

    def __init__(self, core, ctx_t, wk, wv, wq, wo, bk=None, bv=None):
        self.core, self.ctx_t, self.wk, self.wv, self.wq, self.wo, self.bk, self.bv = core, ctx_t, wk, wv, wq, wo, bk, bv

    def signals(self, kv_ready, spread, product, evacuated):
        self.kv_ready, self.spread, self.product, self.evacuated = kv_ready, spread, product, evacuated

    def project(self, pe):
        nc, ps = self.core.nc, self.core.ps
        nc.tensor.matmul(ps[:, 1, 0:B * CK], self.wk, self.ctx_t, start=True, stop=True)
        nc.tensor.matmul(ps[:, 1, B * CK:2 * B * CK], self.wv, self.ctx_t, start=True, stop=True).then_inc(self.kv_ready, 1)

    def spread_heads(self, dve):
        core = self.core
        dve.wait_ge(self.kv_ready, 1)
        for first, dst, mask, bias in ((0, core.k_spread, core.consts["head_rows_scaled"], self.bk),
                                       (B * CK, core.v_spread, core.consts["head_rows"], self.bv)):
            for b in range(B):
                core.nc.vector.scalar_tensor_tensor(
                    dst[:, b, :].rearrange("p (h k) -> p h k", k=CK),
                    core.ps[:, 1, first + b * CK:first + (b + 1) * CK].unsqueeze(1).to_broadcast([P, H, CK]),
                    bias if bias is not None else core.consts["zero"],
                    mask.unsqueeze(2).to_broadcast([P, H, CK]), ALU.add, ALU.mult).then_inc(self.spread, 1)

    def fold_keys(self, pe):
        core = self.core
        pe.wait_ge(self.spread, B)
        for b in range(B):
            last = core.nc.tensor.matmul(core.ps[:, 2 + b, :], self.wq, core.k_spread[:, b, :], start=True, stop=True)
        last.then_inc(self.product, 1)

    def fold_values(self, pe):
        core = self.core
        pe.wait_ge(self.spread, 2 * B)
        for b in range(B):
            for c in range(NC):
                last = core.nc.tensor.matmul(core.ps[:, b, c * P:(c + 1) * P], core.v_spread[:, b, c * P:(c + 1) * P],
                                             self.wo, start=True, stop=True)
        last.then_inc(self.product, 1)

    def evacuate_keys(self, dve):
        core = self.core
        dve.wait_ge(self.product, 1)
        core.nc.vector.tensor_copy(core.a[:, :, :], core.ps[:, 2:4, :]).then_inc(self.evacuated, 1)

    def evacuate_values(self, dve):
        core = self.core
        dve.wait_ge(self.product, 2)
        core.nc.vector.tensor_copy(core.bb[:, :, :], core.ps[:, 0:2, :]).then_inc(self.evacuated, 1)


def fold_context(core, fold):
    with core.stage(4) as (block, (kv_ready, spread, product, evacuated, *_)):
        fold.signals(kv_ready, spread, product, evacuated)

        @block.tensor
        def _(pe):
            fold.project(pe)
            fold.fold_keys(pe)
            fold.fold_values(pe)
            pe.wait_ge(evacuated, 2)

        @block.vector
        def _(dve):
            fold.spread_heads(dve)
            fold.evacuate_keys(dve)
            fold.evacuate_values(dve)


class WideKeysAndValues:

    def __init__(self, core, w, ctx_t):
        self.core, self.ctx_t, self.wk, self.wv = core, ctx_t, w.tiled("wk"), w.tiled("wv")

    def signals(self, kv_ready, spread):
        self.kv_ready, self.spread = kv_ready, spread

    def tensor(self, pe):
        for bank, weights in ((3, self.wk), (4, self.wv)):
            for i in range(8):
                last = self.core.nc.tensor.matmul(self.core.ps[:, bank, i * B * CK:(i + 1) * B * CK], weights[:, i, :],
                                                  self.ctx_t, start=True, stop=True)
            last.then_inc(self.kv_ready, 1)

    def vector(self, dve):
        core = self.core
        for n, (bank, dst, mask) in enumerate(((3, core.k_spread, core.consts["half_rows_scaled"]),
                                               (4, core.v_spread, core.consts["half_rows"]))):
            dve.wait_ge(self.kv_ready, n + 1)
            kv = core.ps[:, bank, :].rearrange("p (i b k) -> p i b k", b=B, k=CK)
            for b in range(B):
                out = dst[:, b, :].rearrange("p (i r k) -> p i r k", r=2, k=CK)
                for r in range(2):
                    core.nc.vector.tensor_scalar(out[:, :, r, :], kv[:, :, b, :], mask[:, r:r + 1], None,
                                                 ALU.mult).then_inc(self.spread, 1)

    def scalar(self, act):
        pass


class WideFold:

    def __init__(self, core, w):
        self.core, self.wq_t, self.wo = core, w.tiled("wq_t"), w.tiled("wo")

    def signals(self, product, evacuated):
        self.product, self.evacuated = product, evacuated

    def tensor(self, pe):
        nc, ps, core = self.core.nc, self.core.ps, self.core
        for b in range(B):
            for i in range(8):
                last = nc.tensor.matmul(ps[:, 3 + b, 64 * i:64 * i + 64], self.wq_t[:, i, :],
                                        core.k_spread[:, b, 64 * i:64 * i + 64], start=True, stop=True)
        last.then_inc(self.product, 1)
        for b in range(B):
            for i in range(8):
                rows = 64 * (i % 2)
                last = nc.tensor.matmul(ps[rows:rows + 64, 5 + b, (i // 2) * P:(i // 2 + 1) * P],
                                        core.v_spread[:, b, 64 * i:64 * i + 64], self.wo[:, i, :], start=True, stop=True)
        last.then_inc(self.product, 1)

    def vector(self, dve):
        dve.wait_ge(self.product, 1)
        self.core.nc.vector.tensor_copy(self.core.a[:, :, :], self.core.ps[:, 3:5, :]).then_inc(self.evacuated, 1)

    def scalar(self, act):
        act.wait_ge(self.product, 2)
        self.core.nc.scalar.activation(self.core.bb[:, :, :], self.core.ps[:, 5:7, :], ACT.Copy).then_inc(self.evacuated, 1)


def cross_attention(core, x_t, resid, mode, rows=None, bq=None, extra=None):
    nc, ps, ident = core.nc, core.ps, core.consts["ident"]
    SCORE_BANKS = (0, 1, 6)
    with core.stage(13) as (block, (scores_ready, max_ready, shifted_ready, exp_ready, sums_ready, rsum_ready, probs_ready,
                                  turned, turned_out, output_ready, added, rows_added, landed, *_)):
        if extra is not None:
            @block.sync
            def _(sp):
                extra(sp, landed)

        def score_bank(n):
            return ps[:, SCORE_BANKS[n % 3], :]

        def by_head(ap):
            return ap.rearrange("p (h k) -> p h k", k=CK)

        @block.tensor
        def _(pe):
            def scores(n):
                if n >= 3:
                    pe.wait_ge(shifted_ready, n - 2)
                if mode == "bias":
                    nc.tensor.matmul(score_bank(n), bq.to_broadcast([P, P]), core.k_spread[:, n // NTB, :],
                                     start=True, stop=False)
                last = nc.tensor.matmul(score_bank(n), x_t[:, n * P:(n + 1) * P], core.a[:, n // NTB, :],
                                        start=(mode != "bias"), stop=(mode != "mask"))
                if mode == "mask":
                    last = nc.tensor.matmul(score_bank(n), core.masks[:, 0, :],
                                            core.key_mask_b[:, n, :].unsqueeze(1).to_broadcast([P, H, CK]),
                                            start=False, stop=True)
                last.then_inc(scores_ready, 1)

            def turn(n):
                pe.wait_ge(probs_ready, n + 1)
                if n >= 2:
                    pe.wait_ge(turned_out, n - 1)
                for c in range(NC):
                    last = nc.tensor.transpose(ps[:, 2 + n % 2, c * P:(c + 1) * P],
                                               core.probs[:, n % 2, c * P:(c + 1) * P], ident)
                last.then_inc(turned, 1)

            def output(n):
                pe.wait_ge(turned_out, n + 1)
                if n >= 2:
                    pe.wait_ge(added, n - 1)
                for c in range(NC):
                    last = nc.tensor.matmul(ps[:, 4 + n % 2, 0:P], core.probs_t[:, n % 2, c * P:(c + 1) * P],
                                            core.bb[:, n // NTB, c * P:(c + 1) * P], start=(c == 0), stop=(c == NC - 1))
                last.then_inc(output_ready, 1)

            scores(0)
            for n in range(NT + 2):
                if n + 1 < NT:
                    scores(n + 1)
                if 0 <= n - 2 < NT:
                    output(n - 2)
                if 0 <= n - 1 < NT:
                    turn(n - 1)

        @block.scalar
        def _(act):
            warm(core, ACT.Exp)
            for n in range(NT + 1):
                if n < NT:
                    act.wait_ge(shifted_ready, n + 1)
                    if n >= 2:
                        act.wait_ge(turned, n - 1)
                    nc.scalar.activation(core.probs[:, n % 2, :], core.shifted[:, n % 2, :], ACT.Exp).then_inc(exp_ready, 1)
                m = n - 1
                if m >= 0:
                    act.wait_ge(turned, m + 1)
                    if m >= 2:
                        act.wait_ge(output_ready, m - 1)
                    nc.scalar.activation(core.probs_t[:, m % 2, :], ps[:, 2 + m % 2, :], ACT.Copy).then_inc(turned_out, 1)

        @block.vector
        def _(dve):
            if rows is not None:
                nc.vector.tensor_tensor(resid, resid, rows.unsqueeze(1).to_broadcast([P, NT, P]), ALU.add).then_inc(rows_added, 1)
            for n in range(NT + 3):
                m, k = n - 1, n - 3
                if n < NT:
                    dve.wait_ge(scores_ready, n + 1)
                    if mode != "clip":
                        nc.vector.tensor_reduce(core.row_max[:, n % 2, :], by_head(score_bank(n)), AX.X, ALU.max).then_inc(max_ready, 1)
                if 0 <= m < NT:
                    dve.wait_ge(exp_ready, m + 1)
                    nc.vector.tensor_reduce(core.row_sum[:, m % 2, :], by_head(core.probs[:, m % 2, :]), AX.X,
                                            ALU.add).then_inc(sums_ready, 1)
                if n < NT:
                    if mode == "clip":
                        nc.vector.tensor_scalar(core.shifted[:, n % 2, :], score_bank(n), 11.0, -11.0, ALU.min,
                                                ALU.max).then_inc(shifted_ready, 1)
                    else:
                        dve.wait_ge(max_ready, n + 1)
                        nc.vector.tensor_tensor(by_head(core.shifted[:, n % 2, :]), by_head(score_bank(n)),
                                                core.row_max[:, n % 2, :].unsqueeze(2).to_broadcast([P, H, CK]),
                                                ALU.subtract).then_inc(shifted_ready, 1)
                if 0 <= m < NT:
                    dve.wait_ge(sums_ready, m + 1)
                    nc.vector.reciprocal(core.row_rsum[:, m % 2, :], core.row_sum[:, m % 2, :]).then_inc(rsum_ready, 1)
                if 0 <= k < NT:
                    if k == 0 and rows is not None:
                        dve.wait_ge(rows_added, 1)
                    dve.wait_ge(output_ready, k + 1)
                    nc.vector.tensor_tensor(resid[:, k, :], resid[:, k, :], ps[:, 4 + k % 2, 0:P], ALU.add).then_inc(added, 1)
                if 0 <= m < NT:
                    dve.wait_ge(rsum_ready, m + 1)
                    nc.vector.tensor_tensor(by_head(core.probs[:, m % 2, :]), by_head(core.probs[:, m % 2, :]),
                                            core.row_rsum[:, m % 2, :].unsqueeze(2).to_broadcast([P, H, CK]),
                                            ALU.mult).then_inc(probs_ready, 1)
            dve.wait_ge(added, NT)


UNITS = B * NC
GROUPS = 2 * NTB
TILE_ORDER = (0, 3, 2, 1)


def row_scores(core, u, g, banks):
    nc = core.nc
    b, c, pair, i = u // NC, u % NC, g // NTB, TILE_ORDER[g % NTB]
    for k in range(2):
        out = banks[:, k, :]
        nc.tensor.matmul(out[:, 0:(i + 1) * P], core.q_stack[:, c, b * S + i * P:b * S + (i + 1) * P],
                         core.k_head[:, (u % 2) * HPC + 2 * pair + k, 0:(i + 1) * P], start=True, stop=False)
        last = nc.tensor.matmul(out[:, i * P:(i + 1) * P], core.masks[:, 0, :], core.masks[:, 1, :], start=False, stop=True)
    return last


def row_maxima(core, u, g, banks):
    pair, i = g // NTB, TILE_ORDER[g % NTB]
    first = ONE_ROW + 2 * pair * HROWS
    return core.nc.vector.tensor_reduce(core.minus_max[:, u % 2, i, first:first + HROWS + 1:HROWS],
                                        banks[:, :, 0:(i + 1) * P], AX.X, ALU.max, negate=True)


def project_heads(core, x_t, wq, wk, wv, turned=None, bias=None):
    nc, ps = core.nc, core.ps
    cos, sin = core.tables["cos"], core.tables["sin"]
    jobs = [(i, b) for b in range(B) for i in range(2)]
    first_key_stack = NC
    weights, turned = (wq, wk), turned or ()
    with core.stage() as (block, (product, parts_ready, whole_ready, high_ready, low_ready, stacked, out_by_scalar,
                                  out_by_vector, v_ready, v_out, keys_masked, rows_ready, max_ready, *_)):
        def row_banks(g):
            return ps[:, 2:4, :] if g % 2 == 0 else ps[:, 6:8, :]


        def stack_bank(n):
            return ps[:, n % 2, :]

        def by_vector(n):
            return n % 2 == 1 and not turned and n < 2 * NC

        def emptied(engine, n):
            if by_vector(n):
                engine.wait_ge(out_by_vector, sum(by_vector(m) for m in range(n + 1)))
            else:
                engine.wait_ge(out_by_scalar, sum(not by_vector(m) for m in range(n + 1)))

        @block.tensor
        def _(pe):
            for t, (i, b) in enumerate(jobs):
                half = x_t[:, b * S:(b + 1) * S]
                nc.tensor.matmul(ps[:, 2 * t, :], weights[i], half, start=True, stop=True).then_inc(product, 1)
                if turned:
                    nc.tensor.matmul(ps[:, 2 * t + 1, :], turned[i], half, start=True, stop=True).then_inc(product, 1)
            for t, (i, b) in enumerate(jobs):
                pe.wait_ge(low_ready, t + 1)
                half = slice(b * S, (b + 1) * S)
                if t == 2:
                    for n in range(NT):
                        last = nc.tensor.matmul(ps[:, 4 + n // NTB, (n % NTB) * P:(n % NTB + 1) * P],
                                                x_t[:, n * P:(n + 1) * P], wv, start=True, stop=True)
                    last.then_inc(v_ready, 1)
                for c in range(NC):
                    n = t * NC + c
                    if n >= 2:
                        emptied(pe, n - 2)
                    nc.tensor.matmul(stack_bank(n), core.pick[:, 2 * i, c, :], core.high[:, i, half], start=True, stop=False)
                    nc.tensor.matmul(stack_bank(n), core.pick[:, 2 * i + 1, c, :], core.low[:, i, half], start=False,
                                     stop=True).then_inc(stacked, 1)
                    if t >= 2:
                        g = (t - 2) * NC + c
                        if g == 0:
                            pe.wait_ge(keys_masked, HPC)
                            emptied(pe, 0)
                        elif g == 1:
                            pe.wait_ge(low_ready, 4)
                        else:
                            pe.wait_ge(max_ready, g - 1)
                        row_scores(core, 0, g, row_banks(g)).then_inc(rows_ready, 1)

        def evacuate(engine, n):
            t, c = n // NC, n % NC
            i, b = jobs[t]
            target = (core.q_stack if i == 0 else core.k_stack)[:, c, b * S:(b + 1) * S]
            row = core.consts["zero" if i == 0 else "one_row"]
            engine.wait_ge(stacked, n + 1)
            if by_vector(n):
                nc.vector.tensor_scalar(target, stack_bank(n), row, None, ALU.add).then_inc(out_by_vector, 1)
            else:
                nc.scalar.activation(target, stack_bank(n), ACT.Identity, bias=row).then_inc(out_by_scalar, 1)

        @block.scalar
        def _(act):
            def high(t):
                i, b = jobs[t]
                half = slice(b * S, (b + 1) * S)
                if turned:
                    act.wait_ge(whole_ready, t + 1)
                    source = core.rotated[:, i, half]
                else:
                    act.wait_ge(product, t + 1)
                    source = ps[:, 2 * t, :]
                nc.scalar.activation(core.high[:, i, half], source, ACT.Copy).then_inc(high_ready, 1)

            high(0)
            high(1)
            for n in range(len(jobs) * NC):
                if n in (NC, NC + 2):
                    high(2 + (n - NC) // 2)
                if not by_vector(n):
                    evacuate(act, n)
            act.wait_ge(v_ready, 1)
            for b in range(B):
                nc.scalar.activation(core.v_ones[:, b * NTB:(b + 1) * NTB, :, 0:HD],
                                     ps[:, 4 + b, :].rearrange("p (n h d) -> p n h d", n=NTB, h=H), ACT.Copy).then_inc(v_out, 1)

        @block.vector
        def _(dve):
            def rotate(t):
                i, b = jobs[t]
                whole, turned_part = core.rotated[:, i, b * S:(b + 1) * S], core.turn_part[:, t % 2, :]
                for half, (table, dst, column) in enumerate(((cos, whole, bias[2 * i]), (sin, turned_part, bias[2 * i + 1]))):
                    dve.wait_ge(product, 2 * t + half + 1)
                    nc.vector.scalar_tensor_tensor(dst, ps[:, 2 * t + half, :], column, table, ALU.add, ALU.mult).then_inc(parts_ready, 1)
                dve.wait_ge(parts_ready, 2 * t + 2)
                nc.vector.tensor_tensor(whole, whole, turned_part, ALU.add).then_inc(whole_ready, 1)

            def low(t):
                i, b = jobs[t]
                half = slice(b * S, (b + 1) * S)
                dve.wait_ge(high_ready, t + 1)
                nc.vector.tensor_tensor(core.low[:, i, half], core.rotated[:, i, half] if turned else ps[:, 2 * t, :],
                                        core.high[:, i, half], ALU.subtract).then_inc(low_ready, 1)

            if turned:
                rotate(0)
            for t in range(3):
                if turned:
                    rotate(t + 1)
                low(t)
            for n in range(2 * NC):
                if by_vector(n):
                    evacuate(dve, n)
            emptied(dve, first_key_stack)
            for j in range(HPC):
                nc.vector.tensor_scalar(core.k_head[:, j, :], core.k_stack[:, 0, 0:S], core.consts["stack_rows"][:, j:j + 1],
                                        None, ALU.mult).then_inc(keys_masked, 1)
            low(3)
            for n in range(2 * NC, len(jobs) * NC):
                g = n - 2 * NC
                if by_vector(n):
                    evacuate(dve, n)
                dve.wait_ge(rows_ready, g + 1)
                row_maxima(core, 0, g, row_banks(g)).then_inc(max_ready, 1)


def self_attention(core, extra=None, fold=None):
    nc, ps = core.nc, core.ps
    ident, ident_b = core.consts["ident"], core.masks[:, 0, :]
    mask_cols = core.masks[:, 2, :]
    PLACE = {0: (4, 0, 0), 1: (5, 0, S), 3: (5, S - P, 2 * S - P), 2: (6, 0, 2 * S)}
    PIECES = ((4, (0,), 0, S), (5, (1, 3), S, S), (6, (2,), 2 * S, S // 2))

    with core.stage() as (block, (keys_masked, rows_ready, max_ready, max_turned, max_added, scores_ready, exp_ready,
                                  attended_raw, raw_out, raw_turned, rsum_ready, attended_ready, landed,
                                  kv_ready, spread, product, evacuated, *_)):
        if fold is not None:
            fold.signals(kv_ready, spread, product, evacuated)
        if extra is not None:
            @block.sync
            def _(sp):
                extra(sp, landed)

        @block.tensor
        def _(pe):
            def maxima(u, g):
                n = (u - 1) * GROUPS + g
                if g == 0:
                    pe.wait_ge(keys_masked, HPC * u)
                    pe.wait_ge(max_added, u)
                if n >= 2:
                    pe.wait_ge(max_ready, n - 1)
                row_scores(core, u, g, ps[:, 2 * (n % 2):2 * (n % 2) + 2, :]).then_inc(rows_ready, 1)

            def turn_maxima(u):
                if u >= 1:
                    pe.wait_ge(max_ready, GROUPS * u)
                for i in range(NTB):
                    last = nc.tensor.transpose(ps[:, 0, i * P:(i + 1) * P], core.minus_max[:, u % 2, i, :], ident)
                last.then_inc(max_turned, 1)

            def scores(u, j, pieces):
                b, c = u // NC, u % NC
                if j == 0 and 0 in pieces:
                    pe.wait_ge(max_added, u + 1)
                for piece in pieces:
                    bank, tiles, _, _ = PIECES[piece]
                    n = (u * HPC + j) * len(PIECES) + piece
                    if n >= len(PIECES):
                        pe.wait_ge(exp_ready, n - len(PIECES) + 1)
                    for kt in tiles:
                        _, col, _ = PLACE[kt]
                        w = S - kt * P
                        nc.tensor.matmul(ps[:, bank, col:col + w], core.k_head[:, (u % 2) * HPC + j, kt * P:(kt + 1) * P],
                                         core.q_stack[:, c, b * S + kt * P:(b + 1) * S], start=True, stop=False)
                        last = nc.tensor.matmul(ps[:, bank, col:col + P], ident_b, mask_cols, start=False, stop=True)
                    last.then_inc(scores_ready, 1)

            def values(u, key_tiles):
                b, c = u // NC, u % NC
                if 0 in key_tiles:
                    pe.wait_ge(exp_ready, (u + 1) * HPC * len(PIECES))
                    if u >= 1:
                        pe.wait_ge(attended_ready, u)
                for kt in key_tiles:
                    _, _, at = PLACE[kt]
                    w = S - kt * P
                    for j in range(HPC):
                        rows = slice(HROWS * j, HROWS * (j + 1))
                        last = nc.tensor.matmul(ps[rows, 7, kt * P:S], core.v_ones[:, b * NTB + kt, HPC * c + j, :],
                                                core.head_probs[:, (u % 2) * HPC + j, at:at + w],
                                                start=(kt == 0), stop=(kt == NTB - 1), tile_position=(0, HROWS * j))
                if NTB - 1 in key_tiles:
                    last.then_inc(attended_raw, 1)

            def turn_raw(u):
                pe.wait_ge(raw_out, u + 1)
                for i in range(NTB):
                    last = nc.tensor.transpose(ps[:, 7, i * P:(i + 1) * P], core.attended_raw[:, u % 2, i * P:(i + 1) * P], ident)
                last.then_inc(raw_turned, 1)

            turn_maxima(0)
            for u in range(1, UNITS + 1):
                for j in range(HPC):
                    scores(u - 1, j, (0, 1))
                    if u < UNITS:
                        maxima(u, 2 * j)
                    scores(u - 1, j, (2,))
                    if u >= 2 and j == 1:
                        turn_raw(u - 2)
                    if u < UNITS:
                        maxima(u, 2 * j + 1)
                    elif fold is not None:
                        if j == 0:
                            fold.project(pe)
                        elif j == 2:
                            fold.fold_keys(pe)
                        elif j == 3:
                            fold.fold_values(pe)
                values(u - 1, (0,))
                if u < UNITS:
                    turn_maxima(u)
                values(u - 1, (1, 2, 3))
            turn_raw(UNITS - 1)

        @block.gpsimd
        def _(pool):
            for u in range(1, UNITS):
                b, c = u // NC, u % NC
                for j in range(HPC):
                    if u >= 2:
                        pool.wait_ge(scores_ready, ((u - 2) * HPC + j + 1) * len(PIECES))
                    nc.gpsimd.tensor_tensor(core.k_head[:, (u % 2) * HPC + j, :], core.k_stack[:, c, b * S:(b + 1) * S],
                                            core.consts["stack_rows"][:, j:j + 1].to_broadcast([P, S]),
                                            ALU.mult).then_inc(keys_masked, 1)
            pool.wait_ge(keys_masked, (UNITS - 1) * HPC)

        def evacuate_raw(act, u):
            act.wait_ge(attended_raw, u + 1)
            nc.scalar.activation(core.attended_raw[:, u % 2, :], ps[:, 7, :], ACT.Copy).then_inc(raw_out, 1)

        @block.scalar
        def _(act):
            warm(core, ACT.Exp)
            for u in range(UNITS):
                for j in range(HPC):
                    if u >= 2 and j == 0:
                        act.wait_ge(attended_raw, u - 1)
                    for piece, (bank, _, at, w) in enumerate(PIECES):
                        act.wait_ge(scores_ready, (u * HPC + j) * len(PIECES) + piece + 1)
                        nc.scalar.activation(core.head_probs[:, (u % 2) * HPC + j, at:at + w], ps[:, bank, 0:w], ACT.Exp,
                                             scale=float(HD) ** -0.5).then_inc(exp_ready, 1)
                    if j == 0 and u >= 1:
                        evacuate_raw(act, u - 1)
            evacuate_raw(act, UNITS - 1)

        @block.vector
        def _(dve):
            def normalise(u):
                b, c = u // NC, u % NC
                turned = ps[:, 7, :].rearrange("p (n h r) -> p n h r", n=NTB, h=HPC)
                rsum = core.head_rsum[:, u % 2, :].rearrange("p (n h) -> p n h", n=NTB)
                dve.wait_ge(raw_turned, u + 1)
                nc.vector.reciprocal(rsum, turned[:, :, :, HD]).then_inc(rsum_ready, 1)
                dve.wait_ge(rsum_ready, u + 1)
                heads = core.attended[:, b * NTB:(b + 1) * NTB, c * HPC * HD:(c + 1) * HPC * HD]
                nc.vector.tensor_tensor(heads.rearrange("p n (h d) -> p n h d", h=HPC), turned[:, :, :, 0:HD],
                                        rsum.unsqueeze(3).to_broadcast([P, NTB, HPC, HD]), ALU.mult).then_inc(attended_ready, 1)

            for u in range(UNITS):
                b, c = u // NC, u % NC
                for g in range(GROUPS if u >= 1 else 0):
                    n = (u - 1) * GROUPS + g
                    dve.wait_ge(rows_ready, n + 1)
                    if g == 0 and u >= 2:
                        dve.wait_ge(max_turned, u - 1)
                    row_maxima(core, u, g, ps[:, 2 * (n % 2):2 * (n % 2) + 2, :]).then_inc(max_ready, 1)
                    if g == 3 and u >= 2:
                        normalise(u - 2)
                dve.wait_ge(max_turned, u + 1)
                q = core.q_stack[:, c, b * S:(b + 1) * S]
                nc.vector.tensor_tensor(q, q, ps[:, 0, :], ALU.add).then_inc(max_added, 1)
            if fold is not None:
                fold.spread_heads(dve)
            normalise(UNITS - 2)
            if fold is not None:
                fold.evacuate_keys(dve)
                fold.evacuate_values(dve)
            normalise(UNITS - 1)


def attention_output(core, wo, resid, rows=None, bv=None):
    nc, ps = core.nc, core.ps
    with core.stage(7) as (block, (turned, turned_out, output_ready, bias_ready, rows_in, rows_added, added, *_)):
        @block.tensor
        def _(pe):
            if bv is not None:
                nc.tensor.matmul(ps[:, 4, 0:P], bv.to_broadcast([P, P]), wo, start=True, stop=True).then_inc(bias_ready, 1)
            for b in range(B):
                for i in range(NTB):
                    last = nc.tensor.transpose(ps[:, b, i * P:(i + 1) * P], core.attended[:, b * NTB + i, :], core.consts["ident"])
                last.then_inc(turned, 1)
            for b in range(B):
                pe.wait_ge(turned_out, b + 1)
                for i in range(NTB):
                    last = nc.tensor.matmul(ps[:, 2 + b, i * P:(i + 1) * P], core.attended_t[:, b, i * P:(i + 1) * P], wo,
                                            start=True, stop=True)
                last.then_inc(output_ready, 1)

        @block.scalar
        def _(act):
            for b in range(B):
                act.wait_ge(turned, b + 1)
                nc.scalar.activation(core.attended_t[:, b, :], ps[:, b, :], ACT.Copy).then_inc(turned_out, 1)

        @block.vector
        def _(dve):
            if bv is not None:
                dve.wait_ge(bias_ready, 1)
                nc.vector.tensor_tensor(core.junk[:, 0, :], ps[:, 4, 0:P], rows, ALU.add).then_inc(rows_in, 1)
                dve.wait_ge(rows_in, 1)
                nc.vector.tensor_tensor(resid, resid, core.junk[:, 0, :].unsqueeze(1).to_broadcast([P, NT, P]),
                                        ALU.add).then_inc(rows_added, 1)
                dve.wait_ge(rows_added, 1)
            for b in range(B):
                dve.wait_ge(output_ready, b + 1)
                half = resid[:, b * NTB:(b + 1) * NTB, :]
                source = ps[:, 2 + b, :].rearrange("p (n d) -> p n d", d=P)
                if bv is not None:
                    nc.vector.tensor_tensor(half, half, source, ALU.add).then_inc(added, 1)
                else:
                    nc.vector.tensor_copy(half, source).then_inc(added, 1)
            dve.wait_ge(added, B)


def feed_forward(core, x_t, n_experts, n_chunks, gate, up, down, acc, comb=None, b1=None, b2=None, add=False,
                 extra=None):
    nc, ps = core.nc, core.ps
    halves = [(e, b) for e in range(n_experts) for b in range(B)]
    with core.stage(13) as (block, (gate_ready, act_ready, hidden_ready, hidden_ready_b, output_ready, accumulated,
                                  comb_turned, comb_out, bias_ready, bias_in, landed, *_)):
        if extra is not None:
            @block.sync
            def _(sp):
                extra(sp, landed)

        per_half = n_chunks

        @block.tensor
        def _(pe):
            if b2 is not None:
                for n in range(NT):
                    last = nc.tensor.transpose(ps[0:E8, 6 + n // NTB, (n % NTB) * P:(n % NTB + 1) * P], comb[:, n, :],
                                               core.consts["ident"])
                last.then_inc(comb_turned, 1)

            def hidden(h):
                e, b = halves[h]
                for c in range(n_chunks):
                    n = h * per_half + c
                    half = x_t[:, b * S:(b + 1) * S]
                    if up is not None:
                        if n >= 2:
                            pe.wait_ge(hidden_ready, n - 1)
                        nc.tensor.matmul(ps[:, 2 * (n % 2), :], gate[:, e * n_chunks + c, :], half, start=True, stop=True)
                        nc.tensor.matmul(ps[:, 2 * (n % 2) + 1, :], up[:, e * n_chunks + c, :], half,
                                         start=True, stop=True).then_inc(gate_ready, 1)
                    else:
                        if n >= 4:
                            pe.wait_ge(hidden_ready if n % 2 == 0 else hidden_ready_b, (n - 4) // 2 + 1)
                        nc.tensor.matmul(ps[:, n % 4, :], gate[:, e * n_chunks + c, :], half,
                                         start=True, stop=True).then_inc(gate_ready, 1)

            def output(h):
                e, b = halves[h]
                done = (h + 1) * per_half
                if up is not None:
                    pe.wait_ge(hidden_ready, done)
                else:
                    pe.wait_ge(hidden_ready, (done + 1) // 2)
                    pe.wait_ge(hidden_ready_b, done // 2)
                if h >= 2:
                    pe.wait_ge(accumulated, h - 1)
                for i in range(NTB):
                    for c in range(n_chunks):
                        last = nc.tensor.matmul(ps[:, 4 + h % 2, i * P:(i + 1) * P], core.hidden[:, h % 2, c, i * P:(i + 1) * P],
                                                down[:, e * n_chunks + c, :], start=(c == 0), stop=(c == n_chunks - 1))
                last.then_inc(output_ready, 1)

            for h in range(len(halves) + 1):
                if h < len(halves):
                    hidden(h)
                if h >= 1:
                    output(h - 1)
                if h == 1 and b2 is not None:
                    pe.wait_ge(comb_out, 1)
                    for n in range(NT):
                        last = nc.tensor.matmul(ps[:, 6 + n // NTB, (n % NTB) * P:(n % NTB + 1) * P],
                                                core.comb_t[0:E8, n * P:(n + 1) * P], b2[0:E8, :], start=True, stop=True)
                    last.then_inc(bias_ready, 1)

        def slot(n):
            h, c = n // per_half, n % per_half
            return core.hidden[:, h % 2, c, :]

        @block.scalar
        def _(act):
            if up is not None:
                warm(core, ACT.Silu)
            if b2 is not None:
                act.wait_ge(comb_turned, 1)
                nc.scalar.activation(core.comb_t[0:E8, :].rearrange("p (b s) -> p b s", b=B), ps[0:E8, 6:8, :],
                                     ACT.Copy).then_inc(comb_out, 1)
            for n in range(len(halves) * per_half):
                if up is not None:
                    act.wait_ge(gate_ready, n + 1)
                    if n >= 2:
                        act.wait_ge(hidden_ready, n - 1)
                    nc.scalar.activation(core.gated[:, n % 2, :], ps[:, 2 * (n % 2), :], ACT.Silu).then_inc(act_ready, 1)
                elif n % 2 == 0:
                    h, c = n // per_half, n % per_half
                    e = halves[h][0]
                    act.wait_ge(gate_ready, n + 1)
                    if h >= 2:
                        act.wait_ge(output_ready, h - 1)
                    nc.scalar.activation(slot(n), ps[:, n % 4, :], ACT.Relu,
                                         bias=b1[:, e * n_chunks + c:e * n_chunks + c + 1]).then_inc(hidden_ready, 1)

        @block.vector
        def _(dve):
            def hidden(h):
                e = halves[h][0]
                for c in range(n_chunks):
                    n = h * per_half + c
                    if up is not None:
                        dve.wait_ge(act_ready, n + 1)
                        if h >= 2 and c == 0:
                            dve.wait_ge(output_ready, h - 1)
                        nc.vector.tensor_tensor(slot(n), core.gated[:, n % 2, :], ps[:, 2 * (n % 2) + 1, :],
                                                ALU.mult).then_inc(hidden_ready, 1)
                    elif n % 2 == 1:
                        dve.wait_ge(gate_ready, n + 1)
                        if h >= 2:
                            dve.wait_ge(output_ready, h - 1)
                        nc.vector.tensor_scalar(slot(n), ps[:, n % 4, :], b1[:, e * n_chunks + c:e * n_chunks + c + 1], 0.0,
                                                ALU.add, ALU.max).then_inc(hidden_ready_b, 1)

            def accumulate(h):
                e, b = halves[h]
                dve.wait_ge(output_ready, h + 1)
                if h >= 2:
                    dve.wait_ge(accumulated, h - 1)
                bank = ps[:, 4 + h % 2, :].rearrange("p (n d) -> p n d", d=P)
                rows = acc[:, b * NTB:(b + 1) * NTB, :]
                if comb is None:
                    if add:
                        last = nc.vector.tensor_tensor(rows, rows, bank, ALU.add)
                    else:
                        last = nc.vector.tensor_copy(rows, bank)
                else:
                    for i in range(NTB):
                        weight = comb[:, b * NTB + i, e:e + 1]
                        if e == 0 and not add:
                            last = nc.vector.tensor_scalar(rows[:, i, :], bank[:, i, :], weight, None, ALU.mult)
                        else:
                            last = nc.vector.scalar_tensor_tensor(rows[:, i, :], bank[:, i, :], weight, rows[:, i, :],
                                                                  ALU.mult, ALU.add)
                last.then_inc(accumulated, 1)

            for h in range(len(halves) + 1):
                if h < len(halves):
                    hidden(h)
                if h >= 1:
                    accumulate(h - 1)
                if h == 3 and b2 is not None:
                    dve.wait_ge(bias_ready, 1)
                    dve.wait_ge(accumulated, h)
                    nc.vector.tensor_tensor(acc, acc, ps[:, 6:8, :].rearrange("p b (n d) -> p (b n) d", d=P),
                                            ALU.add).then_inc(bias_in, 1)
                    dve.wait_ge(bias_in, 1)
            dve.wait_ge(accumulated, len(halves))


def choose_two(core, link, key, chosen, chosen_ready=None):
    nc = core.nc
    greater, equal, rank = core.compare[:, 0], core.compare[:, 1], core.rank
    mine, other = key.unsqueeze(3).to_broadcast([P, NT, E8, E8]), key.unsqueeze(2).to_broadcast([P, NT, E8, E8])
    lower = core.consts["lower"].rearrange("p (e j) -> p e j", j=E8)
    link(nc.vector.tensor_tensor(greater, other, mine, ALU.is_gt))
    link(nc.vector.tensor_tensor(equal, other, mine, ALU.is_equal))
    link(nc.vector.tensor_tensor(equal, equal, lower.unsqueeze(1).to_broadcast([P, NT, E8, E8]), ALU.mult))
    link(nc.vector.tensor_tensor(greater, greater, equal, ALU.add))
    link(nc.vector.tensor_reduce(rank, greater, AX.X, ALU.add))
    last = nc.vector.tensor_scalar(chosen, rank, 1.5, None, ALU.is_lt)
    if chosen_ready is not None:
        last.then_inc(chosen_ready, 1)
        nc.vector.wait_ge(chosen_ready, 1)
    else:
        link(last)


def by_expert(ap):
    return ap.unsqueeze(2).to_broadcast([P, NT, E8])


def route(core, x_t, gate, bias=None, among_chosen=False):
    nc, ps = core.nc, core.ps
    with core.stage(4) as (block, (logits_ready, shifted_ready, exp_ready, link_signal, *_)):
        @block.tensor
        def _(pe):
            for n in range(NT):
                last = nc.tensor.matmul(ps[:, 7, n * E8:(n + 1) * E8], x_t[:, n * P:(n + 1) * P], gate, start=True, stop=True)
            last.then_inc(logits_ready, 1)

        @block.scalar
        def _(act):
            warm(core, ACT.Exp)
            act.wait_ge(shifted_ready, 1)
            nc.scalar.activation(core.exps, core.exps, ACT.Exp).then_inc(exp_ready, 1)

        @block.vector
        def _(dve):
            link = chained(dve, link_signal)
            logits, exps, chosen = core.logits, core.exps, core.chosen
            dve.wait_ge(logits_ready, 1)
            source = ps[:, 7, 0:NT * E8].rearrange("p (n e) -> p n e", e=E8)
            if bias is None:
                link(nc.vector.tensor_copy(logits, source))
            else:
                link(nc.vector.tensor_tensor(logits, source, bias.unsqueeze(1).to_broadcast([P, NT, E8]), ALU.add))
            link(nc.vector.tensor_reduce(core.per_token, logits, AX.X, ALU.max))
            nc.vector.tensor_tensor(exps, logits, by_expert(core.per_token), ALU.subtract).then_inc(shifted_ready, 1)
            if among_chosen:
                choose_two(core, link, logits, chosen)
                dve.wait_ge(exp_ready, 1)
                link(nc.vector.tensor_tensor(exps, exps, chosen, ALU.mult))
            else:
                dve.wait_ge(exp_ready, 1)
            link(nc.vector.tensor_reduce(core.per_token, exps, AX.X, ALU.add))
            link(nc.vector.reciprocal(core.per_token, core.per_token))
            if among_chosen:
                link(nc.vector.tensor_tensor(core.comb, exps, by_expert(core.per_token), ALU.mult))
            else:
                link(nc.vector.tensor_tensor(exps, exps, by_expert(core.per_token), ALU.mult))
                choose_two(core, link, exps, chosen)
                link(nc.vector.tensor_tensor(core.comb, exps, chosen, ALU.mult))


def route_over_tokens(core, x_t, gate, gate_b):
    nc, ps, ident = core.nc, core.ps, core.consts["ident"]
    probs_t = core.comb_t[0:E8, :].rearrange("p (b s) -> p b s", b=B)
    per_batch = core.per_batch[0:E8, :]
    with core.stage() as (block, (logits_ready, shifted_ready, exp_ready, probs_ready, turned, link_signal,
                                  chosen_ready, chosen_turned, parts_ready, parts_turned, evacuated, *_)):
        def turn(source, rows, bank):
            for n in range(NT):
                last = nc.tensor.transpose(ps[0:rows, bank + n // NTB, (n % NTB) * P:(n % NTB + 1) * P], source[:, n, :], ident)
            return last

        def turned_rows(rows, bank):
            return ps[0:rows, bank:bank + 2, :]

        @block.tensor
        def _(pe):
            for b in range(B):
                last = nc.tensor.matmul(ps[0:E8, b, :], gate, x_t[:, b * S:(b + 1) * S], start=True, stop=True)
            last.then_inc(logits_ready, 1)
            pe.wait_ge(probs_ready, 1)
            for n in range(NT):
                last = nc.tensor.transpose(ps[:, 2, n * E8:(n + 1) * E8], core.comb_t[0:E8, n * P:(n + 1) * P], ident[0:E8, 0:E8])
            last.then_inc(turned, 1)
            pe.wait_ge(chosen_ready, 1)
            turn(core.chosen, E8, 3).then_inc(chosen_turned, 1)
            pe.wait_ge(parts_ready, 1)
            turn(core.weight_parts.rearrange("p n r e -> p n (r e)"), 3 * E8, 5).then_inc(parts_turned, 1)

        @block.scalar
        def _(act):
            warm(core, ACT.Exp)
            act.wait_ge(shifted_ready, 1)
            nc.scalar.activation(probs_t, probs_t, ACT.Exp).then_inc(exp_ready, 1)
            act.wait_ge(chosen_turned, 1)
            nc.scalar.activation(core.chosen_t[0:E8, :].rearrange("p (b s) -> p b s", b=B), turned_rows(E8, 3),
                                 ACT.Copy).then_inc(evacuated, 1)

        @block.vector
        def _(dve):
            link = chained(dve, link_signal)
            dve.wait_ge(logits_ready, 1)
            link(nc.vector.tensor_scalar(probs_t, ps[0:E8, 0:2, :], gate_b, None, ALU.add))
            link(nc.vector.tensor_reduce(per_batch, probs_t, AX.X, ALU.max))
            nc.vector.tensor_tensor(probs_t, probs_t, per_batch.unsqueeze(2).to_broadcast([E8, B, S]),
                                    ALU.subtract).then_inc(shifted_ready, 1)
            dve.wait_ge(exp_ready, 1)
            link(nc.vector.tensor_reduce(core.part_sums[0:E8, :, :], probs_t.rearrange("p b (g s) -> p b g s", s=CK), AX.X,
                                         ALU.add))
            link(nc.vector.tensor_reduce(per_batch, core.part_sums[0:E8, :, :], AX.X, ALU.add))
            link(nc.vector.reciprocal(per_batch, per_batch))
            nc.vector.tensor_tensor(probs_t, probs_t, per_batch.unsqueeze(2).to_broadcast([E8, B, S]),
                                    ALU.mult).then_inc(probs_ready, 1)
            dve.wait_ge(turned, 1)
            link(nc.vector.tensor_copy(core.exps, ps[:, 2, 0:NT * E8].rearrange("p (n e) -> p n e", e=E8)))
            choose_two(core, link, core.exps, core.chosen, chosen_ready)
            link(nc.vector.tensor_tensor(core.comb, core.exps, core.chosen, ALU.mult))
            parts = core.weight_parts
            for r in range(2):
                link(nc.vector.tensor_copy(core.rounded, core.comb))
                link(nc.vector.tensor_copy(parts[:, :, r, :], core.rounded))
                target = core.comb if r == 0 else parts[:, :, 2, :]
                last = nc.vector.tensor_tensor(target, core.comb, parts[:, :, r, :], ALU.subtract)
                if r == 0:
                    link(last)
            last.then_inc(parts_ready, 1)
            dve.wait_ge(parts_turned, 1)
            nc.vector.tensor_copy(core.weight_parts_t[0:3 * E8, :].rearrange("p (b s) -> p b s", b=B),
                                  turned_rows(3 * E8, 5)).then_inc(evacuated, 1)


def pooled_experts(core, x_t, w, extra=None):
    nc, ps, ident = core.nc, core.ps, core.consts["ident"]
    jobs = [(e, b) for e in range(E8) for b in range(B)]
    w1, w2, w3 = w.tiled("w1"), w.tiled("w2"), w.tiled("w3")
    first, second, third = core.hidden[:, :, 0, :], core.hidden[:, :, 1, :], core.hidden[:, :, 2, :]
    with core.stage() as (block, (first_raw, first_ready, second_raw, second_ready, third_raw, third_ready,
                                  pooled, landed, *_)):
        if extra is not None:
            @block.sync
            def _(sp):
                extra(sp, landed)

        @block.tensor
        def _(pe):
            for s in range(len(jobs) + 2):
                if s < len(jobs):
                    e, b = jobs[s]
                    if s >= 2:
                        pe.wait_ge(first_ready, s - 1)
                    nc.tensor.matmul(ps[:, s % 2, :], w1[:, e, :], x_t[:, b * S:(b + 1) * S], start=True,
                                     stop=True).then_inc(first_raw, 1)
                j = s - 1
                if 0 <= j < len(jobs):
                    pe.wait_ge(first_ready, j + 1)
                    if j >= 2:
                        pe.wait_ge(second_ready, j - 1)
                    nc.tensor.matmul(ps[:, 2 + j % 2, :], w2[:, jobs[j][0], :], first[:, j % 2, :], start=True,
                                     stop=True).then_inc(second_raw, 1)
                j = s - 2
                if 0 <= j < len(jobs):
                    e, b = jobs[j]
                    pe.wait_ge(second_ready, j + 1)
                    if j >= 2:
                        pe.wait_ge(third_ready, j - 1)
                        pe.wait_ge(pooled, j - 1)
                    nc.tensor.matmul(ps[:, 6 + j % 2, :], core.masks[:, 3, e:e + 1].to_broadcast([P, P]),
                                     core.weight_parts_t[:, b * S:(b + 1) * S], start=True, stop=True)
                    nc.tensor.matmul(ps[:, 4 + j % 2, :], w3[:, e, :], second[:, j % 2, :], start=True,
                                     stop=True).then_inc(third_raw, 1)

        @block.scalar
        def _(act):
            for s in range(len(jobs) + 2):
                if s < len(jobs):
                    act.wait_ge(first_raw, s + 1)
                    if s >= 2:
                        act.wait_ge(second_raw, s - 1)
                    nc.scalar.activation(first[:, s % 2, :], ps[:, s % 2, :], ACT.Relu,
                                         bias=w["b1"][:, jobs[s][0]:jobs[s][0] + 1]).then_inc(first_ready, 1)
                j = s - 2
                if 0 <= j < len(jobs):
                    act.wait_ge(third_raw, j + 1)
                    if j >= 2:
                        act.wait_ge(pooled, j - 1)
                    nc.scalar.activation(third[:, j % 2, :], ps[:, 4 + j % 2, :], ACT.Relu,
                                         bias=w["b3"][:, jobs[j][0]:jobs[j][0] + 1]).then_inc(third_ready, 1)

        def pool(dve, j):
            e, b = jobs[j]
            dve.wait_ge(third_ready, j + 1)
            nc.vector.scalar_tensor_tensor(third[:, j % 2, :], third[:, j % 2, :], 1.0, ps[:, 6 + j % 2, :], ALU.mult,
                                           ALU.mult, accum_out=core.pool_sums[:, e, b:b + 1]).then_inc(pooled, 1)

        @block.vector
        def _(dve):
            for s in range(1, len(jobs) + 3):
                j = s - 1
                if j < len(jobs):
                    e = jobs[j][0]
                    dve.wait_ge(second_raw, j + 1)
                    if j >= 2:
                        dve.wait_ge(third_raw, j - 1)
                    nc.vector.tensor_scalar(second[:, j % 2, :], ps[:, 2 + j % 2, :], w["b2"][:, e:e + 1], 0.0,
                                            ALU.add, ALU.max).then_inc(second_ready, 1)
                j = s - 3
                if 0 <= j < len(jobs):
                    pool(dve, j)


def pooled_output(core, resid):
    nc, ps, ident = core.nc, core.ps, core.consts["ident"]
    with core.stage(5) as (block, (summed, turned, rows_ready, output_ready, added, *_)):
        @block.tensor
        def _(pe):
            pe.wait_ge(summed, 1)
            nc.tensor.transpose(ps[0:E8, 0, 0:P], core.pool_total[:, :], ident).then_inc(turned, 1)
            pe.wait_ge(rows_ready, 1)
            for n in range(NT):
                last = nc.tensor.matmul(ps[:, 1 + n // NTB, (n % NTB) * P:(n % NTB + 1) * P],
                                        core.chosen_t[0:E8, n * P:(n + 1) * P], core.pool_rows[0:E8, :],
                                        start=True, stop=True)
            last.then_inc(output_ready, 1)

        @block.vector
        def _(dve):
            nc.vector.tensor_tensor(core.pool_total[:, :], core.pool_sums[:, :, 0], core.pool_sums[:, :, 1],
                                    ALU.add).then_inc(summed, 1)
            dve.wait_ge(turned, 1)
            nc.vector.tensor_copy(core.pool_rows[0:E8, :], ps[0:E8, 0, 0:P]).then_inc(rows_ready, 1)
            dve.wait_ge(output_ready, 1)
            nc.vector.tensor_tensor(resid, resid, ps[:, 1:3, :].rearrange("p b (n d) -> p (b n) d", d=P),
                                    ALU.add).then_inc(added, 1)
            dve.wait_ge(added, 1)


def norm_context(core, scale, bias, target, before=None):
    nc, ps, ident = core.nc, core.ps, core.consts["ident"]
    rows = B * CK
    x, xn = core.ctx_rows[0:rows, :], core.ctx_norm[0:rows, :]
    mean_var, rstd, root = core.mean_var[0:rows, 0, :], core.rstd[0:rows, 0:1], core.root[0:rows, 0:1]
    with core.stage(5) as (block, (link_signal, root_ready, tile_ready, turned, turned_out, *_)):
        @block.vector
        def _(dve):
            link = chained(dve, link_signal)
            link(nc.vector.bn_stats(core.stats[0:rows, 0, :], x))
            link(nc.vector.bn_aggr(mean_var, core.stats[0:rows, 0, :]))
            dve.wait_ge(root_ready, 1)
            link(nc.vector.reciprocal(rstd, root))
            nc.vector.tensor_scalar(xn, x, mean_var[:, 0:1], rstd, ALU.subtract, ALU.mult).then_inc(tile_ready, 1)
            dve.wait_ge(turned, 1)
            if before is not None:
                dve.wait_ge(before, 16)
            nc.vector.tensor_scalar(target, ps[:, 0, 0:rows], scale, bias, ALU.mult, ALU.add).then_inc(turned_out, 1)

        @block.scalar
        def _(act):
            warm(core, ACT.Sqrt)
            act.wait_ge(link_signal, 2)
            nc.scalar.activation(root, mean_var[:, 1:2], ACT.Sqrt, bias=core.eps_col(1e-5)[0:rows, :]).then_inc(root_ready, 1)

        @block.tensor
        def _(pe):
            pe.wait_ge(tile_ready, 1)
            nc.tensor.transpose(ps[:, 0, 0:rows], xn, ident[0:rows, 0:rows]).then_inc(turned, 1)
            pe.wait_ge(turned_out, 1)


KT3 = NTB + 1


def fold_values(core, w):
    nc, ps = core.nc, core.ps
    wv_t, wo = w.tiled("wv_t"), w.tiled("wo")
    with core.stage() as (block, (product, rows_product, weights_out, rows_in, added, *_)):
        @block.tensor
        def _(pe):
            for h in range(H3):
                nc.tensor.matmul(ps[:, h // 4, (h % 4) * P:(h % 4 + 1) * P], wv_t[:, h, :], wo[:, h, :], start=True,
                                 stop=True).then_inc(product, 1)
            for h in range(H3):
                last = nc.tensor.matmul(ps[:, 2, 0:P], w["bv"][:, h:h + 1].to_broadcast([P, P]), wo[:, h, :],
                                        start=(h == 0), stop=(h == H3 - 1))
            last.then_inc(rows_product, 1)

        @block.scalar
        def _(act):
            for half in range(2):
                act.wait_ge(product, 4 * (half + 1))
                nc.scalar.activation(core.value_weights[:, 4 * half:4 * half + 4, :],
                                     ps[:, half, :].rearrange("p (h d) -> p h d", d=P), ACT.Copy).then_inc(weights_out, 1)

        @block.vector
        def _(dve):
            dve.wait_ge(rows_product, 1)
            nc.vector.tensor_tensor(core.junk[:, 0, :], ps[:, 2, 0:P], w["bo"], ALU.add).then_inc(rows_in, 1)
            dve.wait_ge(rows_in, 1)
            nc.vector.tensor_tensor(core.x, core.x, core.junk[:, 0, :].unsqueeze(1).to_broadcast([P, NT, P]),
                                    ALU.add).then_inc(added, 1)


def latent_attention(core, x_t, media_t, w, extra=None):
    nc, ps, ident = core.nc, core.ps, core.consts["ident"]
    wq, wk, wv = w.tiled("wq"), w.tiled("wk"), core.value_weights
    units = [(b, h) for b in range(B) for h in range(H3)]
    SCALE = float(P) ** -0.5
    ROW_BANKS = (0, 1, 4, 3)
    with core.stage() as (block, (qkv_raw, q_out, k_out, v_out, q_round, k_round, rows_ready, max_ready, max_joined,
                                  max_turned, max_out, scores_ready, exp_ready, output_ready, rsum_ready,
                                  accumulated, zeroed, max_ctx, landed, *_)):
        if extra is not None:
            @block.sync
            def _(sp):
                extra(sp, landed)

        @block.tensor
        def _(pe):
            def front(u):
                b, h = units[u]
                half, media = x_t[:, b * S:(b + 1) * S], media_t[:, b * CK:(b + 1) * CK]
                if u >= 1:
                    pe.wait_ge(max_out, u)
                nc.tensor.matmul(ps[:, 2, 0:CK], wk[:, h, :], media, start=True, stop=True)
                nc.tensor.matmul(ps[0:CK, 2, P:2 * P], media, wv[:, h, :], start=True, stop=True)
                nc.tensor.matmul(ps[:, 1, :], wk[:, h, :], half, start=True, stop=True).then_inc(qkv_raw, 1)
                nc.tensor.matmul(ps[:, 0, :], wq[:, h, :], half, start=True, stop=True).then_inc(qkv_raw, 1)
                for i in range(NTB):
                    last = nc.tensor.matmul(ps[:, 3, i * P:(i + 1) * P], x_t[:, b * S + i * P:b * S + (i + 1) * P],
                                            wv[:, h, :], start=True, stop=True)
                last.then_inc(qkv_raw, 1)

            def rows(u):
                pe.wait_ge(q_round, u + 1)
                pe.wait_ge(k_round, u + 1)
                for i in range(NTB):
                    q = core.q_round[:, i * P:(i + 1) * P]
                    nc.tensor.matmul(ps[:, 2, 2 * P + i * CK:2 * P + (i + 1) * CK], q, core.k_round[:, S:S + CK],
                                     start=True, stop=True)
                    if ROW_BANKS[i] == 3:
                        pe.wait_ge(v_out, u + 1)
                    if ROW_BANKS[i] == 4 and u >= 1:
                        pe.wait_ge(exp_ready, KT3 * u)
                    nc.tensor.matmul(ps[:, ROW_BANKS[i], :], q, core.k_round[:, 0:S], start=True, stop=True).then_inc(rows_ready, 1)

            def turn_maxima(u):
                pe.wait_ge(max_joined, u + 1)
                for i in range(NTB):
                    last = nc.tensor.transpose(ps[:, 1, i * P:(i + 1) * P], core.max3[:, i, :], ident)
                last.then_inc(max_turned, 1)

            def scores(u):
                q, k = core.q3[:, u % 2, :], core.k3[:, u % 2, :]
                pe.wait_ge(max_out, u + 1)
                for kt in range(KT3):
                    n = u * KT3 + kt
                    if n >= 2:
                        pe.wait_ge(exp_ready, n - 1)
                    m = P if kt < NTB else CK
                    out = ps[0:m, 4 + n % 2, :]
                    nc.tensor.matmul(out, k[:, kt * P:kt * P + m], q, start=True, stop=False)
                    nc.tensor.matmul(out, core.ones_b[:, 0:m], core.max_row[:, u % 2, :], start=False, stop=True)\
                        .then_inc(scores_ready, 1)

            def values(u, tiles):
                if 0 in tiles:
                    pe.wait_ge(exp_ready, KT3 * (u + 1))
                    if u >= 1:
                        pe.wait_ge(accumulated, u)
                for i in tiles:
                    out = ps[:, 6 + i // 2, (i % 2) * (P + 1):(i % 2 + 1) * (P + 1)]
                    for kt in range(KT3):
                        last = nc.tensor.matmul(out, core.probs3[:, kt, i * P:(i + 1) * P], core.v3[:, u % 2, kt, :],
                                                start=(kt == 0), stop=(kt == KT3 - 1))
                if NTB - 1 in tiles:
                    last.then_inc(output_ready, 1)

            pe.wait_ge(zeroed, 1)
            front(0)
            rows(0)
            turn_maxima(0)
            for u in range(len(units)):
                more = u + 1 < len(units)
                scores(u)
                if more:
                    front(u + 1)
                values(u, (0,))
                if more:
                    rows(u + 1)
                values(u, (1, 2))
                if more:
                    turn_maxima(u + 1)
                values(u, (3,))

        @block.scalar
        def _(act):
            def front(u):
                b, h = units[u]
                act.wait_ge(qkv_raw, 3 * u + 1)
                bias = w["bk"][:, h:h + 1]
                nc.scalar.activation(core.k3[:, u % 2, 0:S], ps[:, 1, :], ACT.Identity, bias=bias)
                nc.scalar.activation(core.k3[:, u % 2, S:S + CK], ps[:, 2, 0:CK], ACT.Identity, bias=bias)
                nc.scalar.activation(core.v3[0:CK, u % 2, NTB, 0:P], ps[0:CK, 2, P:2 * P], ACT.Copy).then_inc(k_out, 1)
                act.wait_ge(k_out, u + 1)
                nc.scalar.activation(core.k_round[:, :], core.k3[:, u % 2, :], ACT.Copy).then_inc(k_round, 1)
                act.wait_ge(q_out, u + 1)
                nc.scalar.activation(core.q_round[:, :], core.q3[:, u % 2, :], ACT.Copy).then_inc(q_round, 1)

            front(0)
            for u in range(len(units)):
                for kt in range(KT3):
                    m = P if kt < NTB else CK
                    act.wait_ge(scores_ready, u * KT3 + kt + 1)
                    nc.scalar.activation(core.probs3[0:m, kt, :], ps[0:m, 4 + (u * KT3 + kt) % 2, :], ACT.Exp).then_inc(exp_ready, 1)
                if u + 1 < len(units):
                    front(u + 1)

        @block.vector
        def _(dve):
            nc.vector.memset(core.probs3[:, NTB, :], 0.0)
            nc.vector.memset(core.max3[:, :, :], 0.0)
            nc.vector.memset(core.v3[:, :, :, :], 0.0).then_inc(zeroed, 1)
            dve.wait_ge(zeroed, 1)
            nc.vector.memset(core.v3[:, :, 0:NTB, P:P + 1], 1.0)
            nc.vector.memset(core.v3[0:CK, :, NTB, P:P + 1], 1.0)

            def front(u):
                b, h = units[u]
                dve.wait_ge(qkv_raw, 3 * u + 2)
                nc.vector.tensor_scalar(core.q3[:, u % 2, :], ps[:, 0, :], w["bq"][:, h:h + 1], SCALE, ALU.add,
                                        ALU.mult).then_inc(q_out, 1)
                dve.wait_ge(qkv_raw, 3 * u + 3)
                nc.vector.tensor_copy(core.v3[:, u % 2, 0:NTB, 0:P], ps[:, 3, :].rearrange("p (n d) -> p n d", d=P))\
                    .then_inc(v_out, 1)

            def maxima(u):
                for i in range(NTB):
                    dve.wait_ge(rows_ready, NTB * u + i + 1)
                    nc.vector.tensor_reduce(core.max_parts[:, 0, i:i + 1], ps[:, ROW_BANKS[i], :], AX.X, ALU.max,
                                            negate=True).then_inc(max_ready, 1)
                nc.vector.tensor_reduce(core.max_parts[:, 1, :],
                                        ps[:, 2, 2 * P:2 * P + NTB * CK].rearrange("p (i k) -> p i k", k=CK), AX.X, ALU.max,
                                        negate=True).then_inc(max_ctx, 1)
                dve.wait_ge(max_ctx, u + 1)
                if u >= 1:
                    dve.wait_ge(max_turned, u)
                nc.vector.tensor_tensor(core.max3[:, :, 0], core.max_parts[:, 0, :], core.max_parts[:, 1, :],
                                        ALU.min).then_inc(max_joined, 1)
                dve.wait_ge(max_turned, u + 1)
                nc.vector.tensor_copy(core.max_row[:, u % 2, :], ps[:, 1, :]).then_inc(max_out, 1)

            def accumulate(u):
                dve.wait_ge(output_ready, u + 1)
                raw = ps[:, 6:8, 0:2 * (P + 1)].rearrange("p b (i d) -> p b i d", d=P + 1)
                nc.vector.reciprocal(core.rsum3[:, :, :], raw[:, :, :, P]).then_inc(rsum_ready, 1)
                dve.wait_ge(rsum_ready, u + 1)
                if u >= 1:
                    dve.wait_ge(accumulated, u)
                for i in range(NTB):
                    rows = core.x[:, units[u][0] * NTB + i, :]
                    last = nc.vector.scalar_tensor_tensor(rows, raw[:, i // 2, i % 2, 0:P],
                                                          core.rsum3[:, i // 2, i % 2:i % 2 + 1], rows, ALU.mult, ALU.add)
                last.then_inc(accumulated, 1)

            front(0)
            maxima(0)
            for u in range(len(units)):
                if u + 1 < len(units):
                    front(u + 1)
                    maxima(u + 1)
                accumulate(u)
            dve.wait_ge(accumulated, len(units))


def carve(region, start, shape, dt=F32):
    n = 1
    for s in shape:
        n *= s
    columns = n if dt == F32 else n // 2
    view = region[:, start:start + columns]
    if dt != F32:
        view = view.bitcast(dt)
    names = "abcd"[:len(shape)]
    if len(shape) > 1:
        view = view.rearrange(f"p ({' '.join(names)}) -> p {' '.join(names)}", **dict(zip(names, shape)))
    return view, start + columns


def allot(core):
    tokens, experts = [P, NT, P], [P, NT, E8]
    core.ps = core.ctx.enter_context(core.nc.psum_tensor("ps", [P, 8, S], F32))
    core.x = core.sbuf("x", tokens)[:, :, :]
    core.xn = core.sbuf("xn", tokens)[:, :, :]
    core.z = core.sbuf("z", tokens)[:, :, :]
    core.acc = core.sbuf("acc", tokens)[:, :, :]
    core.junk = core.sbuf("junk", tokens)[:, :, :]
    core.x_t = core.sbuf("x_t", [P, T])[:, :]
    core.comb_t = core.sbuf("comb_t", [P, T])[:, :]
    core.chosen_t = core.sbuf("chosen_t", [P, T])[:, :]
    core.weights_1 = core.sbuf("weights_1", [P, max(width("l0x"), width("l2a") + width("l2b"), width("l3x"))])
    core.weights_2 = core.sbuf("weights_2", [P, width("l1f") + width("l2f")])
    core.consts = Fields(core.sbuf("consts", [P, width("consts")]), "consts")
    core.tables = Fields(core.sbuf("tables", [P, width("tables")]), "tables")
    core.masks = core.sbuf("masks", [P, 4, P], BF16)[:, :, :]
    core.ones_b = core.sbuf("ones_b", [P, P], BF16)[:, :]
    core.pick = core.sbuf("pick", [P, 4, NC, P], F16)[:, :, :, :]
    core.key_mask, core.key_low = (core.junk[:, 2 * i:2 * i + 2, :].rearrange("p a (n k) -> p (a n) k", k=CK) for i in range(2))
    core.key_mask_b = core.sbuf("key_mask_b", [P, NT, CK], BF16)[:, :, :]
    core.tokens_i = core.sbuf("tokens_i", [P, NT], I32)[:, :]
    core.tokens_f = core.sbuf("tokens_f", [P, 2, NT])[:, :, :]
    core.stats = core.sbuf("stats", [P, NT, 6])[:, :, :]
    core.mean_var = core.sbuf("mean_var", [P, NT, 2])[:, :, :]
    core.root = core.sbuf("root", [P, NT])[:, :]
    core.shift = core.sbuf("shift", [P, NT])[:, :]
    core.rstd = core.sbuf("rstd", [P, NT])[:, :]
    core.eps = core.sbuf("eps", [P, 2])
    core.warm = core.sbuf("warm", [P, WARM_COLUMNS])
    core.logits = core.sbuf("logits", experts)[:, :, :]
    core.exps = core.sbuf("exps", experts)[:, :, :]
    core.chosen = core.sbuf("chosen", experts)[:, :, :]
    core.comb = core.sbuf("comb", experts)[:, :, :]
    core.rank = core.sbuf("rank", experts)[:, :, :]
    core.weight_parts = core.sbuf("weight_parts", [P, NT, 3, E8])[:, :, :, :]
    core.rounded = core.sbuf("rounded", experts, BF16)[:, :, :]
    core.weight_parts_t = core.sbuf("weight_parts_t", [P, T], BF16)[:, :]
    core.per_token = core.sbuf("per_token", [P, NT])[:, :]
    core.per_batch = core.sbuf("per_batch", [P, B])[:, :]
    core.part_sums = core.sbuf("part_sums", [P, B, S // CK])[:, :, :]
    core.row_max = core.sbuf("row_max", [P, 2, H])[:, :, :]
    core.row_sum = core.sbuf("row_sum", [P, 2, H])[:, :, :]
    core.row_rsum = core.sbuf("row_rsum", [P, 2, H])[:, :, :]
    core.pool_sums = core.sbuf("pool_sums", [P, E8, B])[:, :, :]
    core.pool_total = core.sbuf("pool_total", [P, E8])[:, :]
    core.pool_rows = core.sbuf("pool_rows", [P, P])[:, :]
    core.ctx_rows = core.sbuf("ctx_rows", [P, P])[:, :]
    core.ctx_norm = core.sbuf("ctx_norm", [P, P])[:, :]
    core.ctx_t = core.sbuf("ctx_t", [P, B * CK])[:, :]
    core.media_t = core.sbuf("media_t", [P, B * CK])[:, :]
    stacks = core.sbuf("stacks", [P, B * H3 * S])
    core.q_stack, at = carve(stacks, 0, [NC, T], F16)
    core.k_stack, at = carve(stacks, at, [NC, T], F16)
    core.v_ones, at = carve(stacks, at, [NT, H, HROWS])
    assert at <= B * H3 * S
    core.value_weights, _ = carve(stacks, 0, [H3, P])
    core.k_head = core.sbuf("k_head", [P, 2 * HPC, S], F16)[:, :, :]
    core.minus_max = core.sbuf("minus_max", [P, 2, NTB, P])[:, :, :, :]
    hidden = core.sbuf("hidden", [P, B * NC * S + 2 * S])
    core.attended, at = carve(hidden, 0, [NT, P])
    core.attended_t, at = carve(hidden, at, [B, S])
    core.attended_raw, at = carve(hidden, at, [2, S])
    core.a, at = carve(hidden, at, [B, H * CK])
    core.bb, at = carve(hidden, at, [B, H * CK])
    core.head_rsum = core.sbuf("head_rsum", [P, 2, H])[:, :, :]
    core.k_spread = core.acc.rearrange("p n d -> p (n d)").rearrange("p (b c) -> p b c", b=B)
    core.v_spread = core.junk.rearrange("p n d -> p (n d)").rearrange("p (b c) -> p b c", b=B)
    core.hidden, at = carve(hidden, 0, [2, 4, S])
    core.gated, at = carve(hidden, at, [2, S])
    scratch = core.sbuf("scratch", [P, 2 * HPC * 5 * S // 2])
    core.head_probs, _ = carve(scratch, 0, [2 * HPC, 5 * S // 2])
    core.high, at = carve(scratch, 0, [2, T], F16)
    core.low, at = carve(scratch, at, [2, T], F16)
    core.rotated, at = carve(scratch, at, [2, T])
    core.turn_part, at = carve(scratch, at, [2, S])
    core.compare, _ = carve(scratch, 0, [2, NT * E8 * E8])
    core.compare = core.compare.rearrange("p a (n e j) -> p a n e j", e=E8, j=E8)
    core.shifted, at = carve(scratch, 0, [2, H * CK])
    core.probs, at = carve(scratch, at, [2, H * CK])
    core.probs_t, at = carve(scratch, at, [2, H * CK])
    core.q3, at = carve(scratch, 0, [2, S])
    core.k3, at = carve(scratch, at, [2, S + CK])
    core.probs3, at = carve(scratch, at, [KT3, S])
    core.v3, at = carve(scratch, at, [2, KT3, P + 1])
    core.max3, at = carve(scratch, at, [NTB, P])
    core.q_round, at = carve(scratch, at, [1, S], BF16)
    core.k_round, at = carve(scratch, at, [1, S + CK], BF16)
    core.q_round, core.k_round = core.q_round[:, 0, :], core.k_round[:, 0, :]
    core.max_row, at = carve(scratch, at, [2, S], BF16)
    core.max_parts, at = carve(scratch, at, [2, NTB])
    core.rsum3, at = carve(scratch, at, [2, 2])
    assert at <= 2 * HPC * 5 * S // 2


def first_loads(core):
    nc, ins = core.nc, core.ins
    core.weights_landed = core.ctx.enter_context(nc.semaphore("weights_landed"))
    core.tables_landed = core.ctx.enter_context(nc.semaphore("tables_landed"))
    with core.stage() as (block, (landed, set_done, link_signal, *_)):
        @block.sync
        def _(sp):
            sp.dma_start(core.ctx_rows[0:B * CK, :], ins["ctx"]).then_inc(landed, 16)
            sp.dma_start(core.x, ins["x"].rearrange("(n p) d -> p n d", p=P)).then_inc(landed, 16)
            sp.dma_start(core.consts.all, ins["consts"]).then_inc(landed, 16)
            sp.dma_start(core.tokens_i, ins["tokens"]).then_inc(landed, 16)
            sp.dma_start(Fields(core.weights_1, "l0x").all, ins["l0x"]).then_inc(core.weights_landed, 16)
            sp.dma_start(core.ctx_t, ins["ctx_t"]).then_inc(core.tables_landed, 16)
            sp.dma_start(core.masks, ins["masks"]).then_inc(core.tables_landed, 16)
            sp.dma_start(core.pick, ins["pick"]).then_inc(core.tables_landed, 16)
            sp.dma_start(core.tables.all, ins["tables"]).then_inc(core.tables_landed, 16)
            sp.wait_ge(landed, 4 * 16)

        @block.gpsimd
        def _(pool):
            nc.gpsimd.memset(core.v_ones[:, :, :, :], 0.0).then_inc(set_done, 1)
            pool.wait_ge(set_done, 1)
            nc.gpsimd.memset(core.v_ones[:, :, :, HD:HD + 1], 1.0).then_inc(set_done, 1)
            pool.wait_ge(set_done, 2)

        @block.vector
        def _(dve):
            link = chained(dve, link_signal)
            nc.vector.memset(core.minus_max, 0.0)
            nc.vector.memset(core.weight_parts_t, 0.0)
            nc.vector.memset(core.ones_b, 1.0)
            nc.vector.memset(core.eps[:, 0:1], 1e-5)
            link(nc.vector.memset(core.eps[:, 1:2], 1e-6))
            dve.wait_ge(landed, 4 * 16)
            last, before = core.tokens_f[:, 0, :], core.tokens_f[:, 1, :]
            link(nc.vector.tensor_copy(last, core.tokens_i))
            link(nc.vector.tensor_scalar(before, last, -float(LOOKBACK), None, ALU.add))
            keys = core.consts["keys"].unsqueeze(1).to_broadcast([P, NT, CK])
            link(nc.vector.tensor_tensor(core.key_mask, keys, last.unsqueeze(2).to_broadcast([P, NT, CK]), ALU.is_le))
            link(nc.vector.tensor_tensor(core.key_low, keys, before.unsqueeze(2).to_broadcast([P, NT, CK]), ALU.is_gt))
            link(nc.vector.tensor_tensor(core.key_mask, core.key_mask, core.key_low, ALU.mult))
            link(nc.vector.tensor_scalar(core.key_mask_b, core.key_mask, -NEG, NEG, ALU.mult, ALU.add))


def build(nc, ins, out):
    with ExitStack() as ctx:
        core = Core(nc, ctx, ins, out)
        allot(core)
        x, xn, z, acc, x_t = core.x, core.xn, core.z, core.acc, core.x_t

        def loader(fields, source):
            return lambda sp, landed: load(sp, fields, source, landed)

        first_loads(core)

        w = Fields(core.weights_1, "l0x")
        norm_context(core, w["ctx_w"], w["ctx_b"], core.media_t, before=core.weights_landed)
        norm(core, x, xn, None, "layer", 1e-5, beside=WideKeysAndValues(core, w, core.media_t))
        norm(core, xn, xn, x_t, "layer", 1e-5, w["lat_w"], w["lat_b"], beside=WideFold(core, w))
        dense = Fields(core.weights_2, "l0f")

        def load_dense(sp, landed):
            load(sp, dense, ins["l0f"], landed)
            sp.wait_ge(core.tables_landed, 4 * 16)
        cross_attention(core, x_t, x, "clip", rows=w["bo"], extra=load_dense)

        w = dense
        with core.joined():
            norm(core, x, xn, x_t, "layer", 1e-5)
            project_heads(core, x_t, w["wq"], w["wk"], w["wv"])
        l1x = Fields(core.weights_1, "l1x")
        self_attention(core, extra=loader(l1x, ins["l1x"]))
        with core.joined():
            attention_output(core, w["wo"], acc)
            rms_add(core, acc, w["attn_w"], xn, z)
        with core.joined():
            route(core, x_t, w["router"])
            feed_forward(core, x_t, E8, 1, w.tiled("ew1"), w.tiled("ew3"), w.tiled("ew2"), acc, comb=core.comb)
            rms_add(core, acc, w["moe_w"], x, x)
        with core.joined():
            turn_rows(core, z, x_t, also=x)
            feed_forward(core, x_t, 1, 4, w.tiled("w1"), w.tiled("w3"), w.tiled("w2"), acc)
            rms_add(core, acc, w["ff_w"], x, x)

        w = l1x
        l1f = Fields(core.weights_2, "l1f")
        with core.joined():
            norm(core, x, xn, x_t, "layer", 1e-5)
            fold_context(core, ContextFold(core, core.ctx_t, w["wk_t"], w["wv_t"], w["wq"], w["wo_t"], w["bk"], w["bv"]))
            cross_attention(core, x_t, x, "bias", rows=w["bo"], bq=w["bq"], extra=loader(l1f, ins["l1f"]))

        w = l1f
        l2a = Fields(core.weights_1, "l2a")
        l2b = Fields(core.weights_1, "l2b", width("l2a"))
        l2f = Fields(core.weights_2, "l2f", width("l1f"))
        w12 = w["w12_t"].rearrange("p (e c w) -> p e c w", c=4, w=P)
        with core.joined():
            norm(core, x, xn, x_t, "layer", 1e-5)
            route(core, x_t, w["gate"], among_chosen=True)
            feed_forward(core, x_t, E8, 2, Pairs(w12, 0), Pairs(w12, 2), w.tiled("w3_t"), x, comb=core.comb, add=True,
                         extra=loader(l2a, ins["l2a"][0]))
            norm(core, x, z, None, "layer", 1e-5, extra=loader(l2f, ins["l2f"]))

        with nc.Fori(0, L2_LAYERS) as layer:
            w = l2a
            with core.joined():
                norm(core, z, xn, x_t, "rms", 1e-6, w["n1"])
                project_heads(core, x_t, w["wq"], w["wk"], w["wv"], (w["wq_turned"], w["wk_turned"]),
                              (w["bq"], w["bq_turned"], w["bk"], w["bk_turned"]))
            self_attention(core, extra=loader(l2b, ins["l2b"][bass.ds(layer, 1)].rearrange("a p n -> (a p) n")),
                           fold=ContextFold(core, core.ctx_t, w["wk_cross"], w["wv_cross"], w["wq_cross"], w["wo_cross"]))
            with core.joined():
                attention_output(core, w["wo_t"], z, w["bo"], w["bv"])
                norm(core, z, xn, x_t, "rms", 1e-6, w["n2"])
                cross_attention(core, x_t, z, "mask")
            with core.joined():
                norm(core, z, xn, x_t, "rms", 1e-6, l2b["n3"])
                feed_forward(core, x_t, 1, 4, l2b.tiled("wg"), l2b.tiled("wu"), l2b.tiled("wd"), z, add=True,
                             extra=loader(l2a, ins["l2a"][bass.ds(layer + 1, 1)].rearrange("a p n -> (a p) n")))
        with core.joined():
            rms_add(core, z, l2f["nf"], x, x, 1e-6)
            norm(core, x, xn, x_t, "layer", 1e-5)

        w = l2f
        l3x = Fields(core.weights_1, "l3x")
        route_over_tokens(core, x_t, w["gate"], w["gate_b"][0:E8, :])
        pooled_experts(core, x_t, w, extra=loader(l3x, ins["l3x"]))

        w = l3x
        l3f = Fields(core.weights_2, "l3f")
        with core.joined():
            pooled_output(core, x)
            norm(core, x, xn, None, "layer", 1e-5)
            norm(core, xn, xn, x_t, "layer", 1e-5, w["lat_w"], w["lat_b"])
            norm_context(core, w["media_w"], w["media_b"], core.media_t)
            fold_values(core, w)
        latent_attention(core, x_t, core.media_t, w, extra=loader(l3f, ins["l3f"]))

        w = l3f
        with core.joined():
            norm(core, x, xn, x_t, "layer", 1e-5)
            route(core, x_t, w["gate"], bias=w["gate_b"], among_chosen=True)
        feed_forward(core, x_t, E8, 4, w.tiled("w1"), None, w.tiled("w2"), x, comb=core.comb, b1=w["b1"], b2=w["b2"],
                     add=True)
        finish(core)


class Pairs:

    def __init__(self, tiles, first):
        self.tiles, self.first = tiles, first

    def __getitem__(self, key):
        rows, n, cols = key
        return self.tiles[rows, n // 2, self.first + n % 2, cols]


def finish(core):
    with core.stage() as (block, (written, *_)):
        @block.sync
        def _(sp):
            sp.dma_start(core.out.rearrange("(n p) d -> p n d", p=P), core.x).then_inc(written, 16)
            sp.wait_ge(written, 16)


def rows_of(v):
    return np.broadcast_to(np.asarray(v).reshape(1, -1), (P, np.asarray(v).size))


def cols_of(v):
    return np.ascontiguousarray(np.asarray(v).reshape(-1, P).T)


def tiles_of(w):
    w = np.asarray(w)
    return w.reshape(-1, P, w.shape[1]).transpose(1, 0, 2).reshape(P, -1)


def experts_of(w):
    w = np.asarray(w)
    return w.transpose(1, 0, 2).reshape(P, -1)


def head_turned(w):
    w = np.asarray(w)
    return w.reshape(H, 2, HD // 2, *w.shape[1:])[:, ::-1].reshape(w.shape)


def pack(blob, parts):
    for name, n in LAYOUTS[blob].items():
        assert parts[name].shape == (P, n), (blob, name, parts[name].shape)
    assert len(parts) == len(LAYOUTS[blob])
    return np.ascontiguousarray(np.concatenate([parts[name] for name in LAYOUTS[blob]], axis=1))


def constants():
    row = np.arange(P)
    half = HD // 2
    angle = np.arange(S, dtype=np.float32)[None, :] * \
        (np.float32(1.0) / np.float32(10000.0) ** (np.arange(0, HD, 2, dtype=np.float32) / np.float32(HD)))[row % half][:, None]
    head_rows = (row[:, None] // HD == np.arange(H)[None, :]).astype(np.float32)
    half_rows = (row[:, None] // (P // 2) == np.arange(2)[None, :]).astype(np.float32)
    lower = (np.arange(E8)[None, :] < np.arange(E8)[:, None]).astype(np.float32).reshape(1, -1)
    parts = dict(
        ident=np.eye(P, dtype=np.float32),
        head_rows=head_rows, head_rows_scaled=head_rows * np.float32(HD ** -0.5),
        half_rows=half_rows, half_rows_scaled=half_rows * np.float32((P // 2) ** -0.5),
        stack_rows=(row[:, None] // HROWS == np.arange(HPC)[None, :]).astype(np.float32),
        one_row=(row[:, None] % HROWS == ONE_ROW).astype(np.float32), zero=np.zeros((P, 1), np.float32),
        lower=np.repeat(lower, P, axis=0),
        keys=np.repeat(np.arange(CK, dtype=np.float32)[None, :], P, axis=0))
    above = row[None, :] > row[:, None]
    masks = np.stack([np.eye(P, dtype=np.float32), np.where(above, np.float32(NEG), np.float32(0)),
                      np.where(above.T, np.float32(NEG), np.float32(0)),
                      ((row[:, None] < 3 * E8) & (row[:, None] % E8 == row[None, :])).astype(np.float32)], axis=1)
    pick = np.zeros((P, 4, NC, P), np.float16)
    for which, parts_taken in enumerate(((0, 1), (2,), (0, 2), (1,))):
        for c in range(NC):
            for j in range(HPC):
                for r in parts_taken:
                    for d in range(HD):
                        pick[(c * HPC + j) * HD + d, which, c, j * HROWS + r * HD + d] = 1
    tables = dict(cos=np.cos(angle),
                  sin=np.sin(angle) * np.where(row % HD < half, np.float32(-1), np.float32(1))[:, None])
    consts, tables = (pack(blob, {k: v.astype(np.float32) for k, v in values.items()})
                      for blob, values in (("consts", parts), ("tables", tables)))
    return consts, tables, masks.astype(mybir.dt.np(BF16)), pick


def host_arrays(a):
    l0, f0, l1, f1 = "L0_xattn_", "L0_ffn_", "L1_xattn_", "L1_ffn_"
    l2, f2, l3, f3 = "L2_xattn_", "L2_ffn_", "L3_xattn_", "L3_ffn_"
    inner = H3 * P
    out = {}
    out["consts"], out["tables"], out["masks"], out["pick"] = constants()
    out["x"] = a["x"].reshape(T, P)
    out["ctx"] = a["ctx_1024"].reshape(B * CK, P)
    out["ctx_t"] = np.ascontiguousarray(out["ctx"].T)
    out["tokens"] = np.ascontiguousarray(a["itok_BxS_0_255"].reshape(NT, P).T)
    out["l0x"] = pack("l0x", dict(
        wq_t=tiles_of(a[l0 + "Wq"].T), wk=a[l0 + "Wkv"][:, :inner], wv=a[l0 + "Wkv"][:, inner:], wo=tiles_of(a[l0 + "Wo"]),
        lat_w=cols_of(a[l0 + "ln_l_w"]), lat_b=cols_of(a[l0 + "ln_l_b"]), ctx_w=cols_of(a[l0 + "ln_c_w"]),
        ctx_b=cols_of(a[l0 + "ln_c_b"]), bo=rows_of(a[l0 + "bo"])))
    out["l0f"] = pack("l0f", dict(
        wq=a[f0 + "wq"], wk=a[f0 + "wk"], wv=a[f0 + "wv"], wo=a[f0 + "wo"], w1=a[f0 + "w1"],
        w3=a[f0 + "w3"], w2=tiles_of(a[f0 + "w2"]), router=a[f0 + "router_w"], ew1=experts_of(a[f0 + "ew1"]),
        ew3=experts_of(a[f0 + "ew3"]), ew2=experts_of(a[f0 + "ew2"]), attn_w=rows_of(a[f0 + "attn_norm_w"]),
        ff_w=rows_of(a[f0 + "ff_norm_w"]), moe_w=rows_of(a[f0 + "moe_norm_w"])))
    out["l1x"] = pack("l1x", dict(
        wq=a[l1 + "Wq"], wk_t=a[l1 + "Wk"].T, wv_t=a[l1 + "Wv"].T, wo_t=a[l1 + "Wo"].T, bq=cols_of(a[l1 + "bq"]),
        bk=cols_of(a[l1 + "bk"]), bv=cols_of(a[l1 + "bv"]), bo=rows_of(a[l1 + "bo"])))
    out["l1f"] = pack("l1f", dict(
        w12_t=experts_of(a[f1 + "w12"].transpose(0, 2, 1)),
        w3_t=a[f1 + "w3"].transpose(0, 2, 1).reshape(E8, 2, P, P).transpose(2, 0, 1, 3).reshape(P, -1),
        gate=a[f1 + "gate_w"].T))
    l2a, l2b = [], []
    for i in range(L2_LAYERS):
        wqkv, bqkv = a[l2 + "Wqkv"][i], a[l2 + "bqkv"][i]
        wq, wk, wv = wqkv[0:P], wqkv[P:2 * P], wqkv[2 * P:]
        bq, bk, bv = bqkv[0:P], bqkv[P:2 * P], bqkv[2 * P:]
        wkv = a[l2 + "Wkv_c"][i]
        l2a.append(pack("l2a", dict(
            wq=wq.T, wq_turned=head_turned(wq).T, wk=wk.T, wk_turned=head_turned(wk).T, wv=wv.T,
            wo_t=a[l2 + "Wo"][i].T, bo=rows_of(a[l2 + "bo"][i]),
            wq_cross=a[l2 + "Wq_c"][i], wk_cross=wkv[0:P].T, wv_cross=wkv[P:].T, wo_cross=a[l2 + "Wo_c"][i].T,
            bq=cols_of(bq), bq_turned=cols_of(head_turned(bq)), bk=cols_of(bk), bk_turned=cols_of(head_turned(bk)),
            bv=cols_of(bv), n1=cols_of(a[l2 + "n1"][i]), n2=cols_of(a[l2 + "n2"][i]))))
        l2b.append(pack("l2b", dict(wg=a[l2 + "Wg"][i].T, wu=a[l2 + "Wu"][i].T, wd=tiles_of(a[l2 + "Wd"][i].T),
                                    n3=cols_of(a[l2 + "n3"][i]))))
    l2a.append(np.zeros_like(l2a[0]))
    out["l2a"], out["l2b"] = np.stack(l2a), np.stack(l2b)
    gate_b = np.zeros((P, 1), np.float32)
    gate_b[0:E8, 0] = a[f2 + "gate_b"]
    out["l2f"] = pack("l2f", dict(
        w1=experts_of(a[f2 + "w1"]), w2=experts_of(a[f2 + "w2"]), w3=experts_of(a[f2 + "w3"]), b1=a[f2 + "b1"].T,
        b2=a[f2 + "b2"].T, b3=a[f2 + "b3"].T, gate=a[f2 + "gate_w"], gate_b=gate_b, nf=rows_of(a[l2 + "nf"])))
    out["l3x"] = pack("l3x", dict(
        wq=a[l3 + "Wq"], wk=a[l3 + "Wkv"][:, :inner], wv_t=tiles_of(a[l3 + "Wkv"][:, inner:].T),
        wo=tiles_of(a[l3 + "Wo"]), bq=cols_of(a[l3 + "bq"]), bk=cols_of(a[l3 + "bkv"][:inner]), bv=cols_of(a[l3 + "bkv"][inner:]),
        bo=rows_of(a[l3 + "bo"]), media_w=cols_of(a[l3 + "gamma_media"]), media_b=cols_of(a[l3 + "beta_media"]),
        lat_w=cols_of(a[l3 + "gamma_lat"]), lat_b=cols_of(a[l3 + "beta_lat"])))
    b2 = np.zeros((P, P), np.float32)
    b2[0:E8] = a[f3 + "b2"]
    out["l3f"] = pack("l3f", dict(
        w1=experts_of(a[f3 + "w1"]), w2=a[f3 + "w2"].reshape(E8, 4, P, P).transpose(2, 0, 1, 3).reshape(P, -1),
        b1=a[f3 + "b1"].reshape(E8 * 4, P).T, gate=a[f3 + "w_gate"], gate_b=rows_of(a[f3 + "b_gate"]), b2=b2))
    return out


def kernel(**inputs):
    import concourse.bacc as bacc
    from concourse.bass_utils import run_bass_kernel_spmd

    nc = bacc.Bacc("TRN2", target_bir_lowering=False, num_devices=1)
    arrays = {f"in_{name}": np.ascontiguousarray(v)
              for name, v in host_arrays({k: np.asarray(v) for k, v in inputs.items()}).items()}
    ins = {name[3:]: nc.dram_tensor(name, v.shape, mybir.dt.from_np(v.dtype), kind="ExternalInput").ap()
           for name, v in arrays.items()}
    out = nc.dram_tensor("out", (T, P), F32, kind="ExternalOutput").ap()
    build(nc, ins, out)
    result = run_bass_kernel_spmd(nc, [arrays], core_ids=[0]).results[0]["out"]
    return result.reshape(B, S, P)
```
